# Optimizing a Trainium2 kernel written in Bass

```python
import numpy as np
import jax
import jax.numpy as jnp

def _softmax(x, axis=-1):
    return jax.nn.softmax(x, axis=axis)

def _gelu(x):
    return jax.nn.gelu(x, approximate=True)

def _silu(x):
    return jax.nn.silu(x)

def _sigmoid(x):
    return jax.nn.sigmoid(x)

def _layernorm(x, axis=-1, eps=1e-05):
    m = jnp.mean(x, axis=axis, keepdims=True)
    v = jnp.var(x, axis=axis, keepdims=True)
    return (x - m) / jnp.sqrt(v + eps)

def _scatter_add(tgt, idx, src, axis=0):
    return tgt.at[idx].add(src)

def _segment_sum(src, seg, n):
    return jax.ops.segment_sum(src, seg, n)
kernel_name = 'mk_gnn_resnorm_d2_gnn_r8_3d297f'

def setup_inputs(seed: int=0):
    np.random.seed(seed)
    _w = jnp.asarray

    def _rec_inputs():
        import jax
        import jax.numpy as jnp
        _gk = jax.random.key(seed)
        x = -8.776e-05 + 1 * jax.random.normal(jax.random.fold_in(_gk, 1), (6250, 256), jnp.float32)
        src = jax.random.randint(jax.random.fold_in(_gk, 2), (100000,), 0, 6250, jnp.int32)
        dst = jnp.minimum((6250 * jax.random.uniform(jax.random.fold_in(_gk, 3), (100000,)) ** 2.0).astype(jnp.int32), 49999)
        _o = jnp.argsort(dst, stable=True)
        src = src[_o]
        dst = dst[_o]
        return (x, src, dst)
    x, src, dst = _rec_inputs()

    def _L0_gnn_setup():
        import jax, jax.numpy as jnp
        import numpy as np
        H, D = (8, 32)
        LN_EPS = 1e-05

        def _layernorm(x, g, b):
            mu = jnp.mean(x, axis=-1, keepdims=True)
            var = jnp.mean((x - mu) ** 2, axis=-1, keepdims=True)
            return (x - mu) * jax.lax.rsqrt(var + LN_EPS) * g + b
        key = jax.random.key(seed)
        ks = jax.random.split(key, 8)
        N, E, F = (2500, 40000, 256)
        s = 1.0 / np.sqrt(F)
        return {'feat': jax.random.normal(ks[0], (N, F), jnp.float32), 'edge_src': jax.random.randint(ks[1], (E,), 0, N), 'edge_dst': jax.random.randint(ks[2], (E,), 0, N), 'Wq': jax.random.normal(ks[3], (F, H * D), jnp.float32) * s, 'Wk': jax.random.normal(ks[4], (F, H * D), jnp.float32) * s, 'Wv': jax.random.normal(ks[5], (F, H * D), jnp.float32) * s, 'ln_g': jnp.ones((F,), jnp.float32), 'ln_b': jnp.zeros((F,), jnp.float32), 'W1': jax.random.normal(ks[6], (F, 4 * F), jnp.float32) * s, 'b1': jnp.zeros((4 * F,), jnp.float32), 'prelu_alpha': jnp.full((4 * F,), 0.25, jnp.float32), 'W2': jax.random.normal(ks[7], (4 * F, F), jnp.float32) * (1.0 / np.sqrt(4 * F)), 'b2': jnp.zeros((F,), jnp.float32)}
    _L0_gnn_all = _L0_gnn_setup()
    _L0_gnn_in = {k: v for k, v in _L0_gnn_all.items() if k in ('Wq', 'Wk', 'Wv', 'ln_g', 'ln_b', 'W1', 'b1', 'prelu_alpha', 'W2', 'b2')}
    del _L0_gnn_all

    def _L1_gnn_setup():
        import jax, jax.numpy as jnp
        import numpy as np
        DIM = 256
        HIDDEN = 256
        NUM_ENT = 25000
        NUM_TRI = 25000
        NUM_EDGES = 75000
        key = jax.random.key(seed)
        k1, k2, k3, k4, k5 = jax.random.split(key, 5)
        entity_emb = jax.random.normal(k1, (NUM_ENT, DIM), dtype=jnp.float32)
        src_idx = jax.random.randint(k2, (NUM_EDGES,), 0, NUM_ENT, dtype=jnp.int64)
        dst_idx = jax.random.randint(k3, (NUM_EDGES,), 0, NUM_TRI, dtype=jnp.int64)
        entity_triangle_index = jnp.stack([src_idx, dst_idx], axis=0)
        bound = 1.0 / np.sqrt(DIM)
        W = jax.random.uniform(k4, (HIDDEN, DIM), minval=-bound, maxval=bound, dtype=jnp.float32)
        b = jax.random.uniform(k5, (HIDDEN,), minval=-bound, maxval=bound, dtype=jnp.float32)
        return {'entity_emb': entity_emb, 'entity_triangle_index': entity_triangle_index, 'num_triangles': NUM_TRI, 'W': W, 'b': b}
    _L1_gnn_all = _L1_gnn_setup()
    _L1_gnn_in = {k: v for k, v in _L1_gnn_all.items() if k in ('W', 'b')}
    del _L1_gnn_all
    return {'x': x, 'src': src, 'dst': dst, 'L0_gnn_Wq': _L0_gnn_in['Wq'], 'L0_gnn_Wk': _L0_gnn_in['Wk'], 'L0_gnn_Wv': _L0_gnn_in['Wv'], 'L0_gnn_ln_g': _L0_gnn_in['ln_g'], 'L0_gnn_ln_b': _L0_gnn_in['ln_b'], 'L0_gnn_W1': _L0_gnn_in['W1'], 'L0_gnn_b1': _L0_gnn_in['b1'], 'L0_gnn_prelu_alpha': _L0_gnn_in['prelu_alpha'], 'L0_gnn_W2': _L0_gnn_in['W2'], 'L0_gnn_b2': _L0_gnn_in['b2'], 'L1_gnn_W': _L1_gnn_in['W'], 'L1_gnn_b': _L1_gnn_in['b']}

def reference(x, src, dst, L0_gnn_Wq, L0_gnn_Wk, L0_gnn_Wv, L0_gnn_ln_g, L0_gnn_ln_b, L0_gnn_W1, L0_gnn_b1, L0_gnn_prelu_alpha, L0_gnn_W2, L0_gnn_b2, L1_gnn_W, L1_gnn_b):
    import jax
    import jax.numpy as jnp

    def _L0_gnn_ref(feat, edge_src, edge_dst, Wq, Wk, Wv, ln_g, ln_b, W1, b1, prelu_alpha, W2, b2):
        import jax, jax.numpy as jnp
        import numpy as np
        H, D = (8, 32)
        LN_EPS = 1e-05

        def _layernorm(x, g, b):
            mu = jnp.mean(x, axis=-1, keepdims=True)
            var = jnp.mean((x - mu) ** 2, axis=-1, keepdims=True)
            return (x - mu) * jax.lax.rsqrt(var + LN_EPS) * g + b
        N = feat.shape[0]
        feat_c = jax.lax.stop_gradient(feat)
        q = (feat @ Wq).reshape(N, H, D)
        k = (feat_c @ Wk).reshape(N, H, D)
        v = (feat_c @ Wv).reshape(N, H, D)
        e = jnp.einsum('ehd,ehd->eh', k[edge_src], q[edge_dst]) / np.sqrt(H * D)
        m = jax.ops.segment_max(e, edge_dst, num_segments=N)
        p = jnp.exp(e - m[edge_dst])
        z = jax.ops.segment_sum(p, edge_dst, num_segments=N)
        a = p / z[edge_dst]
        msg = v[edge_src] * a[:, :, None]
        ft2 = jax.ops.segment_sum(msg, edge_dst, num_segments=N)
        rst = ft2.reshape(feat.shape) + feat
        rst = _layernorm(rst, ln_g, ln_b)
        h = rst @ W1 + b1
        h = jnp.where(h > 0, h, prelu_alpha * h)
        ffn = h @ W2 + b2
        rst = _layernorm(rst + ffn, ln_g, ln_b)
        return rst

    def _L1_gnn_ref(entity_emb, entity_triangle_index, num_triangles, W, b):
        import jax, jax.numpy as jnp
        import numpy as np
        DIM = 256
        HIDDEN = 256
        NUM_ENT = 25000
        NUM_TRI = 25000
        NUM_EDGES = 75000
        src_idx = entity_triangle_index[0]
        dst_idx = entity_triangle_index[1]
        msgs = entity_emb[src_idx]
        agg = jax.ops.segment_sum(msgs, dst_idx, num_segments=num_triangles)
        counts = jax.ops.segment_sum(jnp.ones((src_idx.shape[0],), dtype=entity_emb.dtype), dst_idx, num_segments=num_triangles)
        agg = jnp.where(counts[:, None] > 0, agg / jnp.maximum(counts, 1.0)[:, None], agg)
        tri_out = jax.nn.relu(agg @ W.T + b)
        return tri_out
    edge_index = jnp.stack([src, dst])
    x = _layernorm(x + _L0_gnn_ref(x, src, dst, L0_gnn_Wq, L0_gnn_Wk, L0_gnn_Wv, L0_gnn_ln_g, L0_gnn_ln_b, L0_gnn_W1, L0_gnn_b1, L0_gnn_prelu_alpha, L0_gnn_W2, L0_gnn_b2), axis=-1)
    x = _layernorm(x + _L1_gnn_ref(x, edge_index, 6250, L1_gnn_W, L1_gnn_b), axis=-1)
    return x

_drawn_inputs = setup_inputs


def setup_inputs(seed=0):
    import zlib

    import numpy as np

    out = dict(_drawn_inputs(seed))
    spreads = {'L0_gnn_ln_g': (1.0, 0.2),
     'L0_gnn_ln_b': (0.0, 0.1),
     'L0_gnn_b1': (0.0, 0.1),
     'L0_gnn_prelu_alpha': (0.25, 0.6),
     'L0_gnn_b2': (0.0, 0.1)}
    factors = {}
    for name, (base, spread) in spreads.items():
        noise = np.random.default_rng([zlib.crc32(name.encode()), seed]).standard_normal(out[name].shape)
        drawn = base * np.exp(spread * noise) if base else spread * noise
        out[name] = jnp.asarray(drawn.astype(out[name].dtype))
    for name, factor in factors.items():
        out[name] = (out[name] * factor).astype(out[name].dtype)
    return out
```

```python
from contextlib import ExitStack

import concourse.bass as bass
from concourse import mybir

ALU = mybir.AluOpType
ACT = mybir.ActivationFunctionType
AX = mybir.AxisListType
F32 = mybir.dt.float32
BF16 = mybir.dt.bfloat16
I32 = mybir.dt.int32

P = 128
N_NODES, F, HEADS = 6250, 256, 8
DH = F // HEADS
N_EDGES = 100000
HID = 4 * F
HC = HID // P
FC = F // P
BIG = 1.0e30
EPS = 1e-5

WINS = -(-N_NODES // P)
WINS_PAD = WINS + 1
NODES_PAD = WINS_PAD * P
NO_NODE = WINS * P

TILES = -(-N_EDGES // P)
TROWS = 112
TPR = -(-TILES // TROWS)
TILES_PAD = TROWS * TPR
CHUNKS = 16
GS = 4
RING = 4
LAP = GS * RING
SLOTS = -(-(TILES + WINS - 1) // (CHUNKS * GS)) * CHUNKS * GS
SLOTS_TAB = -(-SLOTS // P) * P
SC = SLOTS_TAB // P
LAPS = SLOTS // LAP
PER_CHUNK = SLOTS // CHUNKS
CPOS = PER_CHUNK * P
AW = F + HEADS + 1

assert SLOTS % LAP == 0 and SLOTS_TAB >= SLOTS + LAP and TILES_PAD >= TILES


def wait(eng, sem, value):
    if not isinstance(value, int) or value > 0:
        eng.wait_ge(sem, value)


def laps(eng, body, count):
    body(0, False)
    with eng.Fori(1, count - 1) as i:
        body(i, False)
    body(count - 1, True)


class Shared:

    def __init__(self, nc, life):
        self.nc, self.life = nc, life

    def sb(self, name, shape, dt, life):
        return life.enter_context(self.nc.sbuf_tensor(name, shape, dt))

    def ps(self, name, shape, dt, life):
        return life.enter_context(self.nc.psum_tensor(name, shape, dt))

    def sem(self, name):
        return self.life.enter_context(self.nc.semaphore(name))


def build(nc, x, xT, edges, wqkv, ln_g, ln_b, w1, b1, alpha, w2, b2, wT, bl, out):
    with ExitStack() as top:
        e = Shared(nc, top)
        e.x, e.xT, e.edges, e.wqkv, e.ln_g, e.ln_b = x, xT, edges, wqkv, ln_g, ln_b
        e.w1, e.b1, e.alpha, e.w2, e.b2, e.wT, e.bl, e.out = w1, b1, alpha, w2, b2, wT, bl, out
        e.k_rows = nc.dram_tensor("k_rows", (NODES_PAD, F), F32).ap()
        e.v_rows = nc.dram_tensor("v_rows", (NODES_PAD, F), F32).ap()
        e.x1_rows = nc.dram_tensor("x1_rows", (WINS * P, F), F32).ap()
        e.key_rows = nc.dram_tensor("key_rows", (SLOTS_TAB, P), F32).ap()

        e.src_idx = e.sb("src_idx", [P, SLOTS_TAB], I32, top)
        e.dst_loc = e.sb("dst_loc", [P, SLOTS_TAB], F32, top)
        e.q_at = e.sb("q_at", [P, SLOTS_TAB], I32, top)
        e.acc_at = e.sb("acc_at", [P, SLOTS_TAB], I32, top)
        e.agg_at = e.sb("agg_at", [P, SLOTS_TAB], I32, top)
        e.iota_b = e.sb("iota_b", [P, P], BF16, top)
        e.iota_f = e.sb("iota_f", [P, P], F32, top)
        e.ident_f = e.sb("ident_f", [P, P], F32, top)
        e.ident_b = e.sb("ident_b", [P, P], BF16, top)
        e.eps_col = e.sb("eps_col", [P, 1], F32, top)
        e.stage = e.sb("stage", [P, RING, GS], I32, top)
        e.head_eq = e.sb("head_eq", [P, P], F32, top)
        e.chunk_sel = e.sb("chunk_sel", [P, CHUNKS], F32, top)
        e.score = e.sb("score", [P, SLOTS * HEADS], F32, top)

        build_tables(nc, e)
        with ExitStack() as q_life:
            e.q_parts = e.sb("q_parts", [P, WINS_PAD * 3 * F], BF16, q_life)
            project(nc, e)
            edge_scores(nc, e)
        edge_softmax(nc, e)
        e.cnt_rec = e.sb("cnt_rec", [P, WINS], F32, top)
        e.x1_all = e.sb("x1_all", [P, WINS * F], F32, top)
        with ExitStack() as acc_life:
            e.acc = e.sb("acc", [P, WINS_PAD * AW], F32, acc_life)
            segment_sums(nc, e, "msg", e.v_rows, e.acc, AW, e.acc_at)
            node_ffn(nc, e)
        e.agg = e.sb("agg", [P, WINS_PAD * F], F32, top)
        segment_sums(nc, e, "mean", e.x1_rows, e.agg, F, e.agg_at)
        node_out(nc, e)


def build_tables(nc, e):
    with ExitStack() as ctx:
        ed = e.sb("ed", [TROWS, TPR, 2 * P], I32, ctx)
        edge_dst = e.sb("edge_dst", [TROWS, TPR, 2], F32, ctx)
        thr = e.sb("thr", [TROWS, WINS + 1], F32, ctx)
        past_last = e.sb("past_last", [TROWS, TPR, WINS], F32, ctx)
        past_first = e.sb("past_first", [TROWS, TPR, WINS], F32, ctx)
        ones = e.sb("ones", [P, P], F32, ctx)
        tri = e.sb("tri", [WINS, WINS], F32, ctx)
        wcol = e.sb("wcol", [WINS, 8], F32, ctx)
        slot_row = e.sb("slot_row", [WINS, SLOTS_TAB], F32, ctx)
        slot_col = e.sb("slot_col", [P, SC], F32, ctx)
        begun = e.sb("begun", [WINS, SLOTS_TAB], F32, ctx)
        ended = e.sb("ended", [WINS, SLOTS_TAB], F32, ctx)
        own = e.sb("own", [WINS, SLOTS_TAB], F32, ctx)
        tile_f = e.sb("tile_f", [P, SC], F32, ctx)
        tile_i = e.sb("tile_i", [P, SC], I32, ctx)
        win_base = e.sb("win_base", [P, SC], F32, ctx)
        got = e.sb("got", [P, SC, 2 * P], I32, ctx)
        src_f = e.sb("src_f", [P, SC, P], F32, ctx)
        loc_f = e.sb("loc_f", [P, SC, P], F32, ctx)
        in_lo = e.sb("in_lo", [P, SC, P], F32, ctx)
        in_both = e.sb("in_both", [P, SC, P], F32, ctx)
        node1 = e.sb("node1", [P, SC, P], F32, ctx)
        key = e.sb("key", [P, SC, P], F32, ctx)
        ps_w = e.ps("ps_w", [P, 512], F32, ctx)
        ps_s = e.ps("ps_s", [P, 512], F32, ctx)
        ps_row = e.ps("ps_row", [P, 2, 512], F32, ctx)
        ps_t = e.ps("ps_t", [P, 4, 4, P], F32, ctx)
        consts = e.sem("consts")
        ed_in = e.sem("ed_in")
        tab_d = e.sem("tab_d")
        tab_pe = e.sem("tab_pe")
        rows_in = e.sem("rows_in")
        key_out = e.sem("key_out")
        block = ctx.enter_context(nc.Block())

        @block.sync
        def _(sp):
            sp.dma_start(ed[:], e.edges.rearrange("(p t) c -> p t c", p=TROWS)).then_inc(ed_in, 16)
            sp.wait_ge(tab_d, 20)
            sp.dma_start(e.key_rows.rearrange("(c p) r -> p c r", p=P), key[:]).then_inc(key_out, 16)
            sp.wait_ge(key_out, 16)

        @block.gpsimd
        def _(pool):
            pool.iota(thr[:], [[P, WINS + 1]], base=0, channel_multiplier=0,
                      allow_small_or_imprecise_dtypes=True).then_inc(consts, 1)
            pool.memset(ones[:], 1.0).then_inc(consts, 1)
            pool.iota(slot_row[:], [[1, SLOTS_TAB]], base=0, channel_multiplier=0,
                      allow_small_or_imprecise_dtypes=True).then_inc(consts, 1)
            pool.iota(slot_col[:], [[P, SC]], base=0, channel_multiplier=1,
                      allow_small_or_imprecise_dtypes=True).then_inc(consts, 1)
            pool.iota(e.iota_b[:], [[1, P]], base=0, channel_multiplier=0,
                      allow_small_or_imprecise_dtypes=True).then_inc(consts, 1)
            pool.iota(e.iota_f[:], [[1, P]], base=0, channel_multiplier=0,
                      allow_small_or_imprecise_dtypes=True).then_inc(consts, 1)
            pool.memset(e.ident_f[:], 0.0).then_inc(consts, 1)
            pool.memset(e.head_eq[:], 1.0).then_inc(consts, 1)
            pool.memset(e.eps_col[:], EPS).then_inc(consts, 1)
            pool.wait_ge(consts, 9)
            pool.affine_select(tri[:], ones[0:WINS, 0:WINS], [[1, WINS]], ALU.is_gt, 0.0, base=0,
                               channel_multiplier=-1).then_inc(consts, 1)
            pool.affine_select(e.ident_f[:], e.ident_f[:], [[-1, P]], ALU.not_equal, 1.0, base=0,
                               channel_multiplier=1).then_inc(consts, 1)
            pool.affine_select(e.head_eq[:].rearrange("p (h c) -> p h c", c=CHUNKS),
                               e.head_eq[:].rearrange("p (h c) -> p h c", c=CHUNKS),
                               [[-CHUNKS, HEADS], [0, CHUNKS]], ALU.is_ge, 0.0, base=0,
                               channel_multiplier=1).then_inc(consts, 1)
            pool.wait_ge(consts, 12)
            pool.affine_select(e.head_eq[:].rearrange("p (h c) -> p h c", c=CHUNKS),
                               e.head_eq[:].rearrange("p (h c) -> p h c", c=CHUNKS),
                               [[CHUNKS, HEADS], [0, CHUNKS]], ALU.is_ge, 0.0, base=CHUNKS - 1,
                               channel_multiplier=-1).then_inc(consts, 1)
            pool.wait_ge(tab_d, 14)
            for c in range(SC):
                pool.indirect_dma_start(out=got[:, c, :], out_offset=None, in_=e.edges[:, :],
                                        in_offset=bass.IndirectOffsetOnAxis(ap=tile_i[:, c:c + 1], axis=0)
                                        ).then_inc(rows_in, 16)

        @block.vector
        def _(dve):
            done = [0]

            def step(ins):
                done[0] += 1
                ins.then_inc(tab_d, 1)
                dve.wait_ge(tab_d, done[0])

            dve.wait_ge(consts, 13)
            dve.wait_ge(ed_in, 16)
            step(dve.tensor_copy(edge_dst[:], ed[:, :, P::P - 1]))
            step(dve.tensor_tensor(past_last[:], thr[:, 0:WINS].unsqueeze(1).to_broadcast([TROWS, TPR, WINS]),
                                   edge_dst[:, :, 1:2].to_broadcast([TROWS, TPR, WINS]), ALU.is_gt))
            step(dve.tensor_tensor(past_first[:], thr[:, 1:WINS + 1].unsqueeze(1).to_broadcast([TROWS, TPR, WINS]),
                                   edge_dst[:, :, 0:1].to_broadcast([TROWS, TPR, WINS]), ALU.is_gt))
            dve.wait_ge(tab_pe, 1)
            step(dve.tensor_copy(wcol[:, 0:2], ps_w[0:WINS, 0:2]))
            step(dve.tensor_tensor(wcol[:, 2:3], wcol[:, 1:2], wcol[:, 0:1], ALU.subtract))
            dve.wait_ge(tab_pe, 2)
            step(dve.tensor_copy(wcol[:, 3:4], ps_w[0:WINS, 2:3]))
            step(dve.tensor_tensor(wcol[:, 4:5], wcol[:, 3:4], wcol[:, 2:3], ALU.add))
            step(dve.tensor_tensor(wcol[:, 5:6], wcol[:, 0:1], wcol[:, 3:4], ALU.subtract))
            step(dve.tensor_scalar(begun[:], slot_row[:], wcol[:, 3:4], None, ALU.is_ge))
            step(dve.tensor_scalar(ended[:], slot_row[:], wcol[:, 4:5], None, ALU.is_ge))
            step(dve.tensor_tensor(own[:], begun[:], ended[:], ALU.subtract))
            dve.wait_ge(tab_pe, 3)
            step(dve.tensor_tensor(tile_f[:], ps_s[:, 0:SC], slot_col[:], ALU.add))
            step(dve.tensor_scalar(tile_f[:], tile_f[:], float(TILES_PAD - 1), None, ALU.min))
            step(dve.tensor_copy(tile_i[:], tile_f[:]))
            step(dve.tensor_scalar(win_base[:], ps_s[:, SC:2 * SC], float(P), None, ALU.mult))
            dve.wait_ge(rows_in, 16 * SC)
            step(dve.tensor_tensor(loc_f[:], got[:, :, P:2 * P],
                                   win_base[:].unsqueeze(2).to_broadcast([P, SC, P]), ALU.subtract))
            step(dve.tensor_scalar(in_lo[:], loc_f[:], 0.0, None, ALU.is_ge))
            step(dve.scalar_tensor_tensor(in_both[:], loc_f[:], float(P), in_lo[:], ALU.is_lt, ALU.mult))
            step(dve.tensor_scalar(node1[:], got[:, :, P:2 * P], 1.0, None, ALU.add))
            step(dve.tensor_tensor(key[:], node1[:], in_both[:], ALU.mult))
            step(dve.tensor_copy(src_f[:], got[:, :, 0:P]))
            dve.wait_ge(tab_pe, 4)
            half = SLOTS_TAB // 2
            for n in range(2):
                cols = slice(n * half, (n + 1) * half)
                step(dve.tensor_scalar(e.q_at[:, cols], ps_row[:, n, 0:half], float(3 * F), None, ALU.mult))
                step(dve.tensor_scalar(e.acc_at[:, cols], ps_row[:, n, 0:half], float(AW), None, ALU.mult))
                step(dve.tensor_scalar(e.agg_at[:, cols], ps_row[:, n, 0:half], float(F), None, ALU.mult))
            for c in range(SC):
                dve.wait_ge(tab_pe, 5 + c)
                step(dve.tensor_copy(e.src_idx[:, c * P:(c + 1) * P], ps_t[:, c % 4, 0, :]))
                step(dve.tensor_copy(e.dst_loc[:, c * P:(c + 1) * P], ps_t[:, c % 4, 1, :]))
            step(dve.tensor_copy(e.ident_b[:], e.ident_f[:]))
            step(dve.tensor_reduce(e.chunk_sel[:], e.ident_f[:].rearrange("p (h c) -> p c h", c=CHUNKS),
                                   AX.X, ALU.add))

        @block.tensor
        def _(pe):
            pe.wait_ge(tab_d, 3)
            for r in range(TPR):
                pe.matmul(ps_w[0:WINS, 0:1], past_last[:, r, :], ones[0:TROWS, 0:1],
                          start=(r == 0), stop=(r == TPR - 1))
            for r in range(TPR):
                mm = pe.matmul(ps_w[0:WINS, 1:2], past_first[:, r, :], ones[0:TROWS, 0:1],
                               start=(r == 0), stop=(r == TPR - 1))
            mm.then_inc(tab_pe, 1)
            pe.wait_ge(tab_d, 5)
            pe.matmul(ps_w[0:WINS, 2:3], tri[:], wcol[:, 2:3], start=True, stop=True).then_inc(tab_pe, 1)
            pe.wait_ge(tab_d, 11)
            for c in range(SC):
                pe.matmul(ps_s[:, c:c + 1], own[:, c * P:(c + 1) * P], wcol[:, 5:6], start=True, stop=True)
                mm = pe.matmul(ps_s[:, SC + c:SC + c + 1], ended[:, c * P:(c + 1) * P], ones[0:WINS, 0:1],
                               start=True, stop=True)
            mm.then_inc(tab_pe, 1)
            half = SLOTS_TAB // 2
            for n in range(2):
                mm = pe.matmul(ps_row[:, n, 0:half], ones[0:WINS, :], ended[:, n * half:(n + 1) * half],
                               start=True, stop=True)
            mm.then_inc(tab_pe, 1)
            pe.wait_ge(tab_d, 21)
            for c in range(SC):
                if c >= 4:
                    pe.wait_ge(tab_d, 27 + 2 * (c - 3))
                pe.transpose(ps_t[:, c % 4, 0, :], src_f[:, c, :], e.ident_f[:])
                pe.transpose(ps_t[:, c % 4, 1, :], loc_f[:, c, :], e.ident_f[:]).then_inc(tab_pe, 1)



QB = 5
QLAPS = WINS_PAD // (2 * QB)
Q_SCALE = float(F) ** -0.5


def project(nc, e):
    assert WINS_PAD % (2 * QB) == 0 and Q_SCALE == 2.0 ** -4
    with ExitStack() as ctx:
        xt = e.sb("xt", [P, 2, FC, QB * P], F32, ctx)
        w_sb = e.sb("w_sb", [P, FC, 3 * F], F32, ctx)
        kv_sb = e.sb("kv_sb", [P, 2, QB, 2 * F], F32, ctx)
        q_rest = e.sb("q_rest", [P, 2, F], F32, ctx)
        ps_kv = e.ps("ps_kv", [P, 2, 512], F32, ctx)
        ps_q = e.ps("ps_q", [P, 2, 512], F32, ctx)
        w_in = e.sem("w_in")
        xt_in = [e.sem("xt_in0"), e.sem("xt_in1")]
        projected = e.sem("projected")
        kv_copied = e.sem("kv_copied")
        kv_stored = [e.sem("kv_stored0"), e.sem("kv_stored1")]
        q_hi = e.sem("q_hi")
        q_less_hi = e.sem("q_less_hi")
        q_mid = e.sem("q_mid")
        q_lo = e.sem("q_lo")
        block = ctx.enter_context(nc.Block())
        xT_v = e.xT.rearrange("(c p) n -> p c n", p=P)
        k_v = e.k_rows.rearrange("(w p) f -> p w f", p=P)
        v_v = e.v_rows.rearrange("(w p) f -> p w f", p=P)

        @block.sync
        def _(sp):
            def load(i, b):
                wait(sp, projected, (2 * i + b - 1) * QB)
                sp.dma_start(xt[:, b], xT_v[:, :, bass.ds((2 * i + b) * (QB * P), QB * P)]).then_inc(xt_in[b], 16)

            def store(i, b):
                sp.wait_ge(kv_copied, (2 * i + b + 1) * QB)
                sp.dma_start(k_v[:, bass.ds((2 * i + b) * QB, QB), :], kv_sb[:, b, :, 0:F]).then_inc(kv_stored[b], 16)
                sp.dma_start(v_v[:, bass.ds((2 * i + b) * QB, QB), :], kv_sb[:, b, :, F:2 * F]).then_inc(kv_stored[b], 16)

            def lap(i, last):
                for b in range(2):
                    store(i, b)
                    if not last:
                        load(i + 1, b)

            sp.dma_start(w_sb[:], e.wqkv.rearrange("(c p) n -> p c n", p=P)).then_inc(w_in, 16)
            load(0, 0)
            load(0, 1)
            laps(sp, lap, QLAPS)
            for b in range(2):
                sp.wait_ge(kv_stored[b], 32 * QLAPS)

        @block.tensor
        def _(pe):
            def lap(i, last):
                for b in range(2):
                    pe.wait_ge(xt_in[b], 16 * (i + 1))
                    for m in range(QB):
                        done = (2 * i + b) * QB + m
                        par = (b * QB + m) % 2
                        wait(pe, kv_copied, done - 1)
                        wait(pe, q_lo, done - 1)
                        for c in range(FC):
                            pe.matmul(ps_kv[:, par, :], xt[:, b, c, m * P:(m + 1) * P], w_sb[:, c, 0:2 * F],
                                      start=(c == 0), stop=(c == FC - 1))
                        for c in range(FC):
                            mm = pe.matmul(ps_q[:, par, 0:F], xt[:, b, c, m * P:(m + 1) * P], w_sb[:, c, 2 * F:],
                                           start=(c == 0), stop=(c == FC - 1))
                        mm.then_inc(projected, 1)

            pe.wait_ge(w_in, 16)
            laps(pe, lap, QLAPS)

        @block.scalar
        def _(act):
            def lap(i, last):
                for b in range(2):
                    wait(act, kv_stored[b], 32 * i)
                    for m in range(QB):
                        done = (2 * i + b) * QB + m
                        par = (b * QB + m) % 2
                        act.wait_ge(projected, done + 1)
                        act.activation(kv_sb[:, b, m, :], ps_kv[:, par, :], ACT.Copy).then_inc(kv_copied, 1)
                        act.activation(e.q_parts[:, bass.ds(done * (3 * F), F)], ps_q[:, par, 0:F], ACT.Copy,
                                       scale=Q_SCALE).then_inc(q_hi, 1)

            laps(act, lap, QLAPS)

        @block.vector
        def _(dve):
            def lap(i, last):
                for t in range(2 * QB):
                    done = 2 * QB * i + t
                    par = t % 2
                    at = done * (3 * F)
                    dve.wait_ge(q_hi, done + 1)
                    dve.scalar_tensor_tensor(q_rest[:, par], ps_q[:, par, 0:F], Q_SCALE,
                                             e.q_parts[:, bass.ds(at, F)], ALU.mult, ALU.subtract).then_inc(q_less_hi, 1)
                    dve.wait_ge(q_less_hi, done + 1)
                    dve.tensor_scalar(e.q_parts[:, bass.ds(at + F, F)], q_rest[:, par], 1.0, None,
                                      ALU.mult).then_inc(q_mid, 1)
                    dve.wait_ge(q_mid, done + 1)
                    dve.tensor_tensor(e.q_parts[:, bass.ds(at + 2 * F, F)], q_rest[:, par],
                                      e.q_parts[:, bass.ds(at + F, F)], ALU.subtract).then_inc(q_lo, 1)

            laps(dve, lap, QLAPS)


def edge_scores(nc, e):
    with ExitStack() as ctx:
        k_buf = e.sb("k_buf", [P, RING, GS, F], F32, ctx)
        hot = e.sb("hot", [P, RING, GS, P], BF16, ctx)
        hot_t = e.sb("hot_t", [P, 2, GS, P], BF16, ctx)
        prod = e.sb("prod", [P, 2, GS, F], F32, ctx)
        ps_hot = e.ps("ps_hot", [P, 2, 8, P], BF16, ctx)
        ps_q = e.ps("ps_qe", [P, 2, GS, F], F32, ctx)
        staged = e.sem("ka_staged")
        rows_in = [e.sem(f"ka_rows_in{g}") for g in range(RING)]
        pool_turns = e.sem("ka_pool_turns")
        hot_made = e.sem("ka_hot_made")
        hot_turned = e.sem("ka_hot_turned")
        hot_t_copied = e.sem("ka_hot_t_copied")
        q_picked = e.sem("ka_q_picked")
        multiplied = e.sem("ka_multiplied")
        scored = e.sem("ka_scored")
        block = ctx.enter_context(nc.Block())

        @block.gpsimd
        def _(pool):
            def lap(i, last):
                for g in range(RING):
                    n = i * RING + g
                    pool.wait_ge(staged, n + 1)
                    wait(pool, multiplied, n - RING + 1)
                    pool.sem_inc(pool_turns, 1)
                    for j in range(GS):
                        pool.indirect_dma_start(out=k_buf[:, g, j, :], out_offset=None, in_=e.k_rows[:, :],
                                                in_offset=bass.IndirectOffsetOnAxis(ap=e.stage[:, g, j:j + 1], axis=0)
                                                ).then_inc(rows_in[g], 16)

            laps(pool, lap, LAPS)

        @block.scalar
        def _(act):
            def stage_group(i, g):
                act.activation(e.stage[:, g, :], e.src_idx[:, bass.ds(i * LAP + g * GS, GS)],
                               ACT.Copy).then_inc(staged, 1)

            def lap(i, last):
                for g in range(RING):
                    n = i * RING + g
                    act.wait_ge(hot_turned, n + 1)
                    wait(act, q_picked, n - 1)
                    act.activation(hot_t[:, g % 2], ps_hot[:, g % 2, 0:GS, :], ACT.Copy).then_inc(hot_t_copied, 1)
                    if g == 0:
                        wait(act, rows_in[RING - 1], 16 * GS * i)
                        stage_group(i, RING - 1)
                    elif not last:
                        act.wait_ge(rows_in[g - 1], 16 * GS * (i + 1))
                        stage_group(i + 1, g - 1)

            for g in range(RING - 1):
                stage_group(0, g)
            laps(act, lap, LAPS)

        @block.vector
        def _(dve):
            def make_hot(i, g):
                wait(dve, hot_turned, i * RING + g - RING + 1)
                for j in range(GS):
                    ins = dve.tensor_scalar(hot[:, g, j, :], e.iota_b[:],
                                            e.dst_loc[:, bass.ds(i * LAP + g * GS + j, 1)], None, ALU.is_equal)
                ins.then_inc(hot_made, 1)

            def lap(i, last):
                for g in range(RING):
                    n = i * RING + g
                    dve.wait_ge(rows_in[g], 16 * GS * (i + 1))
                    dve.wait_ge(q_picked, n + 1)
                    dve.tensor_tensor(prod[:, g % 2], k_buf[:, g], ps_q[:, g % 2], ALU.mult).then_inc(multiplied, 1)
                    if g < 2:
                        make_hot(i, g + 2)
                    elif not last:
                        make_hot(i + 1, g - 2)
                    dve.wait_ge(multiplied, n + 1)
                    dve.tensor_reduce(e.score[:, bass.ds(n * (GS * HEADS), GS * HEADS)],
                                      prod[:, g % 2].rearrange("p j (h d) -> p (j h) d", d=DH),
                                      AX.X, ALU.add).then_inc(scored, 1)

            make_hot(0, 0)
            make_hot(0, 1)
            laps(dve, lap, LAPS)

        @block.tensor
        def _(pe):
            win_regs = [pe.alloc_register(f"pick_at{j}") for j in range(GS)]

            def turn(i, g):
                n = i * RING + g
                pe.wait_ge(hot_made, n + 1)
                wait(pe, hot_t_copied, n - 1)
                for j in range(GS):
                    mm = pe.transpose(ps_hot[:, g % 2, j, :], hot[:, g, j, :], e.ident_b[:])
                mm.then_inc(hot_turned, 1)

            def lap(i, last):
                for g in range(RING):
                    n = i * RING + g
                    if g < RING - 1:
                        turn(i, g + 1)
                    elif not last:
                        turn(i + 1, 0)
                    pe.reg_load(win_regs, e.q_at[0:1, bass.ds(n * GS, GS)])
                    pe.wait_ge(hot_t_copied, n + 1)
                    wait(pe, multiplied, n - 1)
                    for j in range(GS):
                        at = pe.snap(win_regs[j], min_val=0, max_val=(WINS_PAD - 1) * 3 * F)
                        for part in range(3):
                            mm = pe.matmul(ps_q[:, g % 2, j, :], hot_t[:, g % 2, j, :],
                                           e.q_parts[:, bass.ds(at + part * F, F)],
                                           start=(part == 0), stop=(part == 2))
                    mm.then_inc(q_picked, 1)

            turn(0, 0)
            laps(pe, lap, LAPS)


def edge_softmax(nc, e):
    QUADS = PER_CHUNK // 4
    with ExitStack() as ctx:
        key = e.sb("key_t", [P, CPOS], F32, ctx)
        cut = e.sb("cut", [P, CPOS + 1], F32, ctx)
        score_t = e.sb("score_t", [P, CPOS], F32, ctx)
        run = e.sb("run", [P, CPOS], F32, ctx)
        packed = e.sb("packed", [P, PER_CHUNK, HEADS, CHUNKS], F32, ctx)
        ends = e.sb("ends", [P, 4], F32, ctx)
        spread = e.sb("spread", [P, 4, CHUNKS], F32, ctx)
        allc = e.sb("allc", [P, 4, CHUNKS], F32, ctx)
        cand = e.sb("cand", [P, 2, 2, CHUNKS], F32, ctx)
        edge_max = e.sb("edge_max", [P, 2], F32, ctx)
        ps_t = e.ps("ps_st", [P, 4, 4, P], F32, ctx)
        ps_c = e.ps("ps_ch", [P, 512], F32, ctx)
        key_in = e.sem("key_in")
        s_packed = e.sem("s_packed")
        s_turned = e.sem("s_turned")
        s_copied = e.sem("s_copied")
        chunk_d = e.sem("chunk_d")
        spread_made = e.sem("spread_made")
        spread_done = e.sem("spread_done")
        m_made = e.sem("m_made")
        m_turned = e.sem("m_turned")
        m_taken = e.sem("m_taken")
        exp_done = e.sem("exp_done")
        block = ctx.enter_context(nc.Block())
        score_v = e.score[:].rearrange("p (c i h) -> p i h c", c=CHUNKS, h=HEADS)

        @block.sync
        def _(sp):
            for h in range(HEADS):
                sp.dma_start(key[h * CHUNKS:(h + 1) * CHUNKS, :],
                             e.key_rows[0:SLOTS, :].rearrange("(c s) r -> c (s r)", c=CHUNKS)).then_inc(key_in, 16)

        @block.gpsimd
        def _(pool):
            for n in range(QUADS):
                pool.tensor_copy(packed[:, 4 * n:4 * n + 4], score_v[:, 4 * n:4 * n + 4]).then_inc(s_packed, 1)

        @block.tensor
        def _(pe):
            for n in range(QUADS):
                pe.wait_ge(s_packed, n + 1)
                if n >= 4:
                    pe.wait_ge(s_copied, n - 3)
                for j in range(4):
                    mm = pe.transpose(ps_t[:, n % 4, j, :], packed[:, 4 * n + j].rearrange("p h c -> p (h c)"),
                                      e.ident_f[:])
                mm.then_inc(s_turned, 1)
            pe.wait_ge(spread_made, 1)
            pe.matmul(ps_c[:, 0:4 * CHUNKS], e.head_eq[:], spread[:].rearrange("p a c -> p (a c)"),
                      start=True, stop=True).then_inc(spread_done, 1)
            pe.wait_ge(m_made, 1)
            pe.wait_ge(s_copied, QUADS)
            for n in range(QUADS):
                if n >= 4:
                    pe.wait_ge(m_taken, n - 3)
                for j in range(4):
                    mm = pe.transpose(ps_t[:, n % 4, j, :], score_t[:, (4 * n + j) * P:(4 * n + j + 1) * P],
                                      e.ident_f[:])
                mm.then_inc(m_turned, 1)

        @block.scalar
        def _(act):
            for n in range(QUADS):
                act.wait_ge(s_turned, n + 1)
                act.activation(score_t[:, 4 * n * P:4 * (n + 1) * P], ps_t[:, n % 4].rearrange("p j r -> p (j r)"),
                               ACT.Copy).then_inc(s_copied, 1)
            act.wait_ge(m_taken, QUADS)
            act.activation(e.score[:], e.score[:], ACT.Exp).then_inc(exp_done, 1)

        @block.vector
        def _(dve):
            done = [0]

            def step(ins):
                done[0] += 1
                ins.then_inc(chunk_d, 1)
                dve.wait_ge(chunk_d, done[0])

            dve.wait_ge(key_in, 16 * HEADS)
            step(dve.memset(cut[:, 0:1], 0.0))
            step(dve.memset(cut[:, CPOS:CPOS + 1], 0.0))
            step(dve.tensor_tensor(cut[:, 1:CPOS], key[:, 1:CPOS], key[:, 0:CPOS - 1], ALU.not_equal))
            step(dve.tensor_scalar(cut[:, 1:CPOS], cut[:, 1:CPOS], -BIG, None, ALU.mult))
            dve.wait_ge(s_copied, QUADS)
            step(dve.tensor_tensor_scan(run[:], cut[:, 0:CPOS], score_t[:], -BIG, ALU.add, ALU.max))
            step(dve.tensor_copy(ends[:, 0:1], run[:, CPOS - 1:CPOS]))
            step(dve.tensor_tensor_scan(run[:, ::-1], cut[:, CPOS:0:-1], score_t[:, ::-1], -BIG, ALU.add, ALU.max))
            step(dve.tensor_copy(ends[:, 1:2], run[:, 0:1]))
            step(dve.tensor_copy(ends[:, 2:3], key[:, CPOS - 1:CPOS]))
            step(dve.tensor_copy(ends[:, 3:4], key[:, 0:1]))
            step(dve.memset(spread[:], 0.0))
            dve.tensor_tensor(spread[:], ends[:].unsqueeze(2).to_broadcast([P, 4, CHUNKS]),
                              e.chunk_sel[:].unsqueeze(1).to_broadcast([P, 4, CHUNKS]), ALU.mult).then_inc(spread_made, 1)
            dve.wait_ge(spread_done, 1)
            step(dve.tensor_copy(allc[:].rearrange("p a c -> p (a c)"), ps_c[:, 0:4 * CHUNKS]))
            for side in range(2):
                step(dve.tensor_scalar(cand[:, side], allc[:, 2:4], ends[:, 3 - side:4 - side], -BIG,
                                       ALU.not_equal, ALU.mult))
                step(dve.tensor_tensor(cand[:, side], cand[:, side], allc[:, 0:2], ALU.add))
                step(dve.tensor_reduce(edge_max[:, side:side + 1], cand[:, side].rearrange("p a c -> p (a c)"),
                                       AX.X, ALU.max))
            step(dve.tensor_tensor_scan(run[:], cut[:, 0:CPOS], score_t[:], edge_max[:, 0:1], ALU.add, ALU.max))
            dve.tensor_tensor_scan(score_t[:, ::-1], cut[:, CPOS:0:-1], run[:, ::-1], edge_max[:, 1:2],
                                   ALU.add, ALU.max).then_inc(m_made, 1)
            for n in range(QUADS):
                dve.wait_ge(m_turned, n + 1)
                sv = score_v[:, 4 * n:4 * n + 4]
                dve.tensor_tensor(sv, sv, ps_t[:, n % 4].rearrange("p j (h c) -> p j h c", c=CHUNKS),
                                  ALU.subtract).then_inc(m_taken, 1)


def segment_sums(nc, e, what, rows, sums, width, sums_at):
    msg = what == "msg"
    with ExitStack() as ctx:
        r_buf = e.sb(f"{what}_rows", [P, RING, GS, F], F32, ctx)
        hot = e.sb(f"{what}_hot", [P, 2, GS, P], F32, ctx)
        weighed = e.sb("weighed", [P, 2, GS, AW], F32, ctx) if msg else None
        ps_sum = e.ps(f"{what}_sum", [P, 2, GS, 512], F32, ctx)
        staged = e.sem(f"{what}_staged")
        rows_in = [e.sem(f"{what}_rows_in{g}") for g in range(RING)]
        pool_turns = e.sem(f"{what}_pool_turns")
        cleared = e.sem(f"{what}_cleared")
        exps_put = e.sem(f"{what}_exps_put")
        weighed_made = e.sem(f"{what}_weighed_made")
        hot_made = e.sem(f"{what}_hot_made")
        summed = e.sem(f"{what}_summed")
        added = e.sem(f"{what}_added")
        block = ctx.enter_context(nc.Block())

        @block.gpsimd
        def _(pool):
            def lap(i, last):
                for g in range(RING):
                    n = i * RING + g
                    pool.wait_ge(staged, n + 1)
                    if msg:
                        wait(pool, weighed_made, n - RING + 1)
                    else:
                        wait(pool, summed, GS * (n - RING + 1))
                    pool.sem_inc(pool_turns, 1)
                    for j in range(GS):
                        pool.indirect_dma_start(out=r_buf[:, g, j, :], out_offset=None, in_=rows[:, :],
                                                in_offset=bass.IndirectOffsetOnAxis(ap=e.stage[:, g, j:j + 1], axis=0)
                                                ).then_inc(rows_in[g], 16)

            laps(pool, lap, LAPS)

        @block.scalar
        def _(act):
            def stage_group(i, g):
                act.activation(e.stage[:, g, :], e.src_idx[:, bass.ds(i * LAP + g * GS, GS)],
                               ACT.Copy).then_inc(staged, 1)

            def lap(i, last):
                for g in range(RING):
                    n = i * RING + g
                    if g == 0:
                        wait(act, rows_in[RING - 1], 16 * GS * i)
                        stage_group(i, RING - 1)
                    elif not last:
                        act.wait_ge(rows_in[g - 1], 16 * GS * (i + 1))
                        stage_group(i + 1, g - 1)
                    if msg:
                        wait(act, summed, GS * (n - 1))
                        act.activation(weighed[:, g % 2, :, F:F + HEADS],
                                       e.score[:, bass.ds(n * (GS * HEADS), GS * HEADS)].rearrange(
                                           "p (j h) -> p j h", h=HEADS), ACT.Copy).then_inc(exps_put, 1)

            for g in range(RING - 1):
                stage_group(0, g)
            laps(act, lap, LAPS)

        @block.vector
        def _(dve):
            at_regs = [dve.alloc_register(f"{what}_at{j}") for j in range(GS)]

            def make_hot(i, g, j):
                if j == 0:
                    wait(dve, summed, GS * (i * RING + g - 1))
                ins = dve.tensor_scalar(hot[:, g % 2, j, :], e.iota_f[:],
                                        e.dst_loc[:, bass.ds(i * LAP + g * GS + j, 1)], None, ALU.is_equal)
                ins.then_inc(hot_made, 1)

            def weigh(i, g):
                n = i * RING + g
                dve.wait_ge(rows_in[g], 16 * GS * (i + 1))
                wait(dve, summed, GS * (n - 1))
                dve.tensor_tensor(
                    weighed[:, g % 2, :, 0:F].rearrange("p j (h d) -> p j h d", d=DH),
                    r_buf[:, g].rearrange("p j (h d) -> p j h d", d=DH),
                    e.score[:, bass.ds(n * (GS * HEADS), GS * HEADS)].rearrange(
                        "p (j h) -> p j h", h=HEADS).unsqueeze(3).to_broadcast([P, GS, HEADS, DH]),
                    ALU.mult).then_inc(weighed_made, 1)

            def add(i, g, j):
                n = i * RING + g
                if j == 0:
                    dve.reg_load(at_regs, sums_at[0:1, bass.ds(n * GS, GS)])
                at = dve.snap(at_regs[j], min_val=0, max_val=(WINS_PAD - 1) * width)
                dve.wait_ge(summed, GS * n + j + 1)
                wait(dve, added, GS * n + j)
                dst = sums[:, bass.ds(at, width)]
                dve.tensor_tensor(dst, dst, ps_sum[:, g % 2, j, 0:width], ALU.add).then_inc(added, 1)

            def lap(i, last):
                for g in range(RING):
                    if msg:
                        weigh(i, g)
                    for j in range(GS):
                        if g < RING - 1:
                            make_hot(i, g + 1, j)
                        elif not last:
                            make_hot(i + 1, 0, j)
                        if g > 0:
                            add(i, g - 1, j)
                        elif not isinstance(i, int) or i > 0:
                            add(i - 1, RING - 1, j)

            dve.memset(sums[:], 0.0).then_inc(cleared, 1)
            if msg:
                dve.memset(weighed[:, :, :, AW - 1:AW], 1.0).then_inc(cleared, 1)
            dve.wait_ge(cleared, 2 if msg else 1)
            for j in range(GS):
                make_hot(0, 0, j)
            laps(dve, lap, LAPS)
            for j in range(GS):
                add(LAPS - 1, RING - 1, j)

        @block.tensor
        def _(pe):
            def lap(i, last):
                for g in range(RING):
                    n = i * RING + g
                    if msg:
                        pe.wait_ge(cleared, 2)
                        pe.wait_ge(exps_put, n + 1)
                        pe.wait_ge(weighed_made, n + 1)
                    else:
                        pe.wait_ge(rows_in[g], 16 * GS * (i + 1))
                    pe.wait_ge(hot_made, GS * (n + 1))
                    wait(pe, added, GS * (n - 1))
                    for j in range(GS):
                        data = weighed[:, g % 2, j, :] if msg else r_buf[:, g, j, :]
                        pe.matmul(ps_sum[:, g % 2, j, 0:width], hot[:, g % 2, j, :], data,
                                  start=True, stop=True).then_inc(summed, 1)

            laps(pe, lap, LAPS)


PAIRS = -(-WINS // 2)
NLAPS = (PAIRS - 1) // 2
assert 2 * NLAPS == PAIRS - 1 and WINS % 2 == 1


def pair_laps(eng, body):
    body(0, 0, 2, 2, 2)
    body(1, 1, 2, 2, 2)
    with eng.Fori(1, NLAPS - 1) as i:
        body(2 * i, 0, 2, 2, 2)
        body(2 * i + 1, 1, 2, 2, 2)
    body(PAIRS - 3, 0, 2, 2, 1)
    body(PAIRS - 2, 1, 2, 1, 0)
    body(PAIRS - 1, 0, 1, 0, 0)


LN_STEPS = 7


def layer_norm(dve, step, dst, src, mv, stats, nw, settled, var_ready, std_ready, count):
    for w in range(nw):
        step(dve.bn_stats(stats[:, w, :], src[:, w, :]), w == nw - 1)
    dve.sem_inc(settled, 1)
    for w in range(nw):
        step(dve.bn_aggr(mv[:, w, 0:2], stats[:, w, :]), w == nw - 1)
    dve.sem_inc(var_ready, 1)
    dve.wait_ge(std_ready, count)
    step(dve.reciprocal(mv[:, 0:nw, 3:4], mv[:, 0:nw, 2:3]))
    for w in range(nw):
        step(dve.tensor_scalar(dst[:, w, :], src[:, w, :], mv[:, w, 0:1], mv[:, w, 3:4],
                               ALU.subtract, ALU.mult), w == nw - 1)


def root(act, mv, nw, eps_col, var_ready, std_ready, count):
    act.wait_ge(var_ready, count)
    act.activation(mv[:, 0:nw, 2:3], mv[:, 0:nw, 1:2], ACT.Sqrt, bias=eps_col).then_inc(std_ready, 1)


def node_ffn(nc, e):
    with ExitStack() as ctx:
        w1_sb = e.sb("w1_sb", [P, FC, HID], F32, ctx)
        w2_sb = e.sb("w2_sb", [P, HC, F], F32, ctx)
        cols = e.sb("cols", [P, 3, HC], F32, ctx)
        neg = e.sb("neg", [P, 2, HC], F32, ctx)
        rows = e.sb("rows", [P, 3, F], F32, ctx)
        x_in = e.sb("x_in", [P, 2, 2, F], F32, ctx)
        rst = e.sb("rst", [P, 2, 2, F], F32, ctx)
        rst_t = e.sb("rst_t", [P, 2, FC, 2 * P], F32, ctx)
        relu_p = e.sb("relu_p", [P, HC, 2 * P], F32, ctx)
        relu_n = e.sb("relu_n", [P, HC, 2 * P], F32, ctx)
        hid = e.sb("hid", [P, HC, 2 * P], F32, ctx)
        zr = e.sb("zr", [P, 2, HEADS], F32, ctx)
        t0 = e.sb("t0", [P, 2, F], F32, ctx)
        mv = e.sb("mv", [P, 2, 4], F32, ctx)
        stats = e.sb("stats", [P, 2, 6], F32, ctx)
        ps_tr = e.ps("ps_tr", [P, FC, 2 * P], F32, ctx)
        ps_h = e.ps("ps_h", [P, 4, 512], F32, ctx)
        ps_f = e.ps("ps_f", [P, 2, 512], F32, ctx)
        par_in = e.sem("par_in")
        x_ld = [e.sem("x_ld0"), e.sem("x_ld1")]
        vec_d = e.sem("vec_d")
        rst_made = e.sem("rst_made")
        rst_turned = e.sem("rst_turned")
        rst_copied = e.sem("rst_copied")
        hid_mm = e.sem("hid_mm")
        relu_d = e.sem("relu_d")
        hid_made = e.sem("hid_made")
        ffn_mm = e.sem("ffn_mm")
        ffn_read = e.sem("ffn_read")
        x1_made = e.sem("x1_made")
        x1_out = e.sem("x1_out")
        neg_made = e.sem("neg_made")
        var_ready = e.sem("var_ready")
        settled = e.sem("settled")
        std_ready = e.sem("std_ready")
        block = ctx.enter_context(nc.Block())
        x_v = e.x.rearrange("(w p) f -> p w f", p=P)
        x1_v = e.x1_rows.rearrange("(w p) f -> p w f", p=P)
        x1_s = e.x1_all[:].rearrange("p (w f) -> p w f", f=F)

        @block.sync
        def _(sp):
            sp.dma_start(w1_sb[:], e.w1.rearrange("(c p) n -> p c n", p=P)).then_inc(par_in, 16)
            sp.dma_start(w2_sb[:], e.w2.rearrange("(c p) n -> p c n", p=P)).then_inc(par_in, 16)
            for k, col in enumerate((e.b1, e.alpha)):
                sp.dma_start(cols[:, k, :], col).then_inc(par_in, 16)
            for k, row in enumerate((e.ln_g, e.ln_b, e.b2)):
                sp.dma_start(rows[:, k, :], row.to_broadcast([P, F])).then_inc(par_in, 16)

            def body(n, par, nw, nxt, nxt2):
                wait(sp, x1_made, n - 1)
                sp.dma_start(x_in[:, par, 0:nw, :], x_v[:, bass.ds(2 * n, nw), :]).then_inc(x_ld[par], 16)

            pair_laps(sp, body)

        @block.gpsimd
        def _(pool):
            def body(n, par, nw, nxt, nxt2):
                pool.wait_ge(x1_made, n + 1)
                pool.dma_start(x1_v[:, bass.ds(2 * n, nw), :], x1_s[:, bass.ds(2 * n, nw), :]).then_inc(x1_out, 16)

            pair_laps(pool, body)
            pool.wait_ge(x1_out, 16 * PAIRS)

        @block.vector
        def _(dve):
            done = [0]

            def pre(n, par, nw, step):
                root_no = 3 * n - 1 if not isinstance(n, int) or n > 0 else 1
                a = e.acc[:, bass.ds(2 * n * AW, nw * AW)].rearrange("p (w a) -> p w a", a=AW)
                h = t0[:, 0:nw]
                step(dve.tensor_scalar(zr[:, 0:nw], a[:, :, F:F + HEADS], 0.5, None, ALU.max))
                step(dve.reciprocal(zr[:, 0:nw], zr[:, 0:nw]))
                step(dve.tensor_tensor(h.rearrange("p w (h d) -> p w h d", d=DH),
                                       a[:, :, 0:F].rearrange("p w (h d) -> p w h d", d=DH),
                                       zr[:, 0:nw].unsqueeze(3).to_broadcast([P, nw, HEADS, DH]), ALU.mult))
                dve.wait_ge(x_ld[par], 8 * (n - par) + 16)
                step(dve.tensor_tensor(h, h, x_in[:, par, 0:nw], ALU.add))
                layer_norm(dve, step, h, h, mv, stats, nw, settled, var_ready, std_ready, root_no)
                step(dve.tensor_tensor(h, h, rows[:, 0:1, :].to_broadcast([P, nw, F]), ALU.mult))
                step(dve.tensor_tensor(rst[:, par, 0:nw], h, rows[:, 1:2, :].to_broadcast([P, nw, F]), ALU.add))
                dve.sem_inc(rst_made, 1)

            def prelu(n, nw):
                wait(dve, ffn_mm, n)
                for hc in range(HC):
                    dve.wait_ge(relu_d, HC * n + hc + 1)
                    dve.scalar_tensor_tensor(hid[:, hc, 0:nw * P], relu_n[:, hc, 0:nw * P], neg[:, 1, hc:hc + 1],
                                             relu_p[:, hc, 0:nw * P], ALU.mult, ALU.add).then_inc(hid_made, 1)

            def post(n, par, nw, step):
                y = t0[:, 0:nw]
                dve.wait_ge(ffn_mm, n + 1)
                dve.tensor_tensor(y, ps_f[:, 0:nw, 0:F], rows[:, 2:3, :].to_broadcast([P, nw, F]),
                                  ALU.add).then_inc(ffn_read, 1)
                dve.wait_ge(ffn_read, n + 1)
                step(dve.tensor_tensor(y, y, rst[:, par, 0:nw], ALU.add))
                first = 3 * n + 3 if nw == 2 else 3 * n + 2
                layer_norm(dve, step, y, y, mv, stats, nw, settled, var_ready, std_ready, first)
                step(dve.tensor_tensor(y, y, rows[:, 0:1, :].to_broadcast([P, nw, F]), ALU.mult))
                step(dve.tensor_tensor(y, y, rows[:, 1:2, :].to_broadcast([P, nw, F]), ALU.add))
                step(dve.tensor_tensor(y, y, x_in[:, par, 0:nw], ALU.add))
                layer_norm(dve, step, x1_s[:, bass.ds(2 * n, nw), :], y, mv, stats, nw,
                           settled, var_ready, std_ready, first + 1)
                dve.sem_inc(x1_made, 1)

            def counted(base):
                k = [0]

                def step(ins, last=True):
                    k[0] += 1
                    ins.then_inc(vec_d, 1)
                    if last:
                        dve.wait_ge(vec_d, base + k[0])
                return step

            PRE = 6 + LN_STEPS
            POST = 4 + 2 * LN_STEPS

            FEWER = 3

            def body(n, par, nw, nxt, nxt2):
                if not isinstance(n, int) or n > 0:
                    post(n - 1, 1 - par, 2, counted(1 + (n + 1) * PRE + (n - 1) * POST - (0 if nxt else FEWER)))
                prelu(n, nw)
                if nxt:
                    pre(n + 1, 1 - par, nxt, counted(1 + (n + 1) * PRE + n * POST))

            dve.wait_ge(par_in, 16 * 7)
            dve.tensor_scalar(neg[:], cols[:, 0:2, :], -1.0, None, ALU.mult).then_inc(neg_made, 1)
            a = e.acc[:].rearrange("p (w a) -> p w a", a=AW)
            dve.tensor_scalar(e.cnt_rec[:].unsqueeze(2), a[:, 0:WINS, AW - 1:AW], 1.0, None, ALU.max).then_inc(vec_d, 1)
            dve.wait_ge(vec_d, 1)
            dve.reciprocal(e.cnt_rec[:], e.cnt_rec[:]).then_inc(neg_made, 1)
            dve.wait_ge(neg_made, 2)
            pre(0, 0, 2, counted(1))
            pair_laps(dve, body)
            post(PAIRS - 1, 0, 1, counted(1 + PAIRS * PRE - FEWER + (PAIRS - 1) * POST))

        @block.scalar
        def _(act):
            act.wait_ge(neg_made, 1)
            act.wait_ge(par_in, 16 * 7)

            def relus(n, nw, chunks):
                for hc in chunks:
                    act.wait_ge(hid_mm, HC * n + hc + 1)
                    if hc == 0:
                        wait(act, hid_made, HC * n)
                    act.activation(relu_p[:, hc, 0:nw * P], ps_h[:, hc % 4, 0:nw * P], ACT.Relu,
                                   bias=cols[:, 0, hc:hc + 1])
                    act.activation(relu_n[:, hc, 0:nw * P], ps_h[:, hc % 4, 0:nw * P], ACT.Relu,
                                   bias=neg[:, 0, hc:hc + 1], scale=-1.0).then_inc(relu_d, 1)

            def copy_turned(n, par, nw):
                act.wait_ge(rst_turned, n + 1)
                act.activation(rst_t[:, par, :, 0:nw * P], ps_tr[:, :, 0:nw * P], ACT.Copy).then_inc(rst_copied, 1)

            def take_root(nw, count):
                root(act, mv, nw, e.eps_col[:], var_ready, std_ready, count)

            def body(n, par, nw, nxt, nxt2):
                later = not isinstance(n, int) or n > 0
                relus(n, nw, range(0, 3))
                if later:
                    take_root(2, 3 * n)
                relus(n, nw, range(3, 6))
                if later:
                    take_root(2, 3 * n + 1)
                relus(n, nw, range(6, HC))
                if nxt:
                    take_root(nxt, 3 * n + 2)
                    copy_turned(n + 1, 1 - par, nxt)

            take_root(2, 1)
            copy_turned(0, 0, 2)
            pair_laps(act, body)
            take_root(1, 3 * PAIRS - 1)
            take_root(1, 3 * PAIRS)

        @block.tensor
        def _(pe):
            pe.wait_ge(par_in, 16 * 7)

            def turn(n, par, nw):
                pe.wait_ge(rst_made, n + 1)
                for w in range(nw):
                    for c in range(FC):
                        mm = pe.transpose(ps_tr[:, c, w * P:(w + 1) * P], rst[:, par, w, c * P:(c + 1) * P],
                                          e.ident_f[:])
                mm.then_inc(rst_turned, 1)

            def body(n, par, nw, nxt, nxt2):
                pe.wait_ge(rst_copied, n + 1)
                for hc in range(HC):
                    wait(pe, relu_d, HC * n + hc - 3)
                    for c in range(FC):
                        mm = pe.matmul(ps_h[:, hc % 4, 0:nw * P], w1_sb[:, c, hc * P:(hc + 1) * P],
                                       rst_t[:, par, c, 0:nw * P], start=(c == 0), stop=(c == FC - 1))
                    mm.then_inc(hid_mm, 1)
                wait(pe, ffn_read, n)
                for hc in range(HC):
                    pe.wait_ge(hid_made, HC * n + hc + 1)
                    for w in range(nw):
                        mm = pe.matmul(ps_f[:, w, 0:F], hid[:, hc, w * P:(w + 1) * P], w2_sb[:, hc, :],
                                       start=(hc == 0), stop=(hc == HC - 1))
                mm.then_inc(ffn_mm, 1)
                if nxt:
                    turn(n + 1, 1 - par, nxt)

            turn(0, 0, 2)
            pair_laps(pe, body)


def node_out(nc, e):
    with ExitStack() as ctx:
        wt_sb = e.sb("wt_sb", [P, FC, F], F32, ctx)
        bl_row = e.sb("bl_row", [P, 1, F], F32, ctx)
        mean = e.sb("mean", [P, 2, 2, F], F32, ctx)
        mean_t = e.sb("mean_t", [P, 2, FC, 2 * P], F32, ctx)
        y = e.sb("y", [P, 2, F], F32, ctx)
        res = e.sb("res", [P, 2, 2, F], F32, ctx)
        mv = e.sb("mv_o", [P, 2, 4], F32, ctx)
        stats = e.sb("stats_o", [P, 2, 6], F32, ctx)
        ps_tr = e.ps("ps_tro", [P, 2, FC, 2 * P], F32, ctx)
        ps_y = e.ps("ps_y", [P, 2, 2, 512], F32, ctx)
        par_in = e.sem("o_par_in")
        vec_d = e.sem("o_vec_d")
        mean_made = e.sem("mean_made")
        mean_turned = e.sem("mean_turned")
        mean_copied = e.sem("mean_copied")
        y_mm = e.sem("y_mm")
        y_read = e.sem("y_read")
        var_ready = e.sem("o_var_ready")
        settled = e.sem("o_settled")
        std_ready = e.sem("o_std_ready")
        res_made = e.sem("res_made")
        res_out = [e.sem("res_out0"), e.sem("res_out1")]
        block = ctx.enter_context(nc.Block())
        x1_s = e.x1_all[:].rearrange("p (w f) -> p w f", f=F)
        full = (WINS - 1) * P
        out_v = e.out[0:full, :].rearrange("(w p) f -> p w f", p=P)

        @block.sync
        def _(sp):
            sp.dma_start(wt_sb[:], e.wT.rearrange("(c p) n -> p c n", p=P)).then_inc(par_in, 16)
            sp.dma_start(bl_row[:, 0, :], e.bl.to_broadcast([P, F])).then_inc(par_in, 16)

            def body(n, par, nw, nxt, nxt2):
                sp.wait_ge(res_made, n + 1)
                if nw == 2:
                    sp.dma_start(out_v[:, bass.ds(2 * n, 2), :], res[:, par]).then_inc(res_out[par], 16)
                else:
                    rest = N_NODES - full
                    sp.dma_start(e.out[full:N_NODES, :], res[0:rest, par, 0, :]).then_inc(res_out[par], 16)

            pair_laps(sp, body)
            sp.wait_ge(res_out[0], 16 * (NLAPS + 1))
            sp.wait_ge(res_out[1], 16 * NLAPS)

        @block.vector
        def _(dve):
            STEPS = 1 + LN_STEPS

            def take_mean(n, par, nw):
                wait(dve, mean_turned, n - 1)
                for w in range(nw):
                    ins = dve.tensor_scalar(mean[:, par, w, :], e.agg[:, bass.ds((2 * n + w) * F, F)],
                                            e.cnt_rec[:, bass.ds(2 * n + w, 1)], None, ALU.mult)
                ins.then_inc(mean_made, 1)

            def body(n, par, nw, nxt, nxt2):
                k = [0]

                def step(ins, last=True):
                    k[0] += 1
                    ins.then_inc(vec_d, 1)
                    if last:
                        dve.wait_ge(vec_d, n * STEPS + k[0])

                if nxt2:
                    take_mean(n + 2, par, nxt2)
                dve.wait_ge(y_mm, n + 1)
                dve.tensor_tensor(y[:, 0:nw], ps_y[:, par, 0:nw, 0:F], bl_row[:].to_broadcast([P, nw, F]),
                                  ALU.add).then_inc(y_read, 1)
                dve.wait_ge(y_read, n + 1)
                step(dve.scalar_tensor_tensor(y[:, 0:nw], y[:, 0:nw], 0.0, x1_s[:, bass.ds(2 * n, nw), :],
                                              ALU.max, ALU.add))
                wait(dve, res_out[par], 8 * (n - par))
                layer_norm(dve, step, res[:, par], y, mv, stats, nw, settled, var_ready, std_ready, n + 1)
                dve.sem_inc(res_made, 1)

            dve.wait_ge(par_in, 32)
            take_mean(0, 0, 2)
            take_mean(1, 1, 2)
            pair_laps(dve, body)

        @block.scalar
        def _(act):
            def copy_turned(n, par, nw):
                act.wait_ge(mean_turned, n + 1)
                wait(act, y_mm, n - 1)
                act.activation(mean_t[:, par, :, 0:nw * P], ps_tr[:, par, :, 0:nw * P],
                               ACT.Copy).then_inc(mean_copied, 1)

            def body(n, par, nw, nxt, nxt2):
                if nxt:
                    copy_turned(n + 1, 1 - par, nxt)
                root(act, mv, nw, e.eps_col[:], var_ready, std_ready, n + 1)

            copy_turned(0, 0, 2)
            pair_laps(act, body)

        @block.tensor
        def _(pe):
            pe.wait_ge(par_in, 32)

            def turn(n, par, nw):
                pe.wait_ge(mean_made, n + 1)
                wait(pe, mean_copied, n - 1)
                for w in range(nw):
                    for c in range(FC):
                        mm = pe.transpose(ps_tr[:, par, c, w * P:(w + 1) * P], mean[:, par, w, c * P:(c + 1) * P],
                                          e.ident_f[:])
                mm.then_inc(mean_turned, 1)

            def body(n, par, nw, nxt, nxt2):
                if nxt:
                    turn(n + 1, 1 - par, nxt)
                pe.wait_ge(mean_copied, n + 1)
                wait(pe, y_read, n - 1)
                for w in range(nw):
                    for c in range(FC):
                        mm = pe.matmul(ps_y[:, par, w, 0:F], mean_t[:, par, c, w * P:(w + 1) * P], wt_sb[:, c, :],
                                       start=(c == 0), stop=(c == FC - 1))
                mm.then_inc(y_mm, 1)

            turn(0, 0, 2)
            pair_laps(pe, body)


_INS = ["x", "xT", "edges", "wqkv", "ln_g", "ln_b", "w1", "b1", "alpha", "w2", "b2", "wT", "bl"]


def kernel(**inputs):
    import numpy as _np
    import concourse.bacc as _bacc
    from concourse.bass_utils import run_bass_kernel_spmd as _run

    g = {k: _np.asarray(v) for k, v in inputs.items()}
    x = _np.zeros((NODES_PAD, F), _np.float32)
    x[:N_NODES] = g["x"]
    edges = _np.zeros((TILES_PAD, 2, P), _np.int32)
    edges[:, 1] = NO_NODE
    pad = TILES_PAD * P - N_EDGES
    edges[:, 0] = _np.concatenate([g["src"], _np.zeros(pad, _np.int32)]).reshape(TILES_PAD, P)
    edges[:, 1] = _np.concatenate([g["dst"], _np.full(pad, NO_NODE, _np.int32)]).reshape(TILES_PAD, P)
    arrays = {
        "x": x,
        "xT": x.T,
        "edges": edges.reshape(TILES_PAD, 2 * P),
        "wqkv": _np.concatenate([g["L0_gnn_Wk"], g["L0_gnn_Wv"], g["L0_gnn_Wq"]], axis=1),
        "ln_g": g["L0_gnn_ln_g"].reshape(1, F),
        "ln_b": g["L0_gnn_ln_b"].reshape(1, F),
        "w1": g["L0_gnn_W1"],
        "b1": g["L0_gnn_b1"].reshape(HC, P).T,
        "alpha": g["L0_gnn_prelu_alpha"].reshape(HC, P).T,
        "w2": g["L0_gnn_W2"],
        "b2": g["L0_gnn_b2"].reshape(1, F),
        "wT": g["L1_gnn_W"].T,
        "bl": g["L1_gnn_b"].reshape(1, F),
    }
    arrays = {f"in_{k}": _np.ascontiguousarray(a) for k, a in arrays.items()}
    nc = _bacc.Bacc("TRN2", target_bir_lowering=False, num_devices=1)
    args = [nc.dram_tensor(f"in_{k}", arrays[f"in_{k}"].shape, mybir.dt.from_np(arrays[f"in_{k}"].dtype),
                           kind="ExternalInput").ap() for k in _INS]
    args.append(nc.dram_tensor("out_0", (N_NODES, F), F32, kind="ExternalOutput").ap())
    build(nc, *args)
    r = _run(nc, [arrays], core_ids=[0])
    return r.results[0]["out_0"]
```

```python
from contextlib import ExitStack

import concourse.bass as bass
from concourse import mybir

ALU = mybir.AluOpType
ACT = mybir.ActivationFunctionType
AX = mybir.AxisListType
F32 = mybir.dt.float32
BF16 = mybir.dt.bfloat16
I32 = mybir.dt.int32

P = 128
N_NODES, F, HEADS = 6250, 256, 8
DH = F // HEADS
N_EDGES = 100000
HID = 4 * F
HC = HID // P
FC = F // P
BIG = 1.0e30
EPS = 1e-5

WINS = -(-N_NODES // P)
WINS_PAD = WINS + 1
NODES_PAD = WINS_PAD * P
NO_NODE = WINS * P

TILES = -(-N_EDGES // P)
TROWS = 112
TPR = -(-TILES // TROWS)
TILES_PAD = TROWS * TPR
GS = 4
RING = 4
LAP = GS * RING
assert LAP * HEADS == P
SLOTS = -(-(TILES + WINS - 1) // (2 * LAP)) * 2 * LAP
SLOTS_TAB = -(-SLOTS // P) * P
SC = SLOTS_TAB // P
LAPS = SLOTS // LAP
AW = F + HEADS + 1
RW = F + AW
ENDS = 2 * LAP + 1

assert SLOTS % (2 * LAP) == 0 and SLOTS_TAB >= SLOTS + LAP and TILES_PAD >= TILES


def wait(eng, sem, value):
    if not isinstance(value, int) or value > 0:
        eng.wait_ge(sem, value)


def laps(eng, body, count):
    body(0, False)
    with eng.Fori(1, count - 1) as i:
        body(i, False)
    body(count - 1, True)


class Shared:

    def __init__(self, nc, life):
        self.nc, self.life = nc, life

    def sb(self, name, shape, dt, life):
        return life.enter_context(self.nc.sbuf_tensor(name, shape, dt))

    def ps(self, name, shape, dt, life):
        return life.enter_context(self.nc.psum_tensor(name, shape, dt))

    def sem(self, name):
        return self.life.enter_context(self.nc.semaphore(name))


def build(nc, x, xT, edges, wqkv, ln_g, ln_b, w1, b1, alpha, w2, b2, wT, bl, out):
    with ExitStack() as top:
        e = Shared(nc, top)
        e.x, e.xT, e.edges, e.wqkv, e.ln_g, e.ln_b = x, xT, edges, wqkv, ln_g, ln_b
        e.w1, e.b1, e.alpha, e.w2, e.b2, e.wT, e.bl, e.out = w1, b1, alpha, w2, b2, wT, bl, out
        e.kv_rows = nc.dram_tensor("kv_rows", (NODES_PAD, 2 * F), F32).ap()
        e.x1_rows = nc.dram_tensor("x1_rows", (WINS * P, F), F32).ap()
        e.cut_rows = nc.dram_tensor("cut_rows", (SLOTS_TAB, P + 1), F32).ap()

        e.src_idx = e.sb("src_idx", [P, SLOTS_TAB], I32, top)
        e.neg_loc = e.sb("neg_loc", [P, SLOTS_TAB], F32, top)
        e.win_at = e.sb("win_at", [P, SLOTS_TAB], I32, top)
        e.iota_f = e.sb("iota_f", [P, P], F32, top)
        e.ident_f = e.sb("ident_f", [P, P], F32, top)
        e.ident_b = e.sb("ident_b", [P, P], BF16, top)
        e.eps_col = e.sb("eps_col", [P, 1], F32, top)
        e.stage = e.sb("stage", [P, 2, RING, GS], I32, top)
        e.acc = e.sb("acc", [P, WINS_PAD * AW], F32, top)

        with ExitStack() as life:
            e.head_eq = e.sb("head_eq", [P, P], F32, life)
            e.slot_sel = e.sb("slot_sel", [P, LAP], F32, life)
            e.apart = e.sb("apart", [P, LAPS, 2, ENDS], BF16, life)
            e.goes_on = e.sb("goes_on", [P, LAPS], F32, life)
            e.first_loc = e.sb("first_loc", [P, LAPS], F32, life)
            build_tables(nc, e)
            e.q_all = e.sb("q_all", [P, WINS_PAD * F], F32, life)
            project(nc, e)
            edge_attention(nc, e)
        e.cnt_rec = e.sb("cnt_rec", [P, WINS], F32, top)
        e.x1_all = e.sb("x1_all", [P, WINS * F], F32, top)
        node_ffn(nc, e)
        edge_mean(nc, e)
        node_out(nc, e)


def build_tables(nc, e):
    with ExitStack() as ctx:
        ed = e.sb("ed", [TROWS, TPR, 2 * P], I32, ctx)
        edge_dst = e.sb("edge_dst", [TROWS, TPR, 2], F32, ctx)
        thr = e.sb("thr", [TROWS, WINS + 1], F32, ctx)
        past_last = e.sb("past_last", [TROWS, TPR, WINS], F32, ctx)
        past_first = e.sb("past_first", [TROWS, TPR, WINS], F32, ctx)
        ones = e.sb("ones", [P, P], F32, ctx)
        tri = e.sb("tri", [WINS, WINS], F32, ctx)
        wcol = e.sb("wcol", [WINS, 8], F32, ctx)
        slot_row = e.sb("slot_row", [WINS, SLOTS_TAB], F32, ctx)
        slot_col = e.sb("slot_col", [P, SC], F32, ctx)
        begun = e.sb("begun", [WINS, SLOTS_TAB], F32, ctx)
        ended = e.sb("ended", [WINS, SLOTS_TAB], F32, ctx)
        own = e.sb("own", [WINS, SLOTS_TAB], F32, ctx)
        tile_f = e.sb("tile_f", [P, SC], F32, ctx)
        tile_i = e.sb("tile_i", [P, SC], I32, ctx)
        win_base = e.sb("win_base", [P, SC], F32, ctx)
        got = e.sb("got", [P, SC, 2 * P], I32, ctx)
        src_f = e.sb("src_f", [P, SC, P], F32, ctx)
        loc_f = e.sb("loc_f", [P, SC, P], F32, ctx)
        in_lo = e.sb("in_lo", [P, SC, P], F32, ctx)
        in_both = e.sb("in_both", [P, SC, P], F32, ctx)
        node1 = e.sb("node1", [P, SC, P], F32, ctx)
        key = e.sb("key", [P, SC, P], F32, ctx)
        cut = e.sb("cut", [P, SC, P + 1], F32, ctx)
        end_diag = e.sb("end_diag", [P, 2, SC, P], F32, ctx)
        end_key = e.sb("end_key", [P, 2, SLOTS_TAB], F32, ctx)
        picked = e.sb("picked", [P, 2, SLOTS_TAB], F32, ctx)
        own_key = e.sb("own_key", [P, 2, SLOTS_TAB // LAP], F32, ctx)
        first_win = e.sb("first_win", [P, LAPS], F32, ctx)
        ps_w = e.ps("ps_w", [P, 512], F32, ctx)
        ps_s = e.ps("ps_s", [P, 512], F32, ctx)
        ps_row = e.ps("ps_row", [P, 2, 512], F32, ctx)
        ps_t = e.ps("ps_t", [P, 4, 4, P], F32, ctx)
        consts = e.sem("consts")
        ed_in = e.sem("ed_in")
        tab_d = e.sem("tab_d")
        tab_pe = e.sem("tab_pe")
        rows_in = e.sem("rows_in")
        cut_out = e.sem("cut_out")
        block = ctx.enter_context(nc.Block())

        @block.sync
        def _(sp):
            sp.dma_start(ed[:], e.edges.rearrange("(p t) c -> p t c", p=TROWS)).then_inc(ed_in, 16)
            sp.wait_ge(tab_d, 23)
            sp.dma_start(e.cut_rows.rearrange("(c p) r -> p c r", p=P), cut[:]).then_inc(cut_out, 16)
            sp.wait_ge(cut_out, 16)

        @block.gpsimd
        def _(pool):
            pool.iota(thr[:], [[P, WINS + 1]], base=0, channel_multiplier=0,
                      allow_small_or_imprecise_dtypes=True).then_inc(consts, 1)
            pool.memset(ones[:], 1.0).then_inc(consts, 1)
            pool.iota(slot_row[:], [[1, SLOTS_TAB]], base=0, channel_multiplier=0,
                      allow_small_or_imprecise_dtypes=True).then_inc(consts, 1)
            pool.iota(slot_col[:], [[P, SC]], base=0, channel_multiplier=1,
                      allow_small_or_imprecise_dtypes=True).then_inc(consts, 1)
            pool.memset(cut[:], 0.0).then_inc(consts, 1)
            pool.iota(e.iota_f[:], [[1, P]], base=0, channel_multiplier=0,
                      allow_small_or_imprecise_dtypes=True).then_inc(consts, 1)
            pool.memset(e.ident_f[:], 0.0).then_inc(consts, 1)
            pool.memset(e.head_eq[:], 1.0).then_inc(consts, 1)
            pool.memset(e.eps_col[:], EPS).then_inc(consts, 1)
            pool.wait_ge(consts, 9)
            pool.affine_select(tri[:], ones[0:WINS, 0:WINS], [[1, WINS]], ALU.is_gt, 0.0, base=0,
                               channel_multiplier=-1).then_inc(consts, 1)
            pool.affine_select(e.ident_f[:], e.ident_f[:], [[-1, P]], ALU.not_equal, 1.0, base=0,
                               channel_multiplier=1).then_inc(consts, 1)
            pool.affine_select(e.head_eq[:].rearrange("p (h s) -> p h s", s=LAP),
                               e.head_eq[:].rearrange("p (h s) -> p h s", s=LAP),
                               [[-LAP, HEADS], [0, LAP]], ALU.is_ge, 0.0, base=0,
                               channel_multiplier=1).then_inc(consts, 1)
            pool.wait_ge(consts, 12)
            pool.affine_select(e.head_eq[:].rearrange("p (h s) -> p h s", s=LAP),
                               e.head_eq[:].rearrange("p (h s) -> p h s", s=LAP),
                               [[LAP, HEADS], [0, LAP]], ALU.is_ge, 0.0, base=LAP - 1,
                               channel_multiplier=-1).then_inc(consts, 1)
            pool.wait_ge(tab_d, 14)
            for c in range(SC):
                pool.indirect_dma_start(out=got[:, c, :], out_offset=None, in_=e.edges[:, :],
                                        in_offset=bass.IndirectOffsetOnAxis(ap=tile_i[:, c:c + 1], axis=0)
                                        ).then_inc(rows_in, 16)

        @block.vector
        def _(dve):
            done = [0]

            def step(ins):
                done[0] += 1
                ins.then_inc(tab_d, 1)
                dve.wait_ge(tab_d, done[0])

            dve.wait_ge(consts, 13)
            dve.wait_ge(ed_in, 16)
            step(dve.tensor_copy(edge_dst[:], ed[:, :, P::P - 1]))
            step(dve.tensor_tensor(past_last[:], thr[:, 0:WINS].unsqueeze(1).to_broadcast([TROWS, TPR, WINS]),
                                   edge_dst[:, :, 1:2].to_broadcast([TROWS, TPR, WINS]), ALU.is_gt))
            step(dve.tensor_tensor(past_first[:], thr[:, 1:WINS + 1].unsqueeze(1).to_broadcast([TROWS, TPR, WINS]),
                                   edge_dst[:, :, 0:1].to_broadcast([TROWS, TPR, WINS]), ALU.is_gt))
            dve.wait_ge(tab_pe, 1)
            step(dve.tensor_copy(wcol[:, 0:2], ps_w[0:WINS, 0:2]))
            step(dve.tensor_tensor(wcol[:, 2:3], wcol[:, 1:2], wcol[:, 0:1], ALU.subtract))
            dve.wait_ge(tab_pe, 2)
            step(dve.tensor_copy(wcol[:, 3:4], ps_w[0:WINS, 2:3]))
            step(dve.tensor_tensor(wcol[:, 4:5], wcol[:, 3:4], wcol[:, 2:3], ALU.add))
            step(dve.tensor_tensor(wcol[:, 5:6], wcol[:, 0:1], wcol[:, 3:4], ALU.subtract))
            step(dve.tensor_scalar(begun[:], slot_row[:], wcol[:, 3:4], None, ALU.is_ge))
            step(dve.tensor_scalar(ended[:], slot_row[:], wcol[:, 4:5], None, ALU.is_ge))
            step(dve.tensor_tensor(own[:], begun[:], ended[:], ALU.subtract))
            dve.wait_ge(tab_pe, 3)
            step(dve.tensor_tensor(tile_f[:], ps_s[:, 0:SC], slot_col[:], ALU.add))
            step(dve.tensor_scalar(tile_f[:], tile_f[:], float(TILES_PAD - 1), None, ALU.min))
            step(dve.tensor_copy(tile_i[:], tile_f[:]))
            step(dve.tensor_scalar(win_base[:], ps_s[:, SC:2 * SC], float(P), None, ALU.mult))
            dve.wait_ge(rows_in, 16 * SC)
            step(dve.tensor_tensor(loc_f[:], got[:, :, P:2 * P],
                                   win_base[:].unsqueeze(2).to_broadcast([P, SC, P]), ALU.subtract))
            step(dve.tensor_scalar(in_lo[:], loc_f[:], 0.0, None, ALU.is_ge))
            step(dve.scalar_tensor_tensor(in_both[:], loc_f[:], float(P), in_lo[:], ALU.is_lt, ALU.mult))
            step(dve.tensor_scalar(node1[:], got[:, :, P:2 * P], 1.0, None, ALU.add))
            step(dve.tensor_tensor(key[:], node1[:], in_both[:], ALU.mult))
            step(dve.tensor_copy(src_f[:], got[:, :, 0:P]))
            step(dve.tensor_tensor(cut[:, :, 1:P], key[:, :, 1:P], key[:, :, 0:P - 1], ALU.not_equal))
            step(dve.tensor_scalar(cut[:, :, 1:P], cut[:, :, 1:P], -BIG, None, ALU.mult))
            step(dve.tensor_tensor(end_diag[:], e.ident_f[:].unsqueeze(1).unsqueeze(1).to_broadcast([P, 2, SC, P]),
                                   key[:, :, P - 1::1 - P].rearrange("p c e -> p e c").unsqueeze(3).to_broadcast(
                                       [P, 2, SC, P]), ALU.mult))
            dve.wait_ge(tab_pe, 4)
            half = SLOTS_TAB // 2
            for n in range(2):
                cols = slice(n * half, (n + 1) * half)
                step(dve.tensor_copy(e.win_at[:, cols], ps_row[:, n, 0:half]))
            for c in range(SC):
                dve.wait_ge(tab_pe, 5 + c)
                step(dve.tensor_copy(e.src_idx[:, c * P:(c + 1) * P], ps_t[:, c % 4, 0, :]))
                step(dve.tensor_scalar(e.neg_loc[:, c * P:(c + 1) * P], ps_t[:, c % 4, 1, :], -1.0, None, ALU.mult))
            step(dve.tensor_copy(e.ident_b[:], e.ident_f[:]))
            step(dve.tensor_reduce(e.slot_sel[:], e.ident_f[:].rearrange("p (h s) -> p s h", s=LAP),
                                   AX.X, ALU.add))
            dve.wait_ge(tab_pe, 5 + SC)
            for n in range(4):
                step(dve.tensor_copy(end_key[:, n // 2, (n % 2) * half:(n % 2 + 1) * half],
                                     ps_t[:, n].rearrange("p a b -> p (a b)")[:, 0:half]))
            step(dve.tensor_tensor(picked[:].rearrange("p e (l s) -> p e l s", s=LAP),
                                   end_key[:].rearrange("p e (l s) -> p e l s", s=LAP),
                                   e.slot_sel[:].unsqueeze(1).unsqueeze(1).to_broadcast([P, 2, SLOTS_TAB // LAP, LAP]),
                                   ALU.mult))
            step(dve.tensor_reduce(own_key[:], picked[:].rearrange("p e (l s) -> p e l s", s=LAP), AX.X, ALU.add))
            step(dve.memset(e.apart[:], 1.0))
            for side in range(2):
                mine = own_key[:, 1 - side, 0:LAPS].unsqueeze(2)
                for end in range(2):
                    step(dve.tensor_tensor(e.apart[:, :, side, end * LAP:(end + 1) * LAP],
                                           end_key[:, end, 0:SLOTS].rearrange("p (l s) -> p l s", s=LAP),
                                           mine.to_broadcast([P, LAPS, LAP]), ALU.not_equal))
                step(dve.tensor_tensor(e.apart[:, 1:LAPS, side, ENDS - 1:ENDS],
                                       end_key[:, 0, LAP - 1:SLOTS - 1:LAP].unsqueeze(2), mine[:, 1:LAPS],
                                       ALU.not_equal))
            step(dve.tensor_scalar(e.goes_on[:].unsqueeze(2), e.apart[:, :, 0, ENDS - 1:ENDS], 0.0, None,
                                   ALU.is_equal))
            step(dve.tensor_scalar(e.apart[:], e.apart[:], -BIG, None, ALU.mult))
            step(dve.tensor_scalar(first_win[:], e.win_at[:, 0:SLOTS:LAP], -float(P), -1.0, ALU.mult, ALU.add))
            step(dve.tensor_tensor(e.first_loc[:], end_key[:, 1, 0:SLOTS:LAP], first_win[:], ALU.add))

        @block.tensor
        def _(pe):
            pe.wait_ge(tab_d, 3)
            for r in range(TPR):
                pe.matmul(ps_w[0:WINS, 0:1], past_last[:, r, :], ones[0:TROWS, 0:1],
                          start=(r == 0), stop=(r == TPR - 1))
            for r in range(TPR):
                mm = pe.matmul(ps_w[0:WINS, 1:2], past_first[:, r, :], ones[0:TROWS, 0:1],
                               start=(r == 0), stop=(r == TPR - 1))
            mm.then_inc(tab_pe, 1)
            pe.wait_ge(tab_d, 5)
            pe.matmul(ps_w[0:WINS, 2:3], tri[:], wcol[:, 2:3], start=True, stop=True).then_inc(tab_pe, 1)
            pe.wait_ge(tab_d, 11)
            for c in range(SC):
                pe.matmul(ps_s[:, c:c + 1], own[:, c * P:(c + 1) * P], wcol[:, 5:6], start=True, stop=True)
                mm = pe.matmul(ps_s[:, SC + c:SC + c + 1], ended[:, c * P:(c + 1) * P], ones[0:WINS, 0:1],
                               start=True, stop=True)
            mm.then_inc(tab_pe, 1)
            half = SLOTS_TAB // 2
            for n in range(2):
                mm = pe.matmul(ps_row[:, n, 0:half], ones[0:WINS, :], ended[:, n * half:(n + 1) * half],
                               start=True, stop=True)
            mm.then_inc(tab_pe, 1)
            pe.wait_ge(tab_d, 21)
            for c in range(SC):
                if c >= 4:
                    pe.wait_ge(tab_d, 26 + 2 * (c - 3))
                pe.transpose(ps_t[:, c % 4, 0, :], src_f[:, c, :], e.ident_f[:])
                pe.transpose(ps_t[:, c % 4, 1, :], loc_f[:, c, :], e.ident_f[:]).then_inc(tab_pe, 1)
            pe.wait_ge(tab_d, 26 + 2 * SC)
            flat = end_diag[:].rearrange("p e c n -> p (e c n)")
            for n in range(4):
                mm = pe.matmul(ps_t[:, n].rearrange("p a b -> p (a b)")[:, 0:half], ones[:],
                               flat[:, n * half:(n + 1) * half], start=True, stop=True)
            mm.then_inc(tab_pe, 1)



QB = 5
QLAPS = WINS_PAD // (2 * QB)
Q_SCALE = float(F) ** -0.5


def project(nc, e):
    assert WINS_PAD % (2 * QB) == 0 and Q_SCALE == 2.0 ** -4
    with ExitStack() as ctx:
        xt = e.sb("xt", [P, 2, FC, QB * P], F32, ctx)
        w_sb = e.sb("w_sb", [P, FC, 3 * F], F32, ctx)
        kv_sb = e.sb("kv_sb", [P, 2, QB, 2 * F], F32, ctx)
        ps_kv = e.ps("ps_kv", [P, 2, 512], F32, ctx)
        ps_q = e.ps("ps_q", [P, 2, 512], F32, ctx)
        w_in = e.sem("w_in")
        xt_in = [e.sem("xt_in0"), e.sem("xt_in1")]
        projected = e.sem("projected")
        kv_copied = e.sem("kv_copied")
        kv_stored = [e.sem("kv_stored0"), e.sem("kv_stored1")]
        q_kept = e.sem("q_kept")
        block = ctx.enter_context(nc.Block())
        xT_v = e.xT.rearrange("(c p) n -> p c n", p=P)
        kv_v = e.kv_rows.rearrange("(w p) f -> p w f", p=P)

        @block.sync
        def _(sp):
            def load(i, b):
                wait(sp, projected, (2 * i + b - 1) * QB)
                sp.dma_start(xt[:, b], xT_v[:, :, bass.ds((2 * i + b) * (QB * P), QB * P)]).then_inc(xt_in[b], 16)

            def store(i, b):
                sp.wait_ge(kv_copied, (2 * i + b + 1) * QB)
                sp.dma_start(kv_v[:, bass.ds((2 * i + b) * QB, QB), :], kv_sb[:, b]).then_inc(kv_stored[b], 16)

            def lap(i, last):
                for b in range(2):
                    store(i, b)
                    if not last:
                        load(i + 1, b)

            sp.dma_start(w_sb[:], e.wqkv.rearrange("(c p) n -> p c n", p=P)).then_inc(w_in, 16)
            load(0, 0)
            load(0, 1)
            laps(sp, lap, QLAPS)
            for b in range(2):
                sp.wait_ge(kv_stored[b], 16 * QLAPS)

        @block.tensor
        def _(pe):
            def lap(i, last):
                for b in range(2):
                    pe.wait_ge(xt_in[b], 16 * (i + 1))
                    for m in range(QB):
                        done = (2 * i + b) * QB + m
                        par = (b * QB + m) % 2
                        wait(pe, kv_copied, done - 1)
                        wait(pe, q_kept, done - 1)
                        for c in range(FC):
                            pe.matmul(ps_kv[:, par, :], xt[:, b, c, m * P:(m + 1) * P], w_sb[:, c, 0:2 * F],
                                      start=(c == 0), stop=(c == FC - 1))
                        for c in range(FC):
                            mm = pe.matmul(ps_q[:, par, 0:F], xt[:, b, c, m * P:(m + 1) * P], w_sb[:, c, 2 * F:],
                                           start=(c == 0), stop=(c == FC - 1))
                        mm.then_inc(projected, 1)

            pe.wait_ge(w_in, 16)
            laps(pe, lap, QLAPS)

        @block.scalar
        def _(act):
            def lap(i, last):
                for b in range(2):
                    wait(act, kv_stored[b], 16 * i)
                    for m in range(QB):
                        done = (2 * i + b) * QB + m
                        par = (b * QB + m) % 2
                        act.wait_ge(projected, done + 1)
                        act.activation(kv_sb[:, b, m, :], ps_kv[:, par, :], ACT.Copy).then_inc(kv_copied, 1)

            laps(act, lap, QLAPS)


        @block.vector
        def _(dve):
            def lap(i, last):
                for t in range(2 * QB):
                    done = 2 * QB * i + t
                    dve.wait_ge(projected, done + 1)
                    dve.tensor_scalar(e.q_all[:, bass.ds(done * F, F)], ps_q[:, t % 2, 0:F], Q_SCALE, None,
                                      ALU.mult).then_inc(q_kept, 1)

            laps(dve, lap, QLAPS)


def edge_laps(eng, turn):
    turn(0, 0, 2)
    turn(0, 1, 2)
    with eng.Fori(1, LAPS // 2 - 1) as i:
        turn(i, 0, 2)
        turn(i, 1, 2)
    turn(LAPS // 2 - 1, 0, 1)
    turn(LAPS // 2 - 1, 1, 0)


def following(i, par, by):
    return (i + (par + by) // 2, (par + by) % 2)


def ahead(i, par, g, by):
    n = par * RING + g + by
    return (i + n // (2 * RING), n // RING % 2, n % RING)


def edge_attention(nc, e):
    with ExitStack() as ctx:
        kv = e.sb("kv", [P, 2, RING, GS, RW], F32, ctx)
        hot_s = e.sb("hot_s", [P, 2, GS, P], BF16, ctx)
        hot_t = e.sb("hot_t", [P, 2, GS, P], F32, ctx)
        hot_m = e.sb("hot_m", [P, 2, GS, P], F32, ctx)
        score = e.sb("score", [P, 2, HEADS, LAP], F32, ctx)
        below = e.sb("below", [P, HEADS, LAP], F32, ctx)
        cut = e.sb("cut_in", [P, 2, P + 1], F32, ctx)
        run = e.sb("run", [P, P], F32, ctx)
        run_b = e.sb("run_b", [P, P], F32, ctx)
        top_m = e.sb("top_m", [P, P], F32, ctx)
        spread = e.sb("spread", [P, ENDS], F32, ctx)
        cand = e.sb("cand", [P, 2, ENDS], F32, ctx)
        end_max = e.sb("end_max", [P, 2], F32, ctx)
        drop = e.sb("drop", [P, 2], F32, ctx)
        node_hot = e.sb("node_hot", [P, P], F32, ctx)
        head_drop = e.sb("head_drop", [P, HEADS], F32, ctx)
        rescale = e.sb("rescale", [P, HEADS], F32, ctx)
        ps_hot = e.ps("ps_hot", [P, 2, GS, P], BF16, ctx)
        ps_lap = e.ps("ps_lap", [P, 512], F32, ctx)
        ps_q = e.ps("ps_q2", [P, 2, 2, F], F32, ctx)
        ps_sum = e.ps("ps_sum", [P, GS, 512], F32, ctx)
        turned_score = ps_lap[:, 0:P]
        turned_m = ps_lap[:, P:2 * P]
        all_ends = ps_lap[:, 2 * P:2 * P + ENDS]
        node_drop = ps_lap[:, 3 * P:3 * P + HEADS]

        staged = e.sem("staged")
        rows_in = [[e.sem(f"rows_in{b}{g}") for g in range(RING)] for b in range(2)]
        pool_turns = e.sem("pool_turns")
        act_turns = e.sem("act_turns")
        cut_in = [e.sem("cut_in0"), e.sem("cut_in1")]
        cleared = e.sem("cleared")
        s_far = e.sem("s_far")
        hot_s_made = e.sem("hot_s_made")
        hot_turned = e.sem("hot_turned")
        hot_t_copied = e.sem("hot_t_copied")
        q_picked = e.sem("q_picked")
        multiplied = e.sem("multiplied")
        scored = e.sem("scored")
        score_turned = e.sem("score_turned")
        spread_made = e.sem("spread_made")
        ends_spread = e.sem("ends_spread")
        lap_d = e.sem("lap_d")
        dropped = e.sem("dropped")
        drop_exp = e.sem("drop_exp")
        m_made = e.sem("m_made")
        m_turned = e.sem("m_turned")
        below_made = e.sem("below_made")
        exps_put = e.sem("exps_put")
        drop_rows_made = e.sem("drop_rows_made")
        node_dropped = e.sem("node_dropped")
        rescale_d = e.sem("rescale_d")
        m_far = e.sem("m_far")
        hot_m_made = e.sem("hot_m_made")
        weighed = e.sem("weighed")
        summed = e.sem("summed")
        added = e.sem("added")
        block = ctx.enter_context(nc.Block())

        def group_no(i, par, g):
            return (2 * i + par) * RING + g

        @block.sync
        def _(sp):
            def turn(i, par, left):
                wait(sp, m_made, 2 * i + par - 1)
                for h in range(HEADS):
                    sp.dma_start(cut[h * LAP:(h + 1) * LAP, par, :],
                                 e.cut_rows[bass.ds((2 * i + par) * LAP, LAP), :]).then_inc(cut_in[par], 16)

            edge_laps(sp, turn)

        @block.gpsimd
        def _(pool):
            def turn(i, par, left):
                for g in range(RING):
                    n = group_no(i, par, g)
                    pool.wait_ge(staged, 2 * i + par + 1)
                    wait(pool, summed, GS * (n - 2 * RING + 1))
                    pool.sem_inc(pool_turns, 1)
                    for j in range(GS):
                        pool.indirect_dma_start(out=kv[:, par, g, j, 0:2 * F], out_offset=None, in_=e.kv_rows[:, :],
                                                in_offset=bass.IndirectOffsetOnAxis(ap=e.stage[:, par, g, j:j + 1],
                                                                                    axis=0)
                                                ).then_inc(rows_in[par][g], 16)

            edge_laps(pool, turn)

        @block.scalar
        def _(act):
            def stage_lap(i, par):
                for g in range(RING):
                    wait(act, rows_in[par][g], 16 * GS * i)
                act.sem_inc(act_turns, 1)
                act.activation(e.stage[:, par].rearrange("p g j -> p (g j)"),
                               e.src_idx[:, bass.ds((2 * i + par) * LAP, LAP)], ACT.Copy).then_inc(staged, 1)

            def make_hot(i, par, g, hot, far, made, free_sem, free_value):
                n = group_no(i, par, g)
                wait(act, free_sem, free_value)
                act.sem_inc(act_turns, 1)
                for j in range(GS):
                    ins = act.activation(hot[:, g % 2, j, :], e.iota_f[:], ACT.Abs,
                                         bias=e.neg_loc[:, bass.ds(n * GS + j, 1)])
                ins.then_inc(far, 1)
                act.wait_ge(far, n + 1)
                act.activation(hot[:, g % 2], hot[:, g % 2], ACT.Relu, bias=1.0, scale=-1.0).then_inc(made, 1)

            def hot_for_score(i, par, g):
                make_hot(i, par, g, hot_s, s_far, hot_s_made, hot_turned, group_no(i, par, g) - 1)

            def hot_for_sum(i, par, g):
                make_hot(i, par, g, hot_m, m_far, hot_m_made, summed, GS * (group_no(i, par, g) - 1))

            def copy_turned(i, par, g):
                n = group_no(i, par, g)
                act.wait_ge(hot_turned, n + 1)
                wait(act, q_picked, 2 * (n - 1))
                act.activation(hot_t[:, g % 2], ps_hot[:, g % 2], ACT.Copy).then_inc(hot_t_copied, 1)

            def exps(i, par):
                lap = 2 * i + par
                act.wait_ge(dropped, lap + 1)
                act.activation(drop[:, 1:2], drop[:, 0:1], ACT.Exp).then_inc(drop_exp, 1)
                act.wait_ge(below_made, lap + 1)
                act.activation(kv[:, par].rearrange("p g j w -> p (g j) w")[:, :, 2 * F:2 * F + HEADS],
                               below[:].rearrange("p h s -> p s h"), ACT.Exp).then_inc(exps_put, 1)

            def turn(i, par, left):
                if left > 1:
                    stage_lap(*following(i, par, 2))
                for g in range(RING):
                    after = RING * (left + 1) - 1 - g
                    if after >= 8:
                        hot_for_score(*ahead(i, par, g, 8))
                    if after >= 7:
                        copy_turned(*ahead(i, par, g, 7))
                    if after >= 1:
                        hot_for_sum(*ahead(i, par, g, 1))
                if left:
                    exps(*following(i, par, 1))

            stage_lap(0, 0)
            stage_lap(0, 1)
            hot_for_score(0, 0, 0)
            for n in range(7):
                hot_for_score(*ahead(0, 0, n, 1))
                copy_turned(*ahead(0, 0, n, 0))
            hot_for_sum(0, 0, 0)
            act.wait_ge(cleared, 3)
            exps(0, 0)
            edge_laps(act, turn)

        @block.vector
        def _(dve):
            regs = [dve.alloc_register(f"sum_win{j}") for j in range(GS)]
            lap_reg = dve.alloc_register("lap_win")
            LAP_STEPS = 6

            def multiply_half(i, par, g, half):
                if half == 0:
                    dve.wait_ge(rows_in[par][g], 16 * GS * (i + 1))
                dve.wait_ge(q_picked, 2 * group_no(i, par, g) + half + 1)
                rows = kv[:, par, g, 2 * half:2 * half + 2, 0:F]
                dve.tensor_tensor(rows, rows, ps_q[:, half], ALU.mult).then_inc(multiplied, 1)

            def score_group(i, par, g):
                n = group_no(i, par, g)
                if g == 0:
                    wait(dve, below_made, 2 * i + par - 1)
                dve.wait_ge(multiplied, 2 * n + 2)
                dve.tensor_reduce(score[:, par, :, g * GS:(g + 1) * GS].rearrange("p h j -> p j h"),
                                  kv[:, par, g, :, 0:F].rearrange("p j (h d) -> p j h d", d=DH),
                                  AX.X, ALU.add).then_inc(scored, 1)

            def weigh_group(i, par, g):
                if g == 0:
                    dve.wait_ge(exps_put, 2 * i + par + 1)
                rows = kv[:, par, g, :, F:2 * F].rearrange("p j (h d) -> p j h d", d=DH)
                dve.tensor_tensor(rows, rows,
                                  kv[:, par, g, :, 2 * F:2 * F + HEADS].unsqueeze(3).to_broadcast([P, GS, HEADS, DH]),
                                  ALU.mult).then_inc(weighed, 1)

            def add_slot(i, par, g, j):
                n = group_no(i, par, g)
                if j == 0:
                    dve.reg_load(regs, e.win_at[0:1, bass.ds(n * GS, GS)])
                win = dve.snap(regs[j], min_val=0, max_val=WINS_PAD - 1)
                dve.wait_ge(summed, GS * n + j + 1)
                wait(dve, added, GS * n + j)
                dst = e.acc[:, bass.ds(win * AW, AW)]
                dve.tensor_tensor(dst, dst, ps_sum[:, j, 0:AW], ALU.add).then_inc(added, 1)

            def own_ends(i, par):
                lap = 2 * i + par
                dve.wait_ge(cut_in[par], 16 * HEADS * (i + 1))
                dve.wait_ge(score_turned, lap + 1)
                dve.tensor_tensor_scan(run[:], cut[:, par, 0:P], turned_score, -BIG, ALU.add,
                                       ALU.max).then_inc(lap_d, 1)
                dve.tensor_tensor_scan(run_b[:, ::-1], cut[:, par, P:0:-1], turned_score[:, ::-1], -BIG, ALU.add,
                                       ALU.max).then_inc(lap_d, 1)

            def spread_own(i, par):
                dve.wait_ge(lap_d, LAP_STEPS * (2 * i + par) + 2)
                dve.tensor_scalar(spread[:, 0:LAP], e.slot_sel[:], run[:, P - 1:P], None,
                                  ALU.mult).then_inc(lap_d, 1)
                dve.tensor_scalar(spread[:, LAP:2 * LAP], e.slot_sel[:], run_b[:, 0:1], None,
                                  ALU.mult).then_inc(spread_made, 1)

            def candidates(i, par):
                lap = 2 * i + par
                dve.wait_ge(ends_spread, lap + 1)
                dve.tensor_tensor(cand[:], e.apart[:, bass.ds(lap, 1)].rearrange("p l a b -> p (l a) b"),
                                  all_ends.unsqueeze(1).to_broadcast([P, 2, ENDS]), ALU.add).then_inc(lap_d, 1)

            def ends_max(i, par):
                dve.wait_ge(lap_d, LAP_STEPS * (2 * i + par) + 4)
                dve.tensor_reduce(end_max[:], cand[:], AX.X, ALU.max).then_inc(lap_d, 1)

            def maxima(i, par):
                lap = 2 * i + par
                dve.wait_ge(lap_d, LAP_STEPS * lap + 5)
                dve.tensor_tensor_scan(run[:], cut[:, par, 0:P], turned_score, end_max[:, 0:1], ALU.add,
                                       ALU.max).then_inc(lap_d, 1)
                dve.scalar_tensor_tensor(drop[:, 0:1], all_ends[:, ENDS - 1:ENDS], end_max[:, 0:1],
                                         e.goes_on[:, bass.ds(lap, 1)], ALU.subtract, ALU.mult).then_inc(dropped, 1)
                dve.wait_ge(lap_d, LAP_STEPS * lap + 6)
                dve.tensor_tensor_scan(top_m[:, ::-1], cut[:, par, P:0:-1], run[:, ::-1], end_max[:, 1:2], ALU.add,
                                       ALU.max).then_inc(m_made, 1)

            def keep_last(i, par):
                dve.wait_ge(m_made, 2 * i + par + 1)
                dve.tensor_tensor(spread[:, ENDS - 1:ENDS], top_m[:, P - 1:P], e.slot_sel[:, LAP - 1:LAP],
                                  ALU.mult).then_inc(rescale_d, 1)

            def take_maxima(i, par):
                lap = 2 * i + par
                dve.wait_ge(m_turned, lap + 1)
                dve.tensor_tensor(below[:].rearrange("p h s -> p (h s)"),
                                  score[:, par].rearrange("p h s -> p (h s)"),
                                  turned_m, ALU.subtract).then_inc(below_made, 1)
                dve.tensor_scalar(node_hot[:], e.iota_f[:], e.first_loc[:, bass.ds(lap, 1)], None,
                                  ALU.is_equal).then_inc(rescale_d, 1)
                dve.wait_ge(drop_exp, lap + 1)
                own = e.ident_f[:, 0:P:LAP]
                dve.scalar_tensor_tensor(head_drop[:], own, drop[:, 1:2], own, ALU.mult,
                                         ALU.subtract).then_inc(drop_rows_made, 1)

            RESCALE_STEPS = 5

            def take_rescale(i, par):
                dve.wait_ge(node_dropped, 2 * i + par + 1)
                dve.tensor_scalar(rescale[:], node_drop, 1.0, None, ALU.add).then_inc(rescale_d, 1)

            def bring_down(i, par):
                lap = 2 * i + par
                dve.reg_load(lap_reg, e.win_at[0:1, bass.ds(lap * LAP, 1)])
                win = dve.snap(lap_reg, min_val=0, max_val=WINS_PAD - 1)
                dve.wait_ge(rescale_d, RESCALE_STEPS * lap + 3)
                wait(dve, added, LAP * lap)
                sums = e.acc[:, bass.ds(win * AW, F)].rearrange("p (h d) -> p h d", d=DH)
                dve.tensor_tensor(sums, sums, rescale[:].unsqueeze(2).to_broadcast([P, HEADS, DH]),
                                  ALU.mult).then_inc(rescale_d, 1)
                exps = e.acc[:, bass.ds(win * AW + F, HEADS)]
                dve.tensor_tensor(exps, exps, rescale[:], ALU.mult).then_inc(rescale_d, 1)

            def turn(i, par, left):
                nxt = following(i, par, 1)
                last = RING - 1
                for g in range(RING):
                    far = g > 0 and RING * (left + 1) - 1 - g >= RING + 1
                    if g > 0:
                        if left:
                            score_group(*nxt, g)
                        add_slot(i, par, g - 1, 0)
                    if far:
                        multiply_half(*ahead(i, par, g, RING + 1), 0)
                    if g == 0:
                        take_rescale(i, par)
                    else:
                        if left and g == last:
                            own_ends(*nxt)
                        add_slot(i, par, g - 1, 1)
                    if far:
                        multiply_half(*ahead(i, par, g, RING + 1), 1)
                    if g == 0:
                        bring_down(i, par)
                    else:
                        if left and g == last:
                            spread_own(*nxt)
                        add_slot(i, par, g - 1, 2)
                    weigh_group(i, par, g)
                    if g == 0:
                        dve.wait_ge(rescale_d, RESCALE_STEPS * (2 * i + par) + 5)
                    else:
                        add_slot(i, par, g - 1, 3)
                if left:
                    candidates(*nxt)
                add_slot(i, par, last, 0)
                if left:
                    ends_max(*nxt)
                add_slot(i, par, last, 1)
                if left:
                    maxima(*nxt)
                if left > 1:
                    score_group(*following(i, par, 2), 0)
                    multiply_half(*following(i, par, 2), 1, 0)
                if left:
                    keep_last(*nxt)
                add_slot(i, par, last, 2)
                if left:
                    take_maxima(*nxt)
                if left > 1:
                    multiply_half(*following(i, par, 2), 1, 1)
                add_slot(i, par, last, 3)

            dve.memset(e.acc[:], 0.0).then_inc(cleared, 1)
            dve.memset(kv[:, :, :, :, RW - 1:RW], 1.0).then_inc(cleared, 1)
            dve.memset(spread[:], 0.0).then_inc(cleared, 1)
            dve.wait_ge(cleared, 3)
            for g in range(RING):
                multiply_half(0, 0, g, 0)
                multiply_half(0, 0, g, 1)
                score_group(0, 0, g)
            own_ends(0, 0)
            multiply_half(0, 1, 0, 0)
            spread_own(0, 0)
            multiply_half(0, 1, 0, 1)
            candidates(0, 0)
            ends_max(0, 0)
            maxima(0, 0)
            score_group(0, 1, 0)
            multiply_half(0, 1, 1, 0)
            keep_last(0, 0)
            take_maxima(0, 0)
            multiply_half(0, 1, 1, 1)
            edge_laps(dve, turn)

        @block.tensor
        def _(pe):
            regs = [pe.alloc_register(f"pick_win{j}") for j in range(GS)]

            def turn_hot(i, par, g):
                n = group_no(i, par, g)
                pe.wait_ge(hot_s_made, n + 1)
                wait(pe, hot_t_copied, n)
                for j in range(GS):
                    mm = pe.transpose(ps_hot[:, g % 2, j, :], hot_s[:, g % 2, j, :], e.ident_b[:])
                mm.then_inc(hot_turned, 1)

            def pick_half(i, par, g, half):
                n = group_no(i, par, g)
                if half == 0:
                    pe.reg_load(regs, e.win_at[0:1, bass.ds(n * GS, GS)])
                    pe.wait_ge(hot_t_copied, n + 1)
                wait(pe, multiplied, 2 * n + half - 1)
                for j in range(2 * half, 2 * half + 2):
                    win = pe.snap(regs[j], min_val=0, max_val=WINS_PAD - 1)
                    mm = pe.matmul(ps_q[:, half, j % 2, :], hot_t[:, g % 2, j, :],
                                   e.q_all[:, bass.ds(win * F, F)], start=True, stop=True)
                mm.then_inc(q_picked, 1)

            def sum_group(i, par, g):
                n = group_no(i, par, g)
                pe.wait_ge(hot_m_made, n + 1)
                pe.wait_ge(weighed, n + 1)
                for j in range(GS):
                    wait(pe, added, GS * (n - 1) + j + 1)
                    pe.matmul(ps_sum[:, j, 0:AW], hot_m[:, g % 2, j, :], kv[:, par, g, j, F:RW],
                              start=True, stop=True).then_inc(summed, 1)

            def turn_score(i, par):
                lap = 2 * i + par
                pe.wait_ge(scored, RING * (lap + 1))
                wait(pe, below_made, lap)
                pe.transpose(turned_score, score[:, par].rearrange("p h s -> p (h s)"), e.ident_f[:]).then_inc(score_turned, 1)

            def spread_ends(i, par):
                pe.wait_ge(spread_made, 2 * i + par + 1)
                pe.matmul(all_ends, e.head_eq[:], spread[:], start=True, stop=True).then_inc(ends_spread, 1)

            def turn_m(i, par):
                lap = 2 * i + par
                pe.wait_ge(m_made, lap + 1)
                pe.transpose(turned_m, top_m[:], e.ident_f[:]).then_inc(m_turned, 1)

            def drop_nodes(i, par):
                pe.wait_ge(drop_rows_made, 2 * i + par + 1)
                pe.matmul(node_drop, node_hot[:], head_drop[:], start=True, stop=True).then_inc(node_dropped, 1)

            def turn(i, par, left):
                nxt = following(i, par, 1)
                for g in range(RING):
                    after = RING * (left + 1) - 1 - g
                    if left and g == RING - 1:
                        turn_score(*nxt)
                    if g > 0 and after >= 6:
                        pick_half(*ahead(i, par, g, 6), 0)
                    if left and g == RING - 1:
                        spread_ends(*nxt)
                    if g > 0 and after >= 6:
                        pick_half(*ahead(i, par, g, 6), 1)
                    if after >= 7:
                        turn_hot(*ahead(i, par, g, 7))
                    sum_group(i, par, g)
                if left:
                    turn_m(*nxt)
                if left > 1:
                    pick_half(*following(i, par, 2), 2, 0)
                if left:
                    drop_nodes(*nxt)
                if left > 1:
                    pick_half(*following(i, par, 2), 2, 1)

            pe.wait_ge(cleared, 3)
            turn_hot(0, 0, 0)
            for n in range(6):
                if n == RING + 1:
                    turn_score(0, 0)
                    spread_ends(0, 0)
                for half in range(2):
                    pick_half(*ahead(0, 0, n, 0), half)
                turn_hot(*ahead(0, 0, n, 1))
            turn_m(0, 0)
            pick_half(0, 1, 2, 0)
            drop_nodes(0, 0)
            pick_half(0, 1, 2, 1)
            edge_laps(pe, turn)


def edge_mean(nc, e):
    with ExitStack() as ctx:
        r_buf = e.sb("r_buf", [P, RING, GS, F], F32, ctx)
        hot = e.sb("hot", [P, 2, GS, P], F32, ctx)
        ps_sum = e.ps("ps_mean", [P, 2, GS, 512], F32, ctx)
        staged = e.sem("r_staged")
        rows_in = [e.sem(f"r_rows_in{g}") for g in range(RING)]
        pool_turns = e.sem("r_pool_turns")
        act_turns = e.sem("r_act_turns")
        cleared = e.sem("r_cleared")
        far = e.sem("r_far")
        hot_made = e.sem("r_hot_made")
        summed = e.sem("r_summed")
        added = e.sem("r_added")
        block = ctx.enter_context(nc.Block())

        @block.gpsimd
        def _(pool):
            def lap(i, last):
                for g in range(RING):
                    n = i * RING + g
                    pool.wait_ge(staged, n + 1)
                    wait(pool, summed, GS * (n - RING + 1))
                    pool.sem_inc(pool_turns, 1)
                    for j in range(GS):
                        pool.indirect_dma_start(out=r_buf[:, g, j, :], out_offset=None, in_=e.x1_rows[:, :],
                                                in_offset=bass.IndirectOffsetOnAxis(ap=e.stage[:, 0, g, j:j + 1],
                                                                                    axis=0)
                                                ).then_inc(rows_in[g], 16)

            laps(pool, lap, LAPS)

        @block.scalar
        def _(act):
            def stage_group(i, g):
                act.activation(e.stage[:, 0, g, :], e.src_idx[:, bass.ds(i * LAP + g * GS, GS)],
                               ACT.Copy).then_inc(staged, 1)

            def lap(i, last):
                for g in range(RING):
                    n = i * RING + g
                    wait(act, summed, GS * (n - 1))
                    act.sem_inc(act_turns, 1)
                    for j in range(GS):
                        ins = act.activation(hot[:, g % 2, j, :], e.iota_f[:], ACT.Abs,
                                             bias=e.neg_loc[:, bass.ds(n * GS + j, 1)])
                    ins.then_inc(far, 1)
                    act.wait_ge(far, n + 1)
                    act.activation(hot[:, g % 2], hot[:, g % 2], ACT.Relu, bias=1.0, scale=-1.0).then_inc(hot_made, 1)
                    if g == 0:
                        wait(act, rows_in[RING - 1], 16 * GS * i)
                        act.sem_inc(act_turns, 1)
                        stage_group(i, RING - 1)
                    elif not last:
                        act.wait_ge(rows_in[g - 1], 16 * GS * (i + 1))
                        act.sem_inc(act_turns, 1)
                        stage_group(i + 1, g - 1)

            for g in range(RING - 1):
                stage_group(0, g)
            laps(act, lap, LAPS)

        @block.vector
        def _(dve):
            regs = [dve.alloc_register(f"mean_win{j}") for j in range(GS)]

            def lap(i, last):
                for g in range(RING):
                    n = i * RING + g
                    dve.reg_load(regs, e.win_at[0:1, bass.ds(n * GS, GS)])
                    for j in range(GS):
                        win = dve.snap(regs[j], min_val=0, max_val=WINS_PAD - 1)
                        dve.wait_ge(summed, GS * n + j + 1)
                        wait(dve, added, GS * n + j)
                        dst = e.acc[:, bass.ds(win * AW, F)]
                        dve.tensor_tensor(dst, dst, ps_sum[:, g % 2, j, 0:F], ALU.add).then_inc(added, 1)

            dve.memset(e.acc[:], 0.0).then_inc(cleared, 1)
            dve.wait_ge(cleared, 1)
            laps(dve, lap, LAPS)

        @block.tensor
        def _(pe):
            def lap(i, last):
                for g in range(RING):
                    n = i * RING + g
                    pe.wait_ge(rows_in[g], 16 * GS * (i + 1))
                    pe.wait_ge(hot_made, n + 1)
                    wait(pe, added, GS * (n - 1))
                    for j in range(GS):
                        pe.matmul(ps_sum[:, g % 2, j, 0:F], hot[:, g % 2, j, :], r_buf[:, g, j, :],
                                  start=True, stop=True).then_inc(summed, 1)

            laps(pe, lap, LAPS)


PAIRS = -(-WINS // 2)
NLAPS = (PAIRS - 1) // 2
assert 2 * NLAPS == PAIRS - 1 and WINS % 2 == 1


def pair_laps(eng, body):
    body(0, 0, 2, 2, 2)
    body(1, 1, 2, 2, 2)
    with eng.Fori(1, NLAPS - 1) as i:
        body(2 * i, 0, 2, 2, 2)
        body(2 * i + 1, 1, 2, 2, 2)
    body(PAIRS - 3, 0, 2, 2, 1)
    body(PAIRS - 2, 1, 2, 1, 0)
    body(PAIRS - 1, 0, 1, 0, 0)


LN_STEPS = 7


def layer_norm(dve, step, dst, src, mv, stats, nw, settled, var_ready, std_ready, count):
    for w in range(nw):
        step(dve.bn_stats(stats[:, w, :], src[:, w, :]), w == nw - 1)
    dve.sem_inc(settled, 1)
    for w in range(nw):
        step(dve.bn_aggr(mv[:, w, 0:2], stats[:, w, :]), w == nw - 1)
    dve.sem_inc(var_ready, 1)
    dve.wait_ge(std_ready, count)
    step(dve.reciprocal(mv[:, 0:nw, 3:4], mv[:, 0:nw, 2:3]))
    for w in range(nw):
        step(dve.tensor_scalar(dst[:, w, :], src[:, w, :], mv[:, w, 0:1], mv[:, w, 3:4],
                               ALU.subtract, ALU.mult), w == nw - 1)


def root(act, mv, nw, eps_col, var_ready, std_ready, count):
    act.wait_ge(var_ready, count)
    act.activation(mv[:, 0:nw, 2:3], mv[:, 0:nw, 1:2], ACT.Sqrt, bias=eps_col).then_inc(std_ready, 1)


def node_ffn(nc, e):
    with ExitStack() as ctx:
        w1_sb = e.sb("w1_sb", [P, FC, HID], F32, ctx)
        w2_sb = e.sb("w2_sb", [P, HC, F], F32, ctx)
        cols = e.sb("cols", [P, 3, HC], F32, ctx)
        neg = e.sb("neg", [P, 2, HC], F32, ctx)
        rows = e.sb("rows", [P, 3, F], F32, ctx)
        x_in = e.sb("x_in", [P, 2, 2, F], F32, ctx)
        rst = e.sb("rst", [P, 2, 2, F], F32, ctx)
        rst_t = e.sb("rst_t", [P, 2, FC, 2 * P], F32, ctx)
        relu_p = e.sb("relu_p", [P, HC, 2 * P], F32, ctx)
        relu_n = e.sb("relu_n", [P, HC, 2 * P], F32, ctx)
        hid = e.sb("hid", [P, HC, 2 * P], F32, ctx)
        zr = e.sb("zr", [P, 2, HEADS], F32, ctx)
        t0 = e.sb("t0", [P, 2, F], F32, ctx)
        mv = e.sb("mv", [P, 2, 4], F32, ctx)
        stats = e.sb("stats", [P, 2, 6], F32, ctx)
        ps_tr = e.ps("ps_tr", [P, FC, 2 * P], F32, ctx)
        ps_h = e.ps("ps_h", [P, 4, 512], F32, ctx)
        ps_f = e.ps("ps_f", [P, 2, 512], F32, ctx)
        par_in = e.sem("par_in")
        x_ld = [e.sem("x_ld0"), e.sem("x_ld1")]
        vec_d = e.sem("vec_d")
        rst_made = e.sem("rst_made")
        rst_turned = e.sem("rst_turned")
        rst_copied = e.sem("rst_copied")
        hid_mm = e.sem("hid_mm")
        relu_d = e.sem("relu_d")
        hid_made = e.sem("hid_made")
        ffn_mm = e.sem("ffn_mm")
        ffn_read = e.sem("ffn_read")
        x1_made = e.sem("x1_made")
        x1_out = e.sem("x1_out")
        neg_made = e.sem("neg_made")
        var_ready = e.sem("var_ready")
        settled = e.sem("settled")
        std_ready = e.sem("std_ready")
        block = ctx.enter_context(nc.Block())
        x_v = e.x.rearrange("(w p) f -> p w f", p=P)
        x1_v = e.x1_rows.rearrange("(w p) f -> p w f", p=P)
        x1_s = e.x1_all[:].rearrange("p (w f) -> p w f", f=F)

        @block.sync
        def _(sp):
            sp.dma_start(w1_sb[:], e.w1.rearrange("(c p) n -> p c n", p=P)).then_inc(par_in, 16)
            sp.dma_start(w2_sb[:], e.w2.rearrange("(c p) n -> p c n", p=P)).then_inc(par_in, 16)
            for k, col in enumerate((e.b1, e.alpha)):
                sp.dma_start(cols[:, k, :], col).then_inc(par_in, 16)
            for k, row in enumerate((e.ln_g, e.ln_b, e.b2)):
                sp.dma_start(rows[:, k, :], row.to_broadcast([P, F])).then_inc(par_in, 16)

            def body(n, par, nw, nxt, nxt2):
                wait(sp, x1_made, n - 1)
                sp.dma_start(x_in[:, par, 0:nw, :], x_v[:, bass.ds(2 * n, nw), :]).then_inc(x_ld[par], 16)

            pair_laps(sp, body)

        @block.gpsimd
        def _(pool):
            def body(n, par, nw, nxt, nxt2):
                pool.wait_ge(x1_made, n + 1)
                pool.dma_start(x1_v[:, bass.ds(2 * n, nw), :], x1_s[:, bass.ds(2 * n, nw), :]).then_inc(x1_out, 16)

            pair_laps(pool, body)
            pool.wait_ge(x1_out, 16 * PAIRS)

        @block.vector
        def _(dve):
            done = [0]

            def pre(n, par, nw, step):
                root_no = 3 * n - 1 if not isinstance(n, int) or n > 0 else 1
                a = e.acc[:, bass.ds(2 * n * AW, nw * AW)].rearrange("p (w a) -> p w a", a=AW)
                h = t0[:, 0:nw]
                step(dve.tensor_scalar(zr[:, 0:nw], a[:, :, F:F + HEADS], 0.5, None, ALU.max))
                step(dve.reciprocal(zr[:, 0:nw], zr[:, 0:nw]))
                step(dve.tensor_tensor(h.rearrange("p w (h d) -> p w h d", d=DH),
                                       a[:, :, 0:F].rearrange("p w (h d) -> p w h d", d=DH),
                                       zr[:, 0:nw].unsqueeze(3).to_broadcast([P, nw, HEADS, DH]), ALU.mult))
                dve.wait_ge(x_ld[par], 8 * (n - par) + 16)
                step(dve.tensor_tensor(h, h, x_in[:, par, 0:nw], ALU.add))
                layer_norm(dve, step, h, h, mv, stats, nw, settled, var_ready, std_ready, root_no)
                step(dve.tensor_tensor(h, h, rows[:, 0:1, :].to_broadcast([P, nw, F]), ALU.mult))
                step(dve.tensor_tensor(rst[:, par, 0:nw], h, rows[:, 1:2, :].to_broadcast([P, nw, F]), ALU.add))
                dve.sem_inc(rst_made, 1)

            def prelu(n, nw):
                wait(dve, ffn_mm, n)
                for hc in range(HC):
                    dve.wait_ge(relu_d, HC * n + hc + 1)
                    dve.scalar_tensor_tensor(hid[:, hc, 0:nw * P], relu_n[:, hc, 0:nw * P], neg[:, 1, hc:hc + 1],
                                             relu_p[:, hc, 0:nw * P], ALU.mult, ALU.add).then_inc(hid_made, 1)

            def post(n, par, nw, step):
                y = t0[:, 0:nw]
                dve.wait_ge(ffn_mm, n + 1)
                dve.tensor_tensor(y, ps_f[:, 0:nw, 0:F], rows[:, 2:3, :].to_broadcast([P, nw, F]),
                                  ALU.add).then_inc(ffn_read, 1)
                dve.wait_ge(ffn_read, n + 1)
                step(dve.tensor_tensor(y, y, rst[:, par, 0:nw], ALU.add))
                first = 3 * n + 3 if nw == 2 else 3 * n + 2
                layer_norm(dve, step, y, y, mv, stats, nw, settled, var_ready, std_ready, first)
                step(dve.tensor_tensor(y, y, rows[:, 0:1, :].to_broadcast([P, nw, F]), ALU.mult))
                step(dve.tensor_tensor(y, y, rows[:, 1:2, :].to_broadcast([P, nw, F]), ALU.add))
                step(dve.tensor_tensor(y, y, x_in[:, par, 0:nw], ALU.add))
                layer_norm(dve, step, x1_s[:, bass.ds(2 * n, nw), :], y, mv, stats, nw,
                           settled, var_ready, std_ready, first + 1)
                dve.sem_inc(x1_made, 1)

            def counted(base):
                k = [0]

                def step(ins, last=True):
                    k[0] += 1
                    ins.then_inc(vec_d, 1)
                    if last:
                        dve.wait_ge(vec_d, base + k[0])
                return step

            PRE = 6 + LN_STEPS
            POST = 4 + 2 * LN_STEPS

            FEWER = 3

            def body(n, par, nw, nxt, nxt2):
                if not isinstance(n, int) or n > 0:
                    post(n - 1, 1 - par, 2, counted(1 + (n + 1) * PRE + (n - 1) * POST - (0 if nxt else FEWER)))
                prelu(n, nw)
                if nxt:
                    pre(n + 1, 1 - par, nxt, counted(1 + (n + 1) * PRE + n * POST))

            dve.wait_ge(par_in, 16 * 7)
            dve.tensor_scalar(neg[:], cols[:, 0:2, :], -1.0, None, ALU.mult).then_inc(neg_made, 1)
            a = e.acc[:].rearrange("p (w a) -> p w a", a=AW)
            dve.tensor_scalar(e.cnt_rec[:].unsqueeze(2), a[:, 0:WINS, AW - 1:AW], 1.0, None, ALU.max).then_inc(vec_d, 1)
            dve.wait_ge(vec_d, 1)
            dve.reciprocal(e.cnt_rec[:], e.cnt_rec[:]).then_inc(neg_made, 1)
            dve.wait_ge(neg_made, 2)
            pre(0, 0, 2, counted(1))
            pair_laps(dve, body)
            post(PAIRS - 1, 0, 1, counted(1 + PAIRS * PRE - FEWER + (PAIRS - 1) * POST))

        @block.scalar
        def _(act):
            act.wait_ge(neg_made, 1)
            act.wait_ge(par_in, 16 * 7)

            def relus(n, nw, chunks):
                for hc in chunks:
                    act.wait_ge(hid_mm, HC * n + hc + 1)
                    if hc == 0:
                        wait(act, hid_made, HC * n)
                    act.activation(relu_p[:, hc, 0:nw * P], ps_h[:, hc % 4, 0:nw * P], ACT.Relu,
                                   bias=cols[:, 0, hc:hc + 1])
                    act.activation(relu_n[:, hc, 0:nw * P], ps_h[:, hc % 4, 0:nw * P], ACT.Relu,
                                   bias=neg[:, 0, hc:hc + 1], scale=-1.0).then_inc(relu_d, 1)

            def copy_turned(n, par, nw):
                act.wait_ge(rst_turned, n + 1)
                act.activation(rst_t[:, par, :, 0:nw * P], ps_tr[:, :, 0:nw * P], ACT.Copy).then_inc(rst_copied, 1)

            def take_root(nw, count):
                root(act, mv, nw, e.eps_col[:], var_ready, std_ready, count)

            def body(n, par, nw, nxt, nxt2):
                later = not isinstance(n, int) or n > 0
                relus(n, nw, range(0, 3))
                if later:
                    take_root(2, 3 * n)
                relus(n, nw, range(3, 6))
                if later:
                    take_root(2, 3 * n + 1)
                relus(n, nw, range(6, HC))
                if nxt:
                    take_root(nxt, 3 * n + 2)
                    copy_turned(n + 1, 1 - par, nxt)

            take_root(2, 1)
            copy_turned(0, 0, 2)
            pair_laps(act, body)
            take_root(1, 3 * PAIRS - 1)
            take_root(1, 3 * PAIRS)

        @block.tensor
        def _(pe):
            pe.wait_ge(par_in, 16 * 7)

            def turn(n, par, nw):
                pe.wait_ge(rst_made, n + 1)
                for w in range(nw):
                    for c in range(FC):
                        mm = pe.transpose(ps_tr[:, c, w * P:(w + 1) * P], rst[:, par, w, c * P:(c + 1) * P],
                                          e.ident_f[:])
                mm.then_inc(rst_turned, 1)

            def body(n, par, nw, nxt, nxt2):
                pe.wait_ge(rst_copied, n + 1)
                for hc in range(HC):
                    wait(pe, relu_d, HC * n + hc - 3)
                    for c in range(FC):
                        mm = pe.matmul(ps_h[:, hc % 4, 0:nw * P], w1_sb[:, c, hc * P:(hc + 1) * P],
                                       rst_t[:, par, c, 0:nw * P], start=(c == 0), stop=(c == FC - 1))
                    mm.then_inc(hid_mm, 1)
                wait(pe, ffn_read, n)
                for hc in range(HC):
                    pe.wait_ge(hid_made, HC * n + hc + 1)
                    for w in range(nw):
                        mm = pe.matmul(ps_f[:, w, 0:F], hid[:, hc, w * P:(w + 1) * P], w2_sb[:, hc, :],
                                       start=(hc == 0), stop=(hc == HC - 1))
                mm.then_inc(ffn_mm, 1)
                if nxt:
                    turn(n + 1, 1 - par, nxt)

            turn(0, 0, 2)
            pair_laps(pe, body)


def node_out(nc, e):
    with ExitStack() as ctx:
        wt_sb = e.sb("wt_sb", [P, FC, F], F32, ctx)
        bl_row = e.sb("bl_row", [P, 1, F], F32, ctx)
        mean = e.sb("mean", [P, 2, 2, F], F32, ctx)
        mean_t = e.sb("mean_t", [P, 2, FC, 2 * P], F32, ctx)
        y = e.sb("y", [P, 2, F], F32, ctx)
        res = e.sb("res", [P, 2, 2, F], F32, ctx)
        mv = e.sb("mv_o", [P, 2, 4], F32, ctx)
        stats = e.sb("stats_o", [P, 2, 6], F32, ctx)
        ps_tr = e.ps("ps_tro", [P, 2, FC, 2 * P], F32, ctx)
        ps_y = e.ps("ps_y", [P, 2, 2, 512], F32, ctx)
        par_in = e.sem("o_par_in")
        vec_d = e.sem("o_vec_d")
        mean_made = e.sem("mean_made")
        mean_turned = e.sem("mean_turned")
        mean_copied = e.sem("mean_copied")
        y_mm = e.sem("y_mm")
        y_read = e.sem("y_read")
        var_ready = e.sem("o_var_ready")
        settled = e.sem("o_settled")
        std_ready = e.sem("o_std_ready")
        res_made = e.sem("res_made")
        res_out = [e.sem("res_out0"), e.sem("res_out1")]
        block = ctx.enter_context(nc.Block())
        x1_s = e.x1_all[:].rearrange("p (w f) -> p w f", f=F)
        full = (WINS - 1) * P
        out_v = e.out[0:full, :].rearrange("(w p) f -> p w f", p=P)

        @block.sync
        def _(sp):
            sp.dma_start(wt_sb[:], e.wT.rearrange("(c p) n -> p c n", p=P)).then_inc(par_in, 16)
            sp.dma_start(bl_row[:, 0, :], e.bl.to_broadcast([P, F])).then_inc(par_in, 16)

            def body(n, par, nw, nxt, nxt2):
                sp.wait_ge(res_made, n + 1)
                if nw == 2:
                    sp.dma_start(out_v[:, bass.ds(2 * n, 2), :], res[:, par]).then_inc(res_out[par], 16)
                else:
                    rest = N_NODES - full
                    sp.dma_start(e.out[full:N_NODES, :], res[0:rest, par, 0, :]).then_inc(res_out[par], 16)

            pair_laps(sp, body)
            sp.wait_ge(res_out[0], 16 * (NLAPS + 1))
            sp.wait_ge(res_out[1], 16 * NLAPS)

        @block.vector
        def _(dve):
            STEPS = 1 + LN_STEPS

            def take_mean(n, par, nw):
                wait(dve, mean_turned, n - 1)
                for w in range(nw):
                    ins = dve.tensor_scalar(mean[:, par, w, :], e.acc[:, bass.ds((2 * n + w) * AW, F)],
                                            e.cnt_rec[:, bass.ds(2 * n + w, 1)], None, ALU.mult)
                ins.then_inc(mean_made, 1)

            def body(n, par, nw, nxt, nxt2):
                k = [0]

                def step(ins, last=True):
                    k[0] += 1
                    ins.then_inc(vec_d, 1)
                    if last:
                        dve.wait_ge(vec_d, n * STEPS + k[0])

                if nxt2:
                    take_mean(n + 2, par, nxt2)
                dve.wait_ge(y_mm, n + 1)
                dve.tensor_tensor(y[:, 0:nw], ps_y[:, par, 0:nw, 0:F], bl_row[:].to_broadcast([P, nw, F]),
                                  ALU.add).then_inc(y_read, 1)
                dve.wait_ge(y_read, n + 1)
                step(dve.scalar_tensor_tensor(y[:, 0:nw], y[:, 0:nw], 0.0, x1_s[:, bass.ds(2 * n, nw), :],
                                              ALU.max, ALU.add))
                wait(dve, res_out[par], 8 * (n - par))
                layer_norm(dve, step, res[:, par], y, mv, stats, nw, settled, var_ready, std_ready, n + 1)
                dve.sem_inc(res_made, 1)

            dve.wait_ge(par_in, 32)
            take_mean(0, 0, 2)
            take_mean(1, 1, 2)
            pair_laps(dve, body)

        @block.scalar
        def _(act):
            def copy_turned(n, par, nw):
                act.wait_ge(mean_turned, n + 1)
                wait(act, y_mm, n - 1)
                act.activation(mean_t[:, par, :, 0:nw * P], ps_tr[:, par, :, 0:nw * P],
                               ACT.Copy).then_inc(mean_copied, 1)

            def body(n, par, nw, nxt, nxt2):
                if nxt:
                    copy_turned(n + 1, 1 - par, nxt)
                root(act, mv, nw, e.eps_col[:], var_ready, std_ready, n + 1)

            copy_turned(0, 0, 2)
            pair_laps(act, body)

        @block.tensor
        def _(pe):
            pe.wait_ge(par_in, 32)

            def turn(n, par, nw):
                pe.wait_ge(mean_made, n + 1)
                wait(pe, mean_copied, n - 1)
                for w in range(nw):
                    for c in range(FC):
                        mm = pe.transpose(ps_tr[:, par, c, w * P:(w + 1) * P], mean[:, par, w, c * P:(c + 1) * P],
                                          e.ident_f[:])
                mm.then_inc(mean_turned, 1)

            def body(n, par, nw, nxt, nxt2):
                if nxt:
                    turn(n + 1, 1 - par, nxt)
                pe.wait_ge(mean_copied, n + 1)
                wait(pe, y_read, n - 1)
                for w in range(nw):
                    for c in range(FC):
                        mm = pe.matmul(ps_y[:, par, w, 0:F], mean_t[:, par, c, w * P:(w + 1) * P], wt_sb[:, c, :],
                                       start=(c == 0), stop=(c == FC - 1))
                mm.then_inc(y_mm, 1)

            turn(0, 0, 2)
            pair_laps(pe, body)


_INS = ["x", "xT", "edges", "wqkv", "ln_g", "ln_b", "w1", "b1", "alpha", "w2", "b2", "wT", "bl"]


def kernel(**inputs):
    import numpy as _np
    import concourse.bacc as _bacc
    from concourse.bass_utils import run_bass_kernel_spmd as _run

    g = {k: _np.asarray(v) for k, v in inputs.items()}
    x = _np.zeros((NODES_PAD, F), _np.float32)
    x[:N_NODES] = g["x"]
    edges = _np.zeros((TILES_PAD, 2, P), _np.int32)
    edges[:, 1] = NO_NODE
    pad = TILES_PAD * P - N_EDGES
    edges[:, 0] = _np.concatenate([g["src"], _np.zeros(pad, _np.int32)]).reshape(TILES_PAD, P)
    edges[:, 1] = _np.concatenate([g["dst"], _np.full(pad, NO_NODE, _np.int32)]).reshape(TILES_PAD, P)
    arrays = {
        "x": x,
        "xT": x.T,
        "edges": edges.reshape(TILES_PAD, 2 * P),
        "wqkv": _np.concatenate([g["L0_gnn_Wk"], g["L0_gnn_Wv"], g["L0_gnn_Wq"]], axis=1),
        "ln_g": g["L0_gnn_ln_g"].reshape(1, F),
        "ln_b": g["L0_gnn_ln_b"].reshape(1, F),
        "w1": g["L0_gnn_W1"],
        "b1": g["L0_gnn_b1"].reshape(HC, P).T,
        "alpha": g["L0_gnn_prelu_alpha"].reshape(HC, P).T,
        "w2": g["L0_gnn_W2"],
        "b2": g["L0_gnn_b2"].reshape(1, F),
        "wT": g["L1_gnn_W"].T,
        "bl": g["L1_gnn_b"].reshape(1, F),
    }
    arrays = {f"in_{k}": _np.ascontiguousarray(a) for k, a in arrays.items()}
    nc = _bacc.Bacc("TRN2", target_bir_lowering=False, num_devices=1)
    args = [nc.dram_tensor(f"in_{k}", arrays[f"in_{k}"].shape, mybir.dt.from_np(arrays[f"in_{k}"].dtype),
                           kind="ExternalInput").ap() for k in _INS]
    args.append(nc.dram_tensor("out_0", (N_NODES, F), F32, kind="ExternalOutput").ap())
    build(nc, *args)
    r = _run(nc, [arrays], core_ids=[0])
    return r.results[0]["out_0"]
```

```python
from contextlib import ExitStack

import concourse.bass as bass
from concourse import mybir

ALU = mybir.AluOpType
ACT = mybir.ActivationFunctionType
AX = mybir.AxisListType
F32 = mybir.dt.float32
BF16 = mybir.dt.bfloat16
I32 = mybir.dt.int32

P = 128
N_NODES, F, HEADS = 6250, 256, 8
DH = F // HEADS
N_EDGES = 100000
HID = 4 * F
HC = HID // P
FC = F // P
BIG = 1.0e30
EPS = 1e-5

WINS = -(-N_NODES // P)
WINS_PAD = WINS + 1
NODES_PAD = WINS_PAD * P
NO_NODE = WINS * P

TILES = -(-N_EDGES // P)
TROWS = 112
TPR = -(-TILES // TROWS)
TILES_PAD = TROWS * TPR
GS = 4
RING = 4
LAP = GS * RING
assert LAP * HEADS == P
SLOTS = -(-(TILES + WINS - 1) // (2 * LAP)) * 2 * LAP
SLOTS_TAB = -(-SLOTS // P) * P
SC = SLOTS_TAB // P
LAPS = SLOTS // LAP
AW = F + HEADS + 1
RW = F + AW
ENDS = 2 * LAP + 1

assert SC <= 8 and SLOTS % (2 * LAP) == 0 and SLOTS_TAB >= SLOTS + LAP and TILES_PAD >= TILES


def wait(eng, sem, value):
    if not isinstance(value, int) or value > 0:
        eng.wait_ge(sem, value)


def laps(eng, body, count):
    body(0, False)
    with eng.Fori(1, count - 1) as i:
        body(i, False)
    body(count - 1, True)


class Shared:

    def __init__(self, nc, life):
        self.nc, self.life = nc, life

    def sb(self, name, shape, dt, life):
        return life.enter_context(self.nc.sbuf_tensor(name, shape, dt))

    def ps(self, name, shape, dt, life):
        return life.enter_context(self.nc.psum_tensor(name, shape, dt))

    def sem(self, name):
        return self.life.enter_context(self.nc.semaphore(name))


def build(nc, x, xT, edges, wqkv, ln_g, ln_b, w1, b1, alpha, w2, b2, wT, bl, out):
    with ExitStack() as top:
        e = Shared(nc, top)
        e.x, e.xT, e.edges, e.wqkv, e.ln_g, e.ln_b = x, xT, edges, wqkv, ln_g, ln_b
        e.w1, e.b1, e.alpha, e.w2, e.b2, e.wT, e.bl, e.out = w1, b1, alpha, w2, b2, wT, bl, out
        e.kv_rows = nc.dram_tensor("kv_rows", (NODES_PAD, 2 * F), F32).ap()
        e.x1_rows = nc.dram_tensor("x1_rows", (WINS * P, F), F32).ap()
        e.edge_rows = nc.dram_tensor("edge_rows", (TILES_PAD, 2 * P), I32).ap()
        e.sorted_pairs = nc.dram_tensor("sorted_pairs", (TILES_PAD * P, 2), I32).ap()
        e.cut_rows = nc.dram_tensor("cut_rows", (SLOTS_TAB, P + 1), F32).ap()

        e.src_idx = e.sb("src_idx", [P, SLOTS_TAB], I32, top)
        e.neg_loc = e.sb("neg_loc", [P, SLOTS_TAB], F32, top)
        e.win_at = e.sb("win_at", [P, SLOTS_TAB], I32, top)
        e.iota_f = e.sb("iota_f", [P, P], F32, top)
        e.ident_f = e.sb("ident_f", [P, P], F32, top)
        e.ident_b = e.sb("ident_b", [P, P], BF16, top)
        e.eps_col = e.sb("eps_col", [P, 1], F32, top)
        e.stage = e.sb("stage", [P, 2, RING, GS], I32, top)
        e.acc = e.sb("acc", [P, WINS_PAD * AW], F32, top)

        with ExitStack() as life:
            e.head_eq = e.sb("head_eq", [P, P], F32, life)
            e.slot_sel = e.sb("slot_sel", [P, LAP], F32, life)
            e.apart = e.sb("apart", [P, LAPS, 2, ENDS], BF16, life)
            e.goes_on = e.sb("goes_on", [P, LAPS], F32, life)
            e.neg_first_loc = e.sb("neg_first_loc", [P, LAPS], F32, life)
            e.q_all = e.sb("q_all", [P, WINS_PAD * F], F32, life)
            with ExitStack() as edge_life:
                e.ed = e.sb("ed", [TROWS, TPR, 2 * P], I32, edge_life)
                e.descents = e.sb("descents", [TROWS, 1], F32, edge_life)
                e.row_ones = e.sb("row_ones", [TROWS, 1], F32, edge_life)
                e.thr = e.sb("thr", [TROWS, WINS + 1], F32, edge_life)
                e.ones = e.sb("ones", [P, P], F32, edge_life)
                e.tri = e.sb("tri", [WINS, WINS], F32, edge_life)
                e.slot_row = e.sb("slot_row", [WINS, SLOTS_TAB], F32, edge_life)
                e.slot_col = e.sb("slot_col", [P, SC], F32, edge_life)
                e.cut = e.sb("cut", [P, SC, P + 1], F32, edge_life)
                project(nc, e)
                sort_edges(nc, e)
                build_tables(nc, e)
            edge_attention(nc, e)
        e.cnt_rec = e.sb("cnt_rec", [P, WINS], F32, top)
        e.x1_all = e.sb("x1_all", [P, WINS * F], F32, top)
        node_ffn(nc, e)
        edge_mean(nc, e)
        node_out(nc, e)


def build_tables(nc, e):
    with ExitStack() as ctx:
        ed = e.ed
        edge_dst = e.sb("edge_dst", [TROWS, TPR, 2], F32, ctx)
        past_last = e.sb("past_last", [TROWS, TPR, WINS], F32, ctx)
        past_first = e.sb("past_first", [TROWS, TPR, WINS], F32, ctx)
        wcol = e.sb("wcol", [WINS, 8], F32, ctx)
        begun = e.sb("begun", [WINS, SLOTS_TAB], F32, ctx)
        ended = e.sb("ended", [WINS, SLOTS_TAB], F32, ctx)
        own = e.sb("own", [WINS, SLOTS_TAB], F32, ctx)
        tile_f = e.sb("tile_f", [P, SC], F32, ctx)
        tile_i = e.sb("tile_i", [P, SC], I32, ctx)
        win_base = e.sb("win_base", [P, SC], F32, ctx)
        got = e.sb("got", [P, SC, 2 * P], I32, ctx)
        src_f = e.sb("src_f", [P, SC, P], F32, ctx)
        loc_f = e.sb("loc_f", [P, SC, P], F32, ctx)
        in_lo = e.sb("in_lo", [P, SC, P], F32, ctx)
        in_both = e.sb("in_both", [P, SC, P], F32, ctx)
        key = e.sb("key", [P, SC, P], F32, ctx)
        end_diag = e.sb("end_diag", [P, 2, SC, P], F32, ctx)
        end_key = e.sb("end_key", [P, 2, SLOTS_TAB], F32, ctx)
        picked = e.sb("picked", [P, 2, SLOTS_TAB], F32, ctx)
        own_key = e.sb("own_key", [P, 2, SLOTS_TAB // LAP], F32, ctx)
        first_win = e.sb("first_win", [P, LAPS], F32, ctx)
        ps_w = e.ps("ps_w", [P, 512], F32, ctx)
        ps_s = e.ps("ps_s", [P, 512], F32, ctx)
        ps_row = e.ps("ps_row", [P, 2, 512], F32, ctx)
        ps_t = e.ps("ps_t", [P, 4, 4, P], F32, ctx)
        ed_out = e.sem("ed_out")
        tab_d = e.sem("tab_d")
        tab_pe = e.sem("tab_pe")
        tab_a = e.sem("tab_a")
        rows_in = e.sem("rows_in")
        cut_out = e.sem("cut_out")
        block = ctx.enter_context(nc.Block())

        @block.sync
        def _(sp):
            sp.dma_start(e.edge_rows.rearrange("(p t) c -> p t c", p=TROWS), ed[:]).then_inc(ed_out, 16)
            sp.wait_ge(tab_d, 21)
            sp.dma_start(e.cut_rows.rearrange("(c p) r -> p c r", p=P), e.cut[:]).then_inc(cut_out, 16)
            sp.wait_ge(cut_out, 16)

        @block.gpsimd
        def _(pool):
            pool.wait_ge(tab_d, 14)
            pool.wait_ge(ed_out, 16)
            for c in range(SC):
                pool.indirect_dma_start(out=got[:, c, :], out_offset=None, in_=e.edge_rows[:, :],
                                        in_offset=bass.IndirectOffsetOnAxis(ap=tile_i[:, c:c + 1], axis=0)
                                        ).then_inc(rows_in, 16)

        @block.vector
        def _(dve):
            done = [0]

            def step(ins):
                done[0] += 1
                ins.then_inc(tab_d, 1)
                dve.wait_ge(tab_d, done[0])

            step(dve.tensor_copy(edge_dst[:], ed[:, :, P::P - 1]))
            step(dve.tensor_tensor(past_last[:], e.thr[:, 0:WINS].unsqueeze(1).to_broadcast([TROWS, TPR, WINS]),
                                   edge_dst[:, :, 1:2].to_broadcast([TROWS, TPR, WINS]), ALU.is_gt))
            step(dve.tensor_tensor(past_first[:], e.thr[:, 1:WINS + 1].unsqueeze(1).to_broadcast([TROWS, TPR, WINS]),
                                   edge_dst[:, :, 0:1].to_broadcast([TROWS, TPR, WINS]), ALU.is_gt))
            dve.wait_ge(tab_pe, 1)
            step(dve.tensor_copy(wcol[:, 0:2], ps_w[0:WINS, 0:2]))
            step(dve.tensor_tensor(wcol[:, 2:3], wcol[:, 1:2], wcol[:, 0:1], ALU.subtract))
            dve.wait_ge(tab_pe, 2)
            step(dve.tensor_copy(wcol[:, 3:4], ps_w[0:WINS, 2:3]))
            step(dve.tensor_tensor(wcol[:, 4:5], wcol[:, 3:4], wcol[:, 2:3], ALU.add))
            step(dve.tensor_tensor(wcol[:, 5:6], wcol[:, 0:1], wcol[:, 3:4], ALU.subtract))
            step(dve.tensor_scalar(begun[:], e.slot_row[:], wcol[:, 3:4], None, ALU.is_ge))
            step(dve.tensor_scalar(ended[:], e.slot_row[:], wcol[:, 4:5], None, ALU.is_ge))
            step(dve.tensor_tensor(own[:], begun[:], ended[:], ALU.subtract))
            dve.wait_ge(tab_pe, 3)
            step(dve.tensor_tensor(tile_f[:], ps_s[:, 0:SC], e.slot_col[:], ALU.add))
            step(dve.tensor_scalar(tile_f[:], tile_f[:], float(TILES_PAD - 1), None, ALU.min))
            step(dve.tensor_copy(tile_i[:], tile_f[:]))
            step(dve.tensor_scalar(win_base[:], ps_s[:, SC:2 * SC], float(P), None, ALU.mult))
            dve.wait_ge(rows_in, 16 * SC)
            step(dve.tensor_tensor(loc_f[:], got[:, :, P:2 * P],
                                   win_base[:].unsqueeze(2).to_broadcast([P, SC, P]), ALU.subtract))
            step(dve.tensor_scalar(in_lo[:], loc_f[:], 0.0, None, ALU.is_ge))
            step(dve.scalar_tensor_tensor(in_both[:], loc_f[:], float(P), in_lo[:], ALU.is_lt, ALU.mult))
            step(dve.scalar_tensor_tensor(key[:], got[:, :, P:2 * P], 1.0, in_both[:], ALU.add, ALU.mult))
            step(dve.tensor_tensor(e.cut[:, :, 1:P], key[:, :, 1:P], key[:, :, 0:P - 1], ALU.not_equal))
            step(dve.tensor_scalar(e.cut[:, :, 1:P], e.cut[:, :, 1:P], -BIG, None, ALU.mult))
            step(dve.tensor_tensor(end_diag[:], e.ident_f[:].unsqueeze(1).unsqueeze(1).to_broadcast([P, 2, SC, P]),
                                   key[:, :, P - 1::1 - P].rearrange("p c e -> p e c").unsqueeze(3).to_broadcast(
                                       [P, 2, SC, P]), ALU.mult))
            dve.wait_ge(tab_pe, 5)
            for b in range(2):
                cols = slice(b * 4 * P, min((b + 1) * 4, SC) * P)
                flat = ps_t[:, 2 + b].rearrange("p a b -> p (a b)")[:, 0:cols.stop - cols.start]
                step(dve.tensor_scalar(e.neg_loc[:, cols], flat, -1.0, None, ALU.mult))
            step(dve.tensor_copy(e.ident_b[:], e.ident_f[:]))
            step(dve.tensor_reduce(e.slot_sel[:], e.ident_f[:].rearrange("p (h s) -> p s h", s=LAP),
                                   AX.X, ALU.add))
            dve.wait_ge(tab_a, 9)
            step(dve.tensor_tensor(picked[:].rearrange("p e (l s) -> p e l s", s=LAP),
                                   end_key[:].rearrange("p e (l s) -> p e l s", s=LAP),
                                   e.slot_sel[:].unsqueeze(1).unsqueeze(1).to_broadcast([P, 2, SLOTS_TAB // LAP, LAP]),
                                   ALU.mult))
            step(dve.tensor_reduce(own_key[:], picked[:].rearrange("p e (l s) -> p e l s", s=LAP), AX.X, ALU.add))
            step(dve.memset(e.apart[:, 0, :, ENDS - 1:ENDS], 1.0))
            for side in range(2):
                mine = own_key[:, 1 - side, 0:LAPS].unsqueeze(2)
                for end in range(2):
                    step(dve.tensor_tensor(e.apart[:, :, side, end * LAP:(end + 1) * LAP],
                                           end_key[:, end, 0:SLOTS].rearrange("p (l s) -> p l s", s=LAP),
                                           mine.to_broadcast([P, LAPS, LAP]), ALU.not_equal))
                step(dve.tensor_tensor(e.apart[:, 1:LAPS, side, ENDS - 1:ENDS],
                                       end_key[:, 0, LAP - 1:SLOTS - 1:LAP].unsqueeze(2), mine[:, 1:LAPS],
                                       ALU.not_equal))
            step(dve.tensor_scalar(e.goes_on[:].unsqueeze(2), e.apart[:, :, 0, ENDS - 1:ENDS], 0.0, None,
                                   ALU.is_equal))
            step(dve.tensor_scalar(e.apart[:], e.apart[:], -BIG, None, ALU.mult))
            step(dve.tensor_scalar(first_win[:], e.win_at[:, 0:SLOTS:LAP], float(P), 1.0, ALU.mult, ALU.add))
            step(dve.tensor_tensor(e.neg_first_loc[:], first_win[:], end_key[:, 1, 0:SLOTS:LAP], ALU.subtract))

        @block.scalar
        def _(act):
            half = SLOTS_TAB // 2
            act.wait_ge(rows_in, 16 * SC)
            act.activation(src_f[:], got[:, :, 0:P], ACT.Copy).then_inc(tab_a, 1)
            act.wait_ge(tab_pe, 4)
            for n in range(2):
                act.activation(e.win_at[:, n * half:(n + 1) * half], ps_row[:, n, 0:half], ACT.Copy).then_inc(tab_a, 1)
            act.wait_ge(tab_pe, 5)
            for b in range(2):
                cols = slice(b * 4 * P, min((b + 1) * 4, SC) * P)
                flat = ps_t[:, b].rearrange("p a b -> p (a b)")[:, 0:cols.stop - cols.start]
                act.activation(e.src_idx[:, cols], flat, ACT.Copy).then_inc(tab_a, 1)
            act.wait_ge(tab_pe, 6)
            for n, bank in enumerate((ps_w[:], ps_s[:], ps_row[:, 0], ps_row[:, 1])):
                act.activation(end_key[:, n // 2, (n % 2) * half:(n % 2 + 1) * half], bank[:, 0:half],
                               ACT.Copy).then_inc(tab_a, 1)

        @block.tensor
        def _(pe):
            pe.wait_ge(tab_d, 3)
            for r in range(TPR):
                pe.matmul(ps_w[0:WINS, 0:1], past_last[:, r, :], e.ones[0:TROWS, 0:1],
                          start=(r == 0), stop=(r == TPR - 1))
            for r in range(TPR):
                mm = pe.matmul(ps_w[0:WINS, 1:2], past_first[:, r, :], e.ones[0:TROWS, 0:1],
                               start=(r == 0), stop=(r == TPR - 1))
            mm.then_inc(tab_pe, 1)
            pe.wait_ge(tab_d, 5)
            pe.matmul(ps_w[0:WINS, 2:3], e.tri[:], wcol[:, 2:3], start=True, stop=True).then_inc(tab_pe, 1)
            pe.wait_ge(tab_d, 11)
            for c in range(SC):
                pe.matmul(ps_s[:, c:c + 1], own[:, c * P:(c + 1) * P], wcol[:, 5:6], start=True, stop=True)
                mm = pe.matmul(ps_s[:, SC + c:SC + c + 1], ended[:, c * P:(c + 1) * P], e.ones[0:WINS, 0:1],
                               start=True, stop=True)
            mm.then_inc(tab_pe, 1)
            half = SLOTS_TAB // 2
            for n in range(2):
                mm = pe.matmul(ps_row[:, n, 0:half], e.ones[0:WINS, :], ended[:, n * half:(n + 1) * half],
                               start=True, stop=True)
            mm.then_inc(tab_pe, 1)
            pe.wait_ge(tab_a, 1)
            for c in range(SC):
                pe.transpose(ps_t[:, c // 4, c % 4, :], src_f[:, c, :], e.ident_f[:])
            pe.wait_ge(tab_d, 16)
            for c in range(SC):
                mm = pe.transpose(ps_t[:, 2 + c // 4, c % 4, :], loc_f[:, c, :], e.ident_f[:])
            mm.then_inc(tab_pe, 1)
            pe.wait_ge(tab_d, 22)
            pe.wait_ge(tab_a, 3)
            flat = end_diag[:].rearrange("p e c n -> p (e c n)")
            for n, bank in enumerate((ps_w[:], ps_s[:], ps_row[:, 0], ps_row[:, 1])):
                mm = pe.matmul(bank[:, 0:half], e.ones[:], flat[:, n * half:(n + 1) * half], start=True, stop=True)
            mm.then_inc(tab_pe, 1)


def sort_edges(nc, e):
    with ExitStack() as ctx:
        unsorted_at = e.sb("unsorted_at", [1, 1], I32, ctx)
        ones = e.sb("s_ones", [P, P], F32, ctx)
        earlier = e.sb("earlier", [P, P], F32, ctx)
        later = e.sb("later", [P, P], F32, ctx)
        ident = e.sb("s_ident", [P, P], F32, ctx)
        node_in = e.sb("node_in", [P, P], F32, ctx)
        win_first = e.sb("win_first", [P, WINS_PAD + 1], F32, ctx)
        pair_i = e.sb("pair_i", [P, 2], I32, ctx)
        row_i = e.sb("row_i", [P, P], I32, ctx)
        dst_f = e.sb("dst_f", [P, 1], F32, ctx)
        row_f = e.sb("row_f", [P, P], F32, ctx)
        reached = e.sb("reached", [P, WINS_PAD + 1], F32, ctx)
        hot_win = e.sb("hot_win", [P, WINS_PAD], F32, ctx)
        win_no = e.sb("win_no", [P, 1], F32, ctx)
        loc = e.sb("s_loc", [P, 1], F32, ctx)
        hot_loc = e.sb("hot_loc", [P, P], F32, ctx)
        hot_loc_t = e.sb("hot_loc_t", [P, P], F32, ctx)
        place = e.sb("place", [P, WINS_PAD], F32, ctx)
        wins_sum = e.sb("wins_sum", [P, WINS_PAD], F32, ctx)
        picked = e.sb("s_picked", [P, WINS_PAD], F32, ctx)
        same = e.sb("same", [P, P], F32, ctx)
        same_earlier = e.sb("same_earlier", [P, P], F32, ctx)
        at = e.sb("at", [P, 2], F32, ctx)
        to = e.sb("to", [P, 1], F32, ctx)
        to_i = e.sb("to_i", [P, 1], I32, ctx)
        pairs_sb = e.sb("pairs_sb", [TROWS, TPR, P, 2], I32, ctx)
        ps_flag = e.ps("ps_flag", [P, 512], F32, ctx)
        ps_count = e.ps("ps_count", [P, 512], F32, ctx)
        ps_turn = e.ps("ps_turn", [P, 512], F32, ctx)
        ps_pick = e.ps("ps_pick", [P, 512], F32, ctx)
        flag_summed = e.sem("flag_summed")
        flag_at = e.sem("flag_at")
        s_consts = e.sem("s_consts")
        tile_free = e.sem("tile_free")
        tile_in = e.sem("tile_in")
        sort_d = e.sem("sort_d")
        hots_made = e.sem("hots_made")
        counted = e.sem("counted")
        prefixed = e.sem("prefixed")
        places_made = e.sem("places_made")
        loc_turned = e.sem("loc_turned")
        loc_t_copied = e.sem("loc_t_copied")
        place_picked = e.sem("place_picked")
        to_made = e.sem("to_made")
        send_turns = e.sem("send_turns")
        sent = e.sem("sent")
        pairs_in = e.sem("pairs_in")
        block = ctx.enter_context(nc.Block())
        T = TILES_PAD

        def flag_of(eng):
            eng.wait_ge(flag_at, 1)
            reg = eng.alloc_register("is_unsorted")
            eng.reg_load(reg, unsorted_at[0:1, 0:1])
            return reg

        @block.sync
        def _(sp):
            reg = flag_of(sp)
            with sp.If_ne(reg, 0):
                for n in range(2):
                    with sp.Fori(0, T) as t:
                        sp.wait_ge(tile_free, t + (n * T + 1))
                        sp.dma_start(pair_i[:], e.edges[bass.ds(t, 1), :].rearrange("o (c p) -> p (o c)", p=P),
                                     allow_slow_non_contiguous=True).then_inc(tile_in, 16)
                        sp.dma_start(row_i[:], e.edges[bass.ds(t, 1), P:2 * P].to_broadcast([P, P])
                                     ).then_inc(tile_in, 16)
                sp.wait_ge(tile_free, 2 * T + 1)
                sp.dma_start(pairs_sb[:], e.sorted_pairs.rearrange("(r t p) c -> r t p c", t=TPR, p=P)
                             ).then_inc(pairs_in, 16)
            sp.end_ifs()

        @block.gpsimd
        def _(pool):
            reg = flag_of(pool)
            with pool.If_ne(reg, 0):
                pool.iota(node_in[:], [[1, P]], base=0, channel_multiplier=0,
                          allow_small_or_imprecise_dtypes=True).then_inc(s_consts, 1)
                pool.iota(win_first[:], [[P, WINS_PAD + 1]], base=0, channel_multiplier=0,
                          allow_small_or_imprecise_dtypes=True).then_inc(s_consts, 1)
                pool.memset(ones[:], 1.0).then_inc(s_consts, 1)
                pool.wait_ge(s_consts, 3)
                pool.affine_select(earlier[:], ones[:], [[-1, P]], ALU.is_gt, 0.0, base=0,
                                   channel_multiplier=1).then_inc(s_consts, 1)
                pool.affine_select(later[:], ones[:], [[1, P]], ALU.is_gt, 0.0, base=0,
                                   channel_multiplier=-1).then_inc(s_consts, 1)
                pool.affine_select(ident[:], ones[:], [[-1, P]], ALU.is_equal, 0.0, base=0,
                                   channel_multiplier=1).then_inc(s_consts, 1)
                with pool.Fori(0, T) as t:
                    pool.wait_ge(to_made, t + 1)
                    pool.sem_inc(send_turns, 1)
                    pool.indirect_dma_start(out=e.sorted_pairs[:, :],
                                            out_offset=bass.IndirectOffsetOnAxis(ap=to_i[:, 0:1], axis=0),
                                            in_=pair_i[:], in_offset=None).then_inc(sent, 16)
                    pool.wait_ge(sent, 16 * t + 16)
                    pool.sem_inc(tile_free, 1)
            pool.end_ifs()

        @block.vector
        def _(dve):
            dve.wait_ge(flag_summed, 1)
            dve.tensor_scalar(unsorted_at[:], ps_flag[0:1, 0:1], 1.0, None, ALU.min).then_inc(flag_at, 1)
            reg = flag_of(dve)
            HOTS, PASS1, PASS2 = 7, 8, 16

            def step_of(base):
                k = [0]

                def step(ins):
                    k[0] += 1
                    ins.then_inc(sort_d, 1)
                    dve.wait_ge(sort_d, base + k[0])
                return step

            def make_hots(n, t, step):
                dve.wait_ge(tile_in, 32 * t + 32 * (n * T + 1))
                step(dve.tensor_copy(dst_f[:], pair_i[:, 1:2]))
                step(dve.tensor_copy(row_f[:], row_i[:]))
                step(dve.tensor_scalar(reached[:], win_first[:], dst_f[:, 0:1], None, ALU.is_le))
                step(dve.tensor_tensor(hot_win[:], reached[:, 0:WINS_PAD], reached[:, 1:WINS_PAD + 1], ALU.subtract))
                step(dve.tensor_reduce(win_no[:], reached[:, 1:WINS_PAD + 1], AX.X, ALU.add))
                step(dve.scalar_tensor_tensor(loc[:], win_no[:], -float(P), dst_f[:], ALU.mult, ALU.add))
                step(dve.tensor_scalar(hot_loc[:], node_in[:], loc[:, 0:1], None, ALU.is_equal))
                dve.sem_inc(hots_made, 1)

            with dve.If_ne(reg, 0):
                step = step_of(0)
                dve.wait_ge(s_consts, 6)
                step(dve.memset(place[:], 0.0))
                dve.sem_inc(tile_free, 1)
                with dve.Fori(0, T) as t:
                    step = step_of(PASS1 * t + 1)
                    make_hots(0, t, step)
                    dve.wait_ge(counted, t + 1)
                    step(dve.tensor_tensor(place[:], place[:], ps_count[:, 0:WINS_PAD], ALU.add))
                    dve.sem_inc(tile_free, 1)
                step = step_of(PASS1 * T + 1)
                dve.wait_ge(prefixed, 2)
                step(dve.memset(picked[:], 0.0))
                step(dve.tensor_tensor_scan(wins_sum[:], ps_pick[:, 0:WINS_PAD], picked[:], 0.0,
                                            ALU.add, ALU.max))
                step(dve.tensor_tensor(wins_sum[:], wins_sum[:], ps_pick[:, 0:WINS_PAD], ALU.subtract))
                step(dve.tensor_tensor(place[:], wins_sum[:], ps_turn[:, 0:WINS_PAD], ALU.add))
                dve.sem_inc(places_made, 1)
                with dve.Fori(0, T) as t:
                    step = step_of(PASS2 * t + (PASS1 * T + 5))
                    make_hots(1, t, step)
                    dve.wait_ge(loc_turned, t + 1)
                    step(dve.tensor_copy(hot_loc_t[:], ps_turn[:, 0:P]))
                    dve.sem_inc(loc_t_copied, 1)
                    dve.wait_ge(place_picked, t + 1)
                    step(dve.tensor_tensor(picked[:], hot_win[:], ps_pick[:, 0:WINS_PAD], ALU.mult))
                    step(dve.tensor_reduce(at[:, 0:1], picked[:], AX.X, ALU.add))
                    step(dve.tensor_scalar(same[:], row_f[:], dst_f[:, 0:1], None, ALU.is_equal))
                    step(dve.tensor_tensor(same_earlier[:], same[:], earlier[:], ALU.mult))
                    step(dve.tensor_reduce(at[:, 1:2], same_earlier[:], AX.X, ALU.add))
                    step(dve.tensor_reduce(to[:], at[:], AX.X, ALU.add))
                    step(dve.tensor_copy(to_i[:], to[:]))
                    dve.wait_ge(counted, t + (T + 1))
                    step(dve.tensor_tensor(place[:], place[:], ps_count[:, 0:WINS_PAD], ALU.add))
                    dve.sem_inc(to_made, 1)
                dve.wait_ge(pairs_in, 16)
                step = step_of((PASS1 + PASS2) * T + 5)
                step(dve.tensor_copy(e.ed[:].rearrange("r t (c p) -> r t c p", p=P),
                                     pairs_sb[:].rearrange("r t p c -> r t c p")))
            dve.end_ifs()

        @block.tensor
        def _(pe):
            pe.matmul(ps_flag[0:1, 0:1], e.descents[:], e.row_ones[:], start=True,
                      stop=True).then_inc(flag_summed, 1)
            reg = flag_of(pe)

            def count(n, t):
                pe.wait_ge(hots_made, t + (n * T + 1))
                pe.matmul(ps_count[:, 0:WINS_PAD], hot_loc[:], hot_win[:], start=True, stop=True).then_inc(counted, 1)

            with pe.If_ne(reg, 0):
                with pe.Fori(0, T) as t:
                    count(0, t)
                pe.wait_ge(tile_free, T + 1)
                pe.matmul(ps_pick[:, 0:WINS_PAD], ones[:], place[:], start=True, stop=True).then_inc(prefixed, 1)
                pe.matmul(ps_turn[:, 0:WINS_PAD], later[:], place[:], start=True, stop=True).then_inc(prefixed, 1)
                pe.wait_ge(places_made, 1)
                with pe.Fori(0, T) as t:
                    count(1, t)
                    pe.transpose(ps_turn[:, 0:P], hot_loc[:], ident[:]).then_inc(loc_turned, 1)
                    pe.wait_ge(loc_t_copied, t + 1)
                    pe.matmul(ps_pick[:, 0:WINS_PAD], hot_loc_t[:], place[:], start=True,
                              stop=True).then_inc(place_picked, 1)
            pe.end_ifs()


QB = 5
QLAPS = WINS_PAD // (2 * QB)
Q_SCALE = float(F) ** -0.5


def project(nc, e):
    assert WINS_PAD % (2 * QB) == 0 and Q_SCALE == 2.0 ** -4
    with ExitStack() as ctx:
        xt = e.sb("xt", [P, 2, FC, QB * P], F32, ctx)
        w_sb = e.sb("w_sb", [P, FC, 3 * F], F32, ctx)
        kv_sb = e.sb("kv_sb", [P, 2, QB, 2 * F], F32, ctx)
        ps_kv = e.ps("ps_kv", [P, 2, 512], F32, ctx)
        ps_q = e.ps("ps_q", [P, 2, 512], F32, ctx)
        tile_next = e.sb("tile_next", [TROWS, P], I32, ctx)
        falls = e.sb("falls", [TROWS, TPR, P], F32, ctx)
        w_in = e.sem("w_in")
        edges_in = e.sem("edges_in")
        falls_d = e.sem("falls_d")
        consts = e.sem("consts")
        xt_in = [e.sem("xt_in0"), e.sem("xt_in1")]
        projected = e.sem("projected")
        kv_copied = e.sem("kv_copied")
        kv_stored = [e.sem("kv_stored0"), e.sem("kv_stored1")]
        q_kept = e.sem("q_kept")
        block = ctx.enter_context(nc.Block())
        xT_v = e.xT.rearrange("(c p) n -> p c n", p=P)
        kv_v = e.kv_rows.rearrange("(w p) f -> p w f", p=P)

        @block.sync
        def _(sp):
            def load(i, b):
                wait(sp, projected, (2 * i + b - 1) * QB)
                sp.dma_start(xt[:, b], xT_v[:, :, bass.ds((2 * i + b) * (QB * P), QB * P)]).then_inc(xt_in[b], 16)

            def store(i, b):
                sp.wait_ge(kv_copied, (2 * i + b + 1) * QB)
                sp.dma_start(kv_v[:, bass.ds((2 * i + b) * QB, QB), :], kv_sb[:, b]).then_inc(kv_stored[b], 16)

            def lap(i, last):
                for b in range(2):
                    store(i, b)
                    if not last:
                        load(i + 1, b)

            sp.dma_start(w_sb[:], e.wqkv.rearrange("(c p) n -> p c n", p=P)).then_inc(w_in, 16)
            load(0, 0)
            load(0, 1)
            sp.dma_start(e.ed[:], e.edges.rearrange("(p t) c -> p t c", p=TROWS)).then_inc(edges_in, 16)
            sp.dma_start(tile_next[0:TROWS - 1, :], e.edges.rearrange("(p t) c -> p t c", p=TROWS)
                         [1:TROWS, 0, P:2 * P]).then_inc(edges_in, 16)
            laps(sp, lap, QLAPS)
            for b in range(2):
                sp.wait_ge(kv_stored[b], 16 * QLAPS)

        @block.gpsimd
        def _(pool):
            pool.iota(e.thr[:], [[P, WINS + 1]], base=0, channel_multiplier=0,
                      allow_small_or_imprecise_dtypes=True).then_inc(consts, 1)
            pool.memset(e.ones[:], 1.0).then_inc(consts, 1)
            pool.iota(e.slot_row[:], [[1, SLOTS_TAB]], base=0, channel_multiplier=0,
                      allow_small_or_imprecise_dtypes=True).then_inc(consts, 1)
            pool.iota(e.slot_col[:], [[P, SC]], base=0, channel_multiplier=1,
                      allow_small_or_imprecise_dtypes=True).then_inc(consts, 1)
            pool.memset(e.cut[:], 0.0).then_inc(consts, 1)
            pool.iota(e.iota_f[:], [[1, P]], base=0, channel_multiplier=0,
                      allow_small_or_imprecise_dtypes=True).then_inc(consts, 1)
            pool.memset(e.ident_f[:], 0.0).then_inc(consts, 1)
            pool.memset(e.head_eq[:], 1.0).then_inc(consts, 1)
            pool.memset(e.eps_col[:], EPS).then_inc(consts, 1)
            pool.wait_ge(consts, 9)
            pool.affine_select(e.tri[:], e.ones[0:WINS, 0:WINS], [[1, WINS]], ALU.is_gt, 0.0, base=0,
                               channel_multiplier=-1).then_inc(consts, 1)
            pool.affine_select(e.ident_f[:], e.ident_f[:], [[-1, P]], ALU.not_equal, 1.0, base=0,
                               channel_multiplier=1).then_inc(consts, 1)
            pool.affine_select(e.head_eq[:].rearrange("p (h s) -> p h s", s=LAP),
                               e.head_eq[:].rearrange("p (h s) -> p h s", s=LAP),
                               [[-LAP, HEADS], [0, LAP]], ALU.is_ge, 0.0, base=0,
                               channel_multiplier=1).then_inc(consts, 1)
            pool.wait_ge(consts, 12)
            pool.affine_select(e.head_eq[:].rearrange("p (h s) -> p h s", s=LAP),
                               e.head_eq[:].rearrange("p (h s) -> p h s", s=LAP),
                               [[LAP, HEADS], [0, LAP]], ALU.is_ge, 0.0, base=LAP - 1,
                               channel_multiplier=-1).then_inc(consts, 1)
            pool.memset(e.acc[:], 0.0).then_inc(consts, 1)

        @block.tensor
        def _(pe):
            def lap(i, last):
                for b in range(2):
                    pe.wait_ge(xt_in[b], 16 * (i + 1))
                    for m in range(QB):
                        done = (2 * i + b) * QB + m
                        par = (b * QB + m) % 2
                        wait(pe, kv_copied, done - 1)
                        wait(pe, q_kept, done - 1)
                        for c in range(FC):
                            pe.matmul(ps_kv[:, par, :], xt[:, b, c, m * P:(m + 1) * P], w_sb[:, c, 0:2 * F],
                                      start=(c == 0), stop=(c == FC - 1))
                        for c in range(FC):
                            mm = pe.matmul(ps_q[:, par, 0:F], xt[:, b, c, m * P:(m + 1) * P], w_sb[:, c, 2 * F:],
                                           start=(c == 0), stop=(c == FC - 1))
                        mm.then_inc(projected, 1)

            pe.wait_ge(w_in, 16)
            laps(pe, lap, QLAPS)

        @block.scalar
        def _(act):
            def lap(i, last):
                for b in range(2):
                    wait(act, kv_stored[b], 16 * i)
                    for m in range(QB):
                        done = (2 * i + b) * QB + m
                        par = (b * QB + m) % 2
                        act.wait_ge(projected, done + 1)
                        act.activation(kv_sb[:, b, m, :], ps_kv[:, par, :], ACT.Copy).then_inc(kv_copied, 1)

            laps(act, lap, QLAPS)


        @block.vector
        def _(dve):
            def lap(i, last):
                for t in range(2 * QB):
                    done = 2 * QB * i + t
                    dve.wait_ge(projected, done + 1)
                    dve.tensor_scalar(e.q_all[:, bass.ds(done * F, F)], ps_q[:, t % 2, 0:F], Q_SCALE, None,
                                      ALU.mult).then_inc(q_kept, 1)

            def mark_falls():
                done = [0]

                def step(ins):
                    done[0] += 1
                    ins.then_inc(falls_d, 1)
                    dve.wait_ge(falls_d, done[0])

                dst = e.ed[:, :, P:2 * P]
                last = TROWS - 1
                dve.wait_ge(edges_in, 32)
                step(dve.memset(e.row_ones[:], 1.0))
                step(dve.memset(falls[:], 0.0))
                step(dve.tensor_tensor(falls[:, :, 1:P], dst[:, :, 1:P], dst[:, :, 0:P - 1], ALU.is_lt))
                step(dve.tensor_tensor(falls[:, 1:TPR, 0:1], dst[:, 1:TPR, 0:1], dst[:, 0:TPR - 1, P - 1:P], ALU.is_lt))
                step(dve.tensor_tensor(falls[0:last, 0, 0:1], tile_next[0:last, 0:1], dst[0:last, TPR - 1, P - 1:P],
                                       ALU.is_lt))
                step(dve.tensor_reduce(e.descents[:], falls[:].rearrange("r t p -> r (t p)"), AX.X, ALU.add))

            lap(0, False)
            mark_falls()
            with dve.Fori(1, QLAPS) as i:
                lap(i, False)


def edge_laps(eng, turn):
    turn(0, 0, 2)
    turn(0, 1, 2)
    with eng.Fori(1, LAPS // 2 - 1) as i:
        turn(i, 0, 2)
        turn(i, 1, 2)
    turn(LAPS // 2 - 1, 0, 1)
    turn(LAPS // 2 - 1, 1, 0)


def following(i, par, by):
    return (i + (par + by) // 2, (par + by) % 2)


def ahead(i, par, g, by):
    n = par * RING + g + by
    return (i + n // (2 * RING), n // RING % 2, n % RING)


def edge_attention(nc, e):
    with ExitStack() as ctx:
        kv = e.sb("kv", [P, 2, RING, GS, RW], F32, ctx)
        hot_s = e.sb("hot_s", [P, 2, GS, P], BF16, ctx)
        hot_t = e.sb("hot_t", [P, 2, GS, P], F32, ctx)
        hot_m = e.sb("hot_m", [P, 2, GS, P], F32, ctx)
        score = e.sb("score", [P, 2, HEADS, LAP], F32, ctx)
        below = e.sb("below", [P, HEADS, LAP], F32, ctx)
        cut = e.sb("cut_in", [P, 2, P + 1], F32, ctx)
        runs = e.sb("runs", [P, 2 * P], F32, ctx)
        run = runs[:, 0:P]
        run_b = runs[:, P:2 * P]
        top_m = e.sb("top_m", [P, P], F32, ctx)
        spread = e.sb("spread", [P, ENDS], F32, ctx)
        cand = e.sb("cand", [P, 2, ENDS], F32, ctx)
        end_max = e.sb("end_max", [P, 2], F32, ctx)
        drop = e.sb("drop", [P, 2], F32, ctx)
        node_hot = e.sb("node_hot", [P, P], F32, ctx)
        head_drop = e.sb("head_drop", [P, HEADS], F32, ctx)
        rescale = e.sb("rescale", [P, HEADS], F32, ctx)
        ps_hot = e.ps("ps_hot", [P, 2, GS, P], BF16, ctx)
        ps_lap = e.ps("ps_lap", [P, 512], F32, ctx)
        ps_q = e.ps("ps_q2", [P, 2, 2, F], F32, ctx)
        ps_sum = e.ps("ps_sum", [P, GS, 512], F32, ctx)
        turned_score = ps_lap[:, 0:P]
        turned_m = ps_lap[:, P:2 * P]
        all_ends = ps_lap[:, 2 * P:2 * P + ENDS]
        node_drop = ps_lap[:, 3 * P:3 * P + HEADS]

        staged = e.sem("staged")
        rows_in = [[e.sem(f"rows_in{b}{g}") for g in range(RING)] for b in range(2)]
        pool_turns = e.sem("pool_turns")
        act_turns = e.sem("act_turns")
        cut_in = [e.sem("cut_in0"), e.sem("cut_in1")]
        cleared = e.sem("cleared")
        s_far = e.sem("s_far")
        hot_s_made = e.sem("hot_s_made")
        hot_turned = e.sem("hot_turned")
        hot_t_copied = e.sem("hot_t_copied")
        q_picked = e.sem("q_picked")
        multiplied = e.sem("multiplied")
        scored = e.sem("scored")
        score_turned = e.sem("score_turned")
        spread_made = e.sem("spread_made")
        ends_spread = e.sem("ends_spread")
        lap_d = e.sem("lap_d")
        dropped = e.sem("dropped")
        drop_exp = e.sem("drop_exp")
        first_far = e.sem("first_far")
        first_marked = e.sem("first_marked")
        m_made = e.sem("m_made")
        m_turned = e.sem("m_turned")
        below_made = e.sem("below_made")
        exps_put = e.sem("exps_put")
        drop_rows_made = e.sem("drop_rows_made")
        node_dropped = e.sem("node_dropped")
        rescale_d = e.sem("rescale_d")
        m_far = e.sem("m_far")
        hot_m_made = e.sem("hot_m_made")
        weighed = e.sem("weighed")
        last_weighed = e.sem("last_weighed")
        summed = e.sem("summed")
        added = e.sem("added")
        block = ctx.enter_context(nc.Block())

        def group_no(i, par, g):
            return (2 * i + par) * RING + g

        def weigh(eng, par, g):
            rows = kv[:, par, g, :, F:2 * F].rearrange("p j (h d) -> p j h d", d=DH)
            exps = kv[:, par, g, :, 2 * F:2 * F + HEADS].unsqueeze(3).to_broadcast([P, GS, HEADS, DH])
            return eng.tensor_tensor(rows, rows, exps, ALU.mult)

        @block.sync
        def _(sp):
            def turn(i, par, left):
                wait(sp, m_made, 2 * i + par - 1)
                for h in range(HEADS):
                    sp.dma_start(cut[h * LAP:(h + 1) * LAP, par, :],
                                 e.cut_rows[bass.ds((2 * i + par) * LAP, LAP), :]).then_inc(cut_in[par], 16)

            edge_laps(sp, turn)

        @block.gpsimd
        def _(pool):
            def weigh_last(i, par):
                pool.wait_ge(exps_put, 2 * i + par + 1)
                pool.sem_inc(pool_turns, 1)
                weigh(pool, par, RING - 1).then_inc(last_weighed, 1)

            def turn(i, par, left):
                if not isinstance(i, int) or i > 0:
                    weigh_last(i - 1, par)
                for g in range(RING):
                    n = group_no(i, par, g)
                    pool.wait_ge(staged, 2 * i + par + 1)
                    wait(pool, summed, GS * (n - 2 * RING + 1))
                    pool.sem_inc(pool_turns, 1)
                    for j in range(GS):
                        pool.indirect_dma_start(out=kv[:, par, g, j, 0:2 * F], out_offset=None, in_=e.kv_rows[:, :],
                                                in_offset=bass.IndirectOffsetOnAxis(ap=e.stage[:, par, g, j:j + 1],
                                                                                    axis=0)
                                                ).then_inc(rows_in[par][g], 16)

            edge_laps(pool, turn)
            weigh_last(LAPS // 2 - 1, 0)
            weigh_last(LAPS // 2 - 1, 1)

        @block.scalar
        def _(act):
            def stage_lap(i, par):
                for g in range(RING):
                    wait(act, rows_in[par][g], 16 * GS * i)
                act.sem_inc(act_turns, 1)
                act.activation(e.stage[:, par].rearrange("p g j -> p (g j)"),
                               e.src_idx[:, bass.ds((2 * i + par) * LAP, LAP)], ACT.Copy).then_inc(staged, 1)

            def make_hot(i, par, g, hot, far, made, free_sem, free_value):
                n = group_no(i, par, g)
                wait(act, free_sem, free_value)
                act.sem_inc(act_turns, 1)
                for j in range(GS):
                    ins = act.activation(hot[:, g % 2, j, :], e.iota_f[:], ACT.Abs,
                                         bias=e.neg_loc[:, bass.ds(n * GS + j, 1)])
                ins.then_inc(far, 1)
                act.wait_ge(far, n + 1)
                act.activation(hot[:, g % 2], hot[:, g % 2], ACT.Relu, bias=1.0, scale=-1.0).then_inc(made, 1)

            def hot_for_score(i, par, g):
                make_hot(i, par, g, hot_s, s_far, hot_s_made, hot_turned, group_no(i, par, g) - 1)

            def hot_for_sum(i, par, g):
                make_hot(i, par, g, hot_m, m_far, hot_m_made, summed, GS * (group_no(i, par, g) - 1))

            def copy_turned(i, par, g):
                n = group_no(i, par, g)
                act.wait_ge(hot_turned, n + 1)
                wait(act, q_picked, 2 * (n - 1))
                act.activation(hot_t[:, g % 2], ps_hot[:, g % 2], ACT.Copy).then_inc(hot_t_copied, 1)

            def mark_first(i, par):
                lap = 2 * i + par
                wait(act, node_dropped, lap)
                act.sem_inc(act_turns, 1)
                act.activation(node_hot[:], e.iota_f[:], ACT.Abs,
                               bias=e.neg_first_loc[:, bass.ds(lap, 1)]).then_inc(first_far, 1)
                act.wait_ge(first_far, lap + 1)
                act.activation(node_hot[:], node_hot[:], ACT.Relu, bias=1.0, scale=-1.0).then_inc(first_marked, 1)

            def exps(i, par):
                lap = 2 * i + par
                act.wait_ge(dropped, lap + 1)
                act.activation(drop[:, 1:2], drop[:, 0:1], ACT.Exp).then_inc(drop_exp, 1)
                act.wait_ge(below_made, lap + 1)
                act.activation(kv[:, par].rearrange("p g j w -> p (g j) w")[:, :, 2 * F:2 * F + HEADS],
                               below[:].rearrange("p h s -> p s h"), ACT.Exp).then_inc(exps_put, 1)

            def turn(i, par, left):
                if left > 1:
                    stage_lap(*following(i, par, 2))
                for g in range(RING):
                    after = RING * (left + 1) - 1 - g
                    if after >= 8:
                        hot_for_score(*ahead(i, par, g, 8))
                    if after >= 7:
                        copy_turned(*ahead(i, par, g, 7))
                    if after >= 1:
                        hot_for_sum(*ahead(i, par, g, 1))
                    if left and g == 1:
                        mark_first(*following(i, par, 1))
                if left:
                    exps(*following(i, par, 1))

            stage_lap(0, 0)
            stage_lap(0, 1)
            hot_for_score(0, 0, 0)
            for n in range(7):
                hot_for_score(*ahead(0, 0, n, 1))
                copy_turned(*ahead(0, 0, n, 0))
            hot_for_sum(0, 0, 0)
            mark_first(0, 0)
            act.wait_ge(cleared, 2)
            exps(0, 0)
            edge_laps(act, turn)

        @block.vector
        def _(dve):
            regs = [dve.alloc_register(f"sum_win{j}") for j in range(GS)]
            lap_reg = dve.alloc_register("lap_win")
            LAP_STEPS, RESCALE_STEPS = 5, 4

            def multiply_half(i, par, g, half):
                if half == 0:
                    dve.wait_ge(rows_in[par][g], 16 * GS * (i + 1))
                dve.wait_ge(q_picked, 2 * group_no(i, par, g) + half + 1)
                rows = kv[:, par, g, 2 * half:2 * half + 2, 0:F]
                dve.tensor_tensor(rows, rows, ps_q[:, half], ALU.mult).then_inc(multiplied, 1)

            def score_group(i, par, g):
                n = group_no(i, par, g)
                if g == 0:
                    wait(dve, below_made, 2 * i + par - 1)
                dve.wait_ge(multiplied, 2 * n + 2)
                dve.tensor_reduce(score[:, par, :, g * GS:(g + 1) * GS].rearrange("p h j -> p j h"),
                                  kv[:, par, g, :, 0:F].rearrange("p j (h d) -> p j h d", d=DH),
                                  AX.X, ALU.add).then_inc(scored, 1)

            def weigh_group(i, par, g):
                if g == 0:
                    dve.wait_ge(exps_put, 2 * i + par + 1)
                weigh(dve, par, g).then_inc(weighed, 1)

            def add_slot(i, par, g, j):
                n = group_no(i, par, g)
                if j == 0:
                    dve.reg_load(regs, e.win_at[0:1, bass.ds(n * GS, GS)])
                win = dve.snap(regs[j], min_val=0, max_val=WINS_PAD - 1)
                dve.wait_ge(summed, GS * n + j + 1)
                wait(dve, added, GS * n + j)
                if g == 0 and j == 0:
                    dve.wait_ge(rescale_d, RESCALE_STEPS * (2 * i + par) + 4)
                dst = e.acc[:, bass.ds(win * AW, AW)]
                dve.tensor_tensor(dst, dst, ps_sum[:, j, 0:AW], ALU.add).then_inc(added, 1)

            def own_ends(i, par):
                lap = 2 * i + par
                dve.wait_ge(cut_in[par], 16 * HEADS * (i + 1))
                dve.wait_ge(score_turned, lap + 1)
                dve.tensor_tensor_scan(run, cut[:, par, 0:P], turned_score, -BIG, ALU.add,
                                       ALU.max).then_inc(lap_d, 1)
                dve.tensor_tensor_scan(run_b[:, ::-1], cut[:, par, P:0:-1], turned_score[:, ::-1], -BIG, ALU.add,
                                       ALU.max).then_inc(lap_d, 1)

            def spread_own(i, par):
                dve.wait_ge(lap_d, LAP_STEPS * (2 * i + par) + 2)
                dve.tensor_tensor(spread[:, 0:2 * LAP].rearrange("p (e s) -> p e s", s=LAP),
                                  e.slot_sel[:].unsqueeze(1).to_broadcast([P, 2, LAP]),
                                  runs[:, P - 1:P + 1].unsqueeze(2).to_broadcast([P, 2, LAP]),
                                  ALU.mult).then_inc(spread_made, 1)

            def candidates(i, par):
                lap = 2 * i + par
                dve.wait_ge(ends_spread, lap + 1)
                dve.tensor_tensor(cand[:], e.apart[:, bass.ds(lap, 1)].rearrange("p l a b -> p (l a) b"),
                                  all_ends.unsqueeze(1).to_broadcast([P, 2, ENDS]), ALU.add).then_inc(lap_d, 1)

            def ends_max(i, par):
                dve.wait_ge(lap_d, LAP_STEPS * (2 * i + par) + 3)
                dve.tensor_reduce(end_max[:], cand[:], AX.X, ALU.max).then_inc(lap_d, 1)

            def maxima(i, par):
                lap = 2 * i + par
                dve.wait_ge(lap_d, LAP_STEPS * lap + 4)
                dve.tensor_tensor_scan(run, cut[:, par, 0:P], turned_score, end_max[:, 0:1], ALU.add,
                                       ALU.max).then_inc(lap_d, 1)
                dve.scalar_tensor_tensor(drop[:, 0:1], all_ends[:, ENDS - 1:ENDS], end_max[:, 0:1],
                                         e.goes_on[:, bass.ds(lap, 1)], ALU.subtract, ALU.mult).then_inc(dropped, 1)
                dve.wait_ge(lap_d, LAP_STEPS * lap + 5)
                dve.tensor_tensor_scan(top_m[:, ::-1], cut[:, par, P:0:-1], run[:, ::-1], end_max[:, 1:2], ALU.add,
                                       ALU.max).then_inc(m_made, 1)

            def keep_last(i, par):
                dve.wait_ge(m_made, 2 * i + par + 1)
                dve.tensor_tensor(spread[:, ENDS - 1:ENDS], top_m[:, P - 1:P], e.slot_sel[:, LAP - 1:LAP],
                                  ALU.mult).then_inc(rescale_d, 1)

            def drop_rows(i, par):
                dve.wait_ge(drop_exp, 2 * i + par + 1)
                own = e.ident_f[:, 0:P:LAP]
                dve.scalar_tensor_tensor(head_drop[:], own, drop[:, 1:2], own, ALU.mult,
                                         ALU.subtract).then_inc(drop_rows_made, 1)

            def take_maxima(i, par):
                dve.wait_ge(m_turned, 2 * i + par + 1)
                dve.tensor_tensor(below[:].rearrange("p h s -> p (h s)"),
                                  score[:, par].rearrange("p h s -> p (h s)"),
                                  turned_m, ALU.subtract).then_inc(below_made, 1)

            def take_rescale(i, par):
                dve.wait_ge(node_dropped, 2 * i + par + 1)
                dve.tensor_scalar(rescale[:], node_drop, 1.0, None, ALU.add).then_inc(rescale_d, 1)

            def bring_down(i, par):
                lap = 2 * i + par
                dve.reg_load(lap_reg, e.win_at[0:1, bass.ds(lap * LAP, 1)])
                win = dve.snap(lap_reg, min_val=0, max_val=WINS_PAD - 1)
                dve.wait_ge(rescale_d, RESCALE_STEPS * lap + 2)
                wait(dve, added, LAP * lap)
                sums = e.acc[:, bass.ds(win * AW, F)].rearrange("p (h d) -> p h d", d=DH)
                dve.tensor_tensor(sums, sums, rescale[:].unsqueeze(2).to_broadcast([P, HEADS, DH]),
                                  ALU.mult).then_inc(rescale_d, 1)
                exps = e.acc[:, bass.ds(win * AW + F, HEADS)]
                dve.tensor_tensor(exps, exps, rescale[:], ALU.mult).then_inc(rescale_d, 1)

            def turn(i, par, left):
                nxt = following(i, par, 1)
                last = RING - 1
                for g in range(RING):
                    far = g > 0 and RING * (left + 1) - 1 - g >= RING + 1
                    if g > 0:
                        if left:
                            score_group(*nxt, g)
                        add_slot(i, par, g - 1, 0)
                    if far:
                        multiply_half(*ahead(i, par, g, RING + 1), 0)
                    if g > 0:
                        if left and g == last:
                            own_ends(*nxt)
                        add_slot(i, par, g - 1, 1)
                    if far:
                        multiply_half(*ahead(i, par, g, RING + 1), 1)
                    if g > 0:
                        if left and g == last:
                            spread_own(*nxt)
                        add_slot(i, par, g - 1, 2)
                    if g < last:
                        weigh_group(i, par, g)
                    elif left > 1:
                        score_group(*following(i, par, 2), 0)
                    if g == 0:
                        bring_down(i, par)
                    else:
                        add_slot(i, par, g - 1, 3)
                if left:
                    candidates(*nxt)
                add_slot(i, par, last, 0)
                if left:
                    ends_max(*nxt)
                add_slot(i, par, last, 1)
                if left:
                    maxima(*nxt)
                if left > 1:
                    multiply_half(*following(i, par, 2), 1, 0)
                if left:
                    drop_rows(*nxt)
                    keep_last(*nxt)
                add_slot(i, par, last, 2)
                if left:
                    take_maxima(*nxt)
                add_slot(i, par, last, 3)
                if left > 1:
                    multiply_half(*following(i, par, 2), 1, 1)
                if left:
                    take_rescale(*nxt)

            dve.memset(kv[:, :, :, :, RW - 1:RW], 1.0).then_inc(cleared, 1)
            dve.memset(spread[:], 0.0).then_inc(cleared, 1)
            dve.wait_ge(cleared, 2)
            for g in range(RING):
                multiply_half(0, 0, g, 0)
                multiply_half(0, 0, g, 1)
                score_group(0, 0, g)
            own_ends(0, 0)
            multiply_half(0, 1, 0, 0)
            spread_own(0, 0)
            multiply_half(0, 1, 0, 1)
            candidates(0, 0)
            ends_max(0, 0)
            maxima(0, 0)
            score_group(0, 1, 0)
            multiply_half(0, 1, 1, 0)
            drop_rows(0, 0)
            keep_last(0, 0)
            take_maxima(0, 0)
            multiply_half(0, 1, 1, 1)
            take_rescale(0, 0)
            edge_laps(dve, turn)

        @block.tensor
        def _(pe):
            regs = [pe.alloc_register(f"pick_win{j}") for j in range(GS)]

            def turn_hot(i, par, g):
                n = group_no(i, par, g)
                pe.wait_ge(hot_s_made, n + 1)
                wait(pe, hot_t_copied, n)
                for j in range(GS):
                    mm = pe.transpose(ps_hot[:, g % 2, j, :], hot_s[:, g % 2, j, :], e.ident_b[:])
                mm.then_inc(hot_turned, 1)

            def pick_half(i, par, g, half):
                n = group_no(i, par, g)
                if half == 0:
                    pe.reg_load(regs, e.win_at[0:1, bass.ds(n * GS, GS)])
                    pe.wait_ge(hot_t_copied, n + 1)
                wait(pe, multiplied, 2 * n + half - 1)
                for j in range(2 * half, 2 * half + 2):
                    win = pe.snap(regs[j], min_val=0, max_val=WINS_PAD - 1)
                    mm = pe.matmul(ps_q[:, half, j % 2, :], hot_t[:, g % 2, j, :],
                                   e.q_all[:, bass.ds(win * F, F)], start=True, stop=True)
                mm.then_inc(q_picked, 1)

            def sum_group(i, par, g):
                n = group_no(i, par, g)
                pe.wait_ge(hot_m_made, n + 1)
                if g < RING - 1:
                    pe.wait_ge(weighed, (2 * i + par) * (RING - 1) + g + 1)
                else:
                    pe.wait_ge(last_weighed, 2 * i + par + 1)
                for j in range(GS):
                    wait(pe, added, GS * (n - 1) + j + 1)
                    pe.matmul(ps_sum[:, j, 0:AW], hot_m[:, g % 2, j, :], kv[:, par, g, j, F:RW],
                              start=True, stop=True).then_inc(summed, 1)

            def turn_score(i, par):
                lap = 2 * i + par
                pe.wait_ge(scored, RING * (lap + 1))
                wait(pe, below_made, lap)
                pe.transpose(turned_score, score[:, par].rearrange("p h s -> p (h s)"), e.ident_f[:]).then_inc(score_turned, 1)

            def spread_ends(i, par):
                pe.wait_ge(spread_made, 2 * i + par + 1)
                pe.matmul(all_ends, e.head_eq[:], spread[:], start=True, stop=True).then_inc(ends_spread, 1)

            def turn_m(i, par):
                lap = 2 * i + par
                pe.wait_ge(m_made, lap + 1)
                pe.transpose(turned_m, top_m[:], e.ident_f[:]).then_inc(m_turned, 1)

            def drop_nodes(i, par):
                pe.wait_ge(drop_rows_made, 2 * i + par + 1)
                pe.wait_ge(first_marked, 2 * i + par + 1)
                pe.wait_ge(below_made, 2 * i + par + 1)
                pe.matmul(node_drop, node_hot[:], head_drop[:], start=True, stop=True).then_inc(node_dropped, 1)

            def turn(i, par, left):
                nxt = following(i, par, 1)
                for g in range(RING):
                    after = RING * (left + 1) - 1 - g
                    if left and g == RING - 1:
                        turn_score(*nxt)
                    if g > 0 and after >= 6:
                        pick_half(*ahead(i, par, g, 6), 0)
                    if left and g == RING - 1:
                        spread_ends(*nxt)
                    if g > 0 and after >= 6:
                        pick_half(*ahead(i, par, g, 6), 1)
                    if after >= 7:
                        turn_hot(*ahead(i, par, g, 7))
                    sum_group(i, par, g)
                if left:
                    turn_m(*nxt)
                    drop_nodes(*nxt)
                if left > 1:
                    pick_half(*following(i, par, 2), 2, 0)
                    pick_half(*following(i, par, 2), 2, 1)

            pe.wait_ge(cleared, 2)
            turn_hot(0, 0, 0)
            for n in range(6):
                if n == RING + 1:
                    turn_score(0, 0)
                    spread_ends(0, 0)
                for half in range(2):
                    pick_half(*ahead(0, 0, n, 0), half)
                turn_hot(*ahead(0, 0, n, 1))
            turn_m(0, 0)
            drop_nodes(0, 0)
            pick_half(0, 1, 2, 0)
            pick_half(0, 1, 2, 1)
            edge_laps(pe, turn)


def edge_mean(nc, e):
    with ExitStack() as ctx:
        r_buf = e.sb("r_buf", [P, RING, GS, F], F32, ctx)
        hot = e.sb("hot", [P, 2, GS, P], F32, ctx)
        ps_sum = e.ps("ps_mean", [P, 2, GS, 512], F32, ctx)
        staged = e.sem("r_staged")
        rows_in = [e.sem(f"r_rows_in{g}") for g in range(RING)]
        pool_turns = e.sem("r_pool_turns")
        act_turns = e.sem("r_act_turns")
        cleared = e.sem("r_cleared")
        far = e.sem("r_far")
        hot_made = e.sem("r_hot_made")
        summed = e.sem("r_summed")
        added = e.sem("r_added")
        block = ctx.enter_context(nc.Block())

        @block.gpsimd
        def _(pool):
            def lap(i, last):
                for g in range(RING):
                    n = i * RING + g
                    pool.wait_ge(staged, n + 1)
                    wait(pool, summed, GS * (n - RING + 1))
                    pool.sem_inc(pool_turns, 1)
                    for j in range(GS):
                        pool.indirect_dma_start(out=r_buf[:, g, j, :], out_offset=None, in_=e.x1_rows[:, :],
                                                in_offset=bass.IndirectOffsetOnAxis(ap=e.stage[:, 0, g, j:j + 1],
                                                                                    axis=0)
                                                ).then_inc(rows_in[g], 16)

            laps(pool, lap, LAPS)

        @block.scalar
        def _(act):
            def stage_group(i, g):
                act.activation(e.stage[:, 0, g, :], e.src_idx[:, bass.ds(i * LAP + g * GS, GS)],
                               ACT.Copy).then_inc(staged, 1)

            def lap(i, last):
                for g in range(RING):
                    n = i * RING + g
                    wait(act, summed, GS * (n - 1))
                    act.sem_inc(act_turns, 1)
                    for j in range(GS):
                        ins = act.activation(hot[:, g % 2, j, :], e.iota_f[:], ACT.Abs,
                                             bias=e.neg_loc[:, bass.ds(n * GS + j, 1)])
                    ins.then_inc(far, 1)
                    act.wait_ge(far, n + 1)
                    act.activation(hot[:, g % 2], hot[:, g % 2], ACT.Relu, bias=1.0, scale=-1.0).then_inc(hot_made, 1)
                    if g == 0:
                        wait(act, rows_in[RING - 1], 16 * GS * i)
                        act.sem_inc(act_turns, 1)
                        stage_group(i, RING - 1)
                    elif not last:
                        act.wait_ge(rows_in[g - 1], 16 * GS * (i + 1))
                        act.sem_inc(act_turns, 1)
                        stage_group(i + 1, g - 1)

            for g in range(RING - 1):
                stage_group(0, g)
            laps(act, lap, LAPS)

        @block.vector
        def _(dve):
            regs = [dve.alloc_register(f"mean_win{j}") for j in range(GS)]

            def lap(i, last):
                for g in range(RING):
                    n = i * RING + g
                    dve.reg_load(regs, e.win_at[0:1, bass.ds(n * GS, GS)])
                    for j in range(GS):
                        win = dve.snap(regs[j], min_val=0, max_val=WINS_PAD - 1)
                        dve.wait_ge(summed, GS * n + j + 1)
                        wait(dve, added, GS * n + j)
                        dst = e.acc[:, bass.ds(win * AW, F)]
                        dve.tensor_tensor(dst, dst, ps_sum[:, g % 2, j, 0:F], ALU.add).then_inc(added, 1)

            dve.memset(e.acc[:], 0.0).then_inc(cleared, 1)
            dve.wait_ge(cleared, 1)
            laps(dve, lap, LAPS)

        @block.tensor
        def _(pe):
            def lap(i, last):
                for g in range(RING):
                    n = i * RING + g
                    pe.wait_ge(rows_in[g], 16 * GS * (i + 1))
                    pe.wait_ge(hot_made, n + 1)
                    wait(pe, added, GS * (n - 1))
                    for j in range(GS):
                        pe.matmul(ps_sum[:, g % 2, j, 0:F], hot[:, g % 2, j, :], r_buf[:, g, j, :],
                                  start=True, stop=True).then_inc(summed, 1)

            laps(pe, lap, LAPS)


PAIRS = -(-WINS // 2)
NLAPS = (PAIRS - 1) // 2
assert 2 * NLAPS == PAIRS - 1 and WINS % 2 == 1


def pair_laps(eng, body):
    body(0, 0, 2, 2, 2)
    body(1, 1, 2, 2, 2)
    with eng.Fori(1, NLAPS - 1) as i:
        body(2 * i, 0, 2, 2, 2)
        body(2 * i + 1, 1, 2, 2, 2)
    body(PAIRS - 3, 0, 2, 2, 1)
    body(PAIRS - 2, 1, 2, 1, 0)
    body(PAIRS - 1, 0, 1, 0, 0)


def node_ffn(nc, e):
    with ExitStack() as ctx:
        w1_sb = e.sb("w1_sb", [P, FC, HID], F32, ctx)
        w2_sb = e.sb("w2_sb", [P, HC, F], F32, ctx)
        cols = e.sb("cols", [P, 2, HC], F32, ctx)
        neg = e.sb("neg", [P, 2, HC], F32, ctx)
        rows = e.sb("rows", [P, 3, F], F32, ctx)
        rst = e.sb("rst", [P, 2, 2, F], F32, ctx)
        rst_t = e.sb("rst_t", [P, 2, FC, 2 * P], F32, ctx)
        relu_p = e.sb("relu_p", [P, HC, 2 * P], F32, ctx)
        relu_n = e.sb("relu_n", [P, HC, 2 * P], F32, ctx)
        hid = e.sb("hid", [P, 2, HC, 2 * P], F32, ctx)
        zr = e.sb("zr", [P, 2, HEADS], F32, ctx)
        first = e.sb("first", [P, 2, F], F32, ctx)
        second = e.sb("second", [P, 2, F], F32, ctx)
        mv = e.sb("mv", [P, 4, 4], F32, ctx)
        stats = e.sb("stats", [P, 4, 6], F32, ctx)
        mv3 = e.sb("mv3", [P, 2, 4], F32, ctx)
        stats3 = e.sb("stats3", [P, 2, 6], F32, ctx)
        ps_tr = e.ps("ps_tr", [P, FC, 2 * P], F32, ctx)
        ps_h = e.ps("ps_h", [P, 4, 512], F32, ctx)
        ps_f = e.ps("ps_f", [P, 2, 512], F32, ctx)
        par_in = e.sem("par_in")
        w1_in = e.sem("w1_in")
        w2_in = e.sem("w2_in")
        x_ld = [e.sem("x_ld0"), e.sem("x_ld1")]
        vec_d = e.sem("vec_d")
        rst_made = e.sem("rst_made")
        rst_kept = e.sem("rst_kept")
        keep_turns = e.sem("keep_turns")
        rst_turned = e.sem("rst_turned")
        rst_copied = e.sem("rst_copied")
        hid_mm = e.sem("hid_mm")
        relu_d = e.sem("relu_d")
        hid_made = e.sem("hid_made")
        ffn_mm = e.sem("ffn_mm")
        ffn_read = e.sem("ffn_read")
        x1_made = e.sem("x1_made")
        x1_out = e.sem("x1_out")
        neg_made = e.sem("neg_made")
        settled = e.sem("settled")
        var_ready = e.sem("var_ready")
        std_ready = e.sem("std_ready")
        var3_ready = e.sem("var3_ready")
        std3_ready = e.sem("std3_ready")
        block = ctx.enter_context(nc.Block())
        x_v = e.x.rearrange("(w p) f -> p w f", p=P)
        x1_v = e.x1_rows.rearrange("(w p) f -> p w f", p=P)
        x1_s = e.x1_all[:].rearrange("p (w f) -> p w f", f=F)

        def sums(n, nw):
            return e.acc[:, bass.ds(2 * n * AW, nw * AW)].rearrange("p (w a) -> p w a", a=AW)

        def roots_of(post_nw, pre_nw):
            return slice(0 if post_nw else 2, 2 + pre_nw if pre_nw else post_nw)

        @block.sync
        def _(sp):
            def load_x(n, par, nw):
                wait(sp, rst_made, n - 1)
                sp.dma_start(x1_s[:, bass.ds(2 * n, nw), :], x_v[:, bass.ds(2 * n, nw), :]).then_inc(x_ld[par], 16)

            def body(n, par, nw, nxt, nxt2):
                if nxt2:
                    load_x(n + 2, par, nxt2)

            load_x(0, 0, 2)
            sp.dma_start(rows[:, 0, :], e.ln_g.to_broadcast([P, F])).then_inc(par_in, 16)
            sp.dma_start(rows[:, 1, :], e.ln_b.to_broadcast([P, F])).then_inc(par_in, 16)
            sp.dma_start(rows[:, 2, :], e.b2.to_broadcast([P, F])).then_inc(par_in, 16)
            for k, col in enumerate((e.b1, e.alpha)):
                sp.dma_start(cols[:, k, :], col).then_inc(par_in, 16)
            sp.dma_start(w1_sb[:], e.w1.rearrange("(c p) n -> p c n", p=P)).then_inc(w1_in, 16)
            load_x(1, 1, 2)
            sp.dma_start(w2_sb[:], e.w2.rearrange("(c p) n -> p c n", p=P)).then_inc(w2_in, 16)
            pair_laps(sp, body)

        @block.gpsimd
        def _(pool):
            def keep(n, par, nw):
                pool.wait_ge(rst_made, n + 1)
                pool.sem_inc(keep_turns, 1)
                pool.tensor_tensor(sums(n, nw)[:, :, 0:F], rst[:, par, 0:nw], rows[:, 2:3, :].to_broadcast([P, nw, F]),
                                   ALU.add).then_inc(rst_kept, 1)

            def body(n, par, nw, nxt, nxt2):
                if nxt2:
                    keep(n + 2, par, nxt2)
                pool.wait_ge(x1_made, n + 1)
                pool.dma_start(x1_v[:, bass.ds(2 * n, nw), :], x1_s[:, bass.ds(2 * n, nw), :]).then_inc(x1_out, 16)

            keep(0, 0, 2)
            keep(1, 1, 2)
            pair_laps(pool, body)
            pool.wait_ge(x1_out, 16 * PAIRS)

        @block.vector
        def _(dve):
            STEPS = 28

            def period(n, post_nw, mid_nw, pre_nw, par):
                base = STEPS * (n + 2)
                k = [0]

                def step(ins):
                    k[0] += 1
                    ins.then_inc(vec_d, 1)
                    return k[0]

                def need(count):
                    dve.wait_ge(vec_d, base + count)

                def prelu(chunks):
                    for hc in chunks:
                        if mid_nw:
                            dve.wait_ge(relu_d, HC * (n + 1) + hc + 1)
                            if hc == 0:
                                wait(dve, ffn_mm, n)
                            dve.scalar_tensor_tensor(hid[:, 1 - par, hc, 0:mid_nw * P], relu_n[:, hc, 0:mid_nw * P],
                                                     neg[:, 1, hc:hc + 1], relu_p[:, hc, 0:mid_nw * P],
                                                     ALU.mult, ALU.add).then_inc(hid_made, 1)

                y, h = second[:, 0:post_nw], first[:, 0:pre_nw]
                if pre_nw:
                    a = sums(n + 2, pre_nw)
                    z_at = step(dve.tensor_scalar(zr[:, 0:pre_nw], a[:, :, F:F + HEADS], 0.5, None, ALU.max))
                if post_nw:
                    dve.wait_ge(ffn_mm, n)
                    dve.wait_ge(rst_kept, n)
                    wait(dve, x1_made, n - 1)
                    y_at = step(dve.tensor_tensor(y, ps_f[:, 0:post_nw, 0:F], sums(n - 1, post_nw)[:, :, 0:F],
                                                  ALU.add))
                if pre_nw:
                    need(z_at)
                    z_at = step(dve.reciprocal(zr[:, 0:pre_nw], zr[:, 0:pre_nw]))
                if pre_nw:
                    need(z_at)
                    h_at = step(dve.tensor_tensor(h.rearrange("p w (h d) -> p w h d", d=DH),
                                                  a[:, :, 0:F].rearrange("p w (h d) -> p w h d", d=DH),
                                                  zr[:, 0:pre_nw].unsqueeze(3).to_broadcast([P, pre_nw, HEADS, DH]),
                                                  ALU.mult))
                if post_nw:
                    need(y_at)
                    dve.sem_inc(ffn_read, 1)
                    for w in range(post_nw):
                        y_at = step(dve.bn_stats(stats[:, w, :], y[:, w, :]))
                if pre_nw:
                    dve.wait_ge(x_ld[par], 8 * (n + 2 - par) + 16)
                    need(h_at)
                    h_at = step(dve.tensor_tensor(h, h, x1_s[:, bass.ds(2 * (n + 2), pre_nw), :], ALU.add))
                if post_nw:
                    need(y_at)
                    dve.sem_inc(settled, 1)
                    for w in range(post_nw):
                        var_at = step(dve.bn_aggr(mv[:, w, 0:2], stats[:, w, :]))
                if pre_nw:
                    need(h_at)
                    for w in range(pre_nw):
                        h_at = step(dve.bn_stats(stats[:, 2 + w, :], h[:, w, :]))
                    need(h_at)
                    dve.sem_inc(settled, 1)
                    for w in range(pre_nw):
                        var_at = step(dve.bn_aggr(mv[:, 2 + w, 0:2], stats[:, 2 + w, :]))
                need(var_at)
                dve.sem_inc(var_ready, 1)
                both = [(second, w, w) for w in range(post_nw)] + [(first, w, 2 + w) for w in range(pre_nw)]
                for row, w, m in both:
                    row_at = step(dve.scalar_tensor_tensor(row[:, w, :], row[:, w, :], mv[:, m, 0:1], rows[:, 0, :],
                                                           ALU.subtract, ALU.mult))
                dve.wait_ge(std_ready, n + 3)
                own = roots_of(post_nw, pre_nw)
                step(dve.reciprocal(mv[:, own, 3:4], mv[:, own, 2:3]))
                prelu(range(0, 1))
                need(row_at + 1)
                if pre_nw:
                    wait(dve, rst_turned, n + 1)
                    wait(dve, rst_kept, n + 1)
                for row, w, m in both:
                    if row is second:
                        y_at = step(dve.scalar_tensor_tensor(row[:, w, :], row[:, w, :], mv[:, m, 3:4], rows[:, 1, :],
                                                             ALU.mult, ALU.add))
                    else:
                        ins = dve.scalar_tensor_tensor(rst[:, par, w, :], row[:, w, :], mv[:, m, 3:4], rows[:, 1, :],
                                                       ALU.mult, ALU.add)
                if pre_nw:
                    ins.then_inc(rst_made, 1)
                if post_nw:
                    need(y_at)
                    y_at = step(dve.tensor_tensor(y, y, x1_s[:, bass.ds(2 * (n - 1), post_nw), :], ALU.add))
                prelu(range(1, 3))
                if post_nw:
                    need(y_at)
                    for w in range(post_nw):
                        y_at = step(dve.bn_stats(stats3[:, w, :], y[:, w, :]))
                prelu(range(3, 4))
                if post_nw:
                    need(y_at)
                    dve.sem_inc(settled, 1)
                    for w in range(post_nw):
                        y_at = step(dve.bn_aggr(mv3[:, w, 0:2], stats3[:, w, :]))
                    need(y_at)
                    dve.sem_inc(var3_ready, 1)
                prelu(range(4, HC - 1))
                if post_nw:
                    dve.wait_ge(std3_ready, n)
                    y_at = step(dve.reciprocal(mv3[:, 0:post_nw, 3:4], mv3[:, 0:post_nw, 2:3]))
                prelu(range(HC - 1, HC))
                if post_nw:
                    need(y_at)
                    for w in range(post_nw):
                        ins = dve.tensor_scalar(x1_s[:, bass.ds(2 * (n - 1) + w, 1), :].rearrange("p w f -> p (w f)"),
                                                y[:, w, :], mv3[:, w, 0:1], mv3[:, w, 3:4], ALU.subtract, ALU.mult)
                    ins.then_inc(x1_made, 1)
                assert k[0] <= STEPS
                if k[0] < STEPS:
                    dve.sem_inc(vec_d, STEPS - k[0])

            def body(n, par, nw, nxt, nxt2):
                first_one = isinstance(n, int) and n == 0
                period(n, 0 if first_one else 2, nxt, nxt2, par)

            dve.wait_ge(par_in, 16 * 5)
            dve.tensor_scalar(neg[:], cols[:], -1.0, None, ALU.mult).then_inc(neg_made, 1)
            a = e.acc[:].rearrange("p (w a) -> p w a", a=AW)
            dve.tensor_scalar(e.cnt_rec[:].unsqueeze(2), a[:, 0:WINS, AW - 1:AW], 1.0, None,
                              ALU.max).then_inc(neg_made, 1)
            dve.wait_ge(neg_made, 2)
            dve.reciprocal(e.cnt_rec[:], e.cnt_rec[:]).then_inc(neg_made, 1)
            dve.wait_ge(neg_made, 3)
            period(-2, 0, 0, 2, 0)
            period(-1, 0, 2, 2, 1)
            pair_laps(dve, body)
            period(PAIRS, 1, 0, 0, 1)

        @block.scalar
        def _(act):
            act.wait_ge(neg_made, 1)

            def relus(n, nw, chunks):
                for hc in chunks:
                    act.wait_ge(hid_mm, HC * n + hc + 1)
                    if hc == 0:
                        wait(act, hid_made, HC * n)
                    act.activation(relu_p[:, hc, 0:nw * P], ps_h[:, hc % 4, 0:nw * P], ACT.Relu,
                                   bias=cols[:, 0, hc:hc + 1])
                    act.activation(relu_n[:, hc, 0:nw * P], ps_h[:, hc % 4, 0:nw * P], ACT.Relu,
                                   bias=neg[:, 0, hc:hc + 1], scale=-1.0).then_inc(relu_d, 1)

            def period(n, post_nw, mid_nw, pre_nw, par):
                if mid_nw:
                    relus(n + 1, mid_nw, range(0, HC // 2))
                own = roots_of(post_nw, pre_nw)
                act.wait_ge(var_ready, n + 3)
                act.activation(mv[:, own, 2:3], mv[:, own, 1:2], ACT.Sqrt, bias=e.eps_col[:]).then_inc(std_ready, 1)
                if mid_nw:
                    relus(n + 1, mid_nw, range(HC // 2, HC))
                if post_nw:
                    act.wait_ge(var3_ready, n)
                    act.activation(mv3[:, 0:post_nw, 2:3], mv3[:, 0:post_nw, 1:2], ACT.Sqrt,
                                   bias=e.eps_col[:]).then_inc(std3_ready, 1)
                if pre_nw:
                    act.wait_ge(rst_turned, n + 3)
                    act.activation(rst_t[:, par, :, 0:pre_nw * P], ps_tr[:, :, 0:pre_nw * P],
                                   ACT.Copy).then_inc(rst_copied, 1)

            def body(n, par, nw, nxt, nxt2):
                first_one = isinstance(n, int) and n == 0
                if nxt or not isinstance(n, int) or n < PAIRS - 1:
                    period(n, 0 if first_one else 2, nxt, nxt2, par)
                else:
                    period(n, 2, 0, 0, par)

            period(-2, 0, 0, 2, 0)
            period(-1, 0, 2, 2, 1)
            pair_laps(act, body)
            period(PAIRS, 1, 0, 0, 1)

        @block.tensor
        def _(pe):
            def turn(n, par, nw):
                pe.wait_ge(rst_made, n + 1)
                wait(pe, rst_copied, n)
                for w in range(nw):
                    for c in range(FC):
                        mm = pe.transpose(ps_tr[:, c, w * P:(w + 1) * P],
                                          rst[:, par, w, c * P:(c + 1) * P], e.ident_f[:])
                mm.then_inc(rst_turned, 1)

            def first_product(n, par, nw):
                pe.wait_ge(rst_copied, n + 1)
                for hc in range(HC):
                    wait(pe, relu_d, HC * n + hc - 3)
                    for c in range(FC):
                        mm = pe.matmul(ps_h[:, hc % 4, 0:nw * P], w1_sb[:, c, hc * P:(hc + 1) * P],
                                       rst_t[:, par, c, 0:nw * P], start=(c == 0), stop=(c == FC - 1))
                    mm.then_inc(hid_mm, 1)

            def body(n, par, nw, nxt, nxt2):
                if nxt:
                    first_product(n + 1, 1 - par, nxt)
                wait(pe, ffn_read, n)
                for hc in range(HC):
                    pe.wait_ge(hid_made, HC * n + hc + 1)
                    for w in range(nw):
                        mm = pe.matmul(ps_f[:, w, 0:F], hid[:, par, hc, w * P:(w + 1) * P], w2_sb[:, hc, :],
                                       start=(hc == 0), stop=(hc == HC - 1))
                    if nxt2 and hc == HC - 3:
                        turn(n + 2, par, nxt2)
                mm.then_inc(ffn_mm, 1)

            turn(0, 0, 2)
            pe.wait_ge(w1_in, 16)
            first_product(0, 0, 2)
            turn(1, 1, 2)
            pe.wait_ge(w2_in, 16)
            pair_laps(pe, body)


def node_out(nc, e):
    with ExitStack() as ctx:
        wt_sb = e.sb("wt_sb", [P, FC, F], F32, ctx)
        bl_row = e.sb("bl_row", [P, 1, F], F32, ctx)
        mean = e.sb("mean", [P, 2, 2, F], F32, ctx)
        mean_t = e.sb("mean_t", [P, 2, FC, 2 * P], F32, ctx)
        y = e.sb("y", [P, 2, 2, F], F32, ctx)
        res = e.sb("res", [P, 2, 2, F], F32, ctx)
        mv = e.sb("mv_o", [P, 2, 2, 4], F32, ctx)
        stats = e.sb("stats_o", [P, 2, 6], F32, ctx)
        ps_tr = e.ps("ps_tro", [P, 2, FC, 2 * P], F32, ctx)
        ps_y = e.ps("ps_y", [P, 2, 2, 512], F32, ctx)
        par_in = e.sem("o_par_in")
        vec_d = e.sem("o_vec_d")
        mean_made = e.sem("mean_made")
        mean_turns = e.sem("mean_turns")
        mean_turned = e.sem("mean_turned")
        mean_copied = e.sem("mean_copied")
        y_mm = e.sem("y_mm")
        y_read = e.sem("y_read")
        var_ready = e.sem("o_var_ready")
        settled = e.sem("o_settled")
        std_ready = e.sem("o_std_ready")
        res_made = e.sem("res_made")
        res_out = [e.sem("res_out0"), e.sem("res_out1")]
        block = ctx.enter_context(nc.Block())
        x1_s = e.x1_all[:].rearrange("p (w f) -> p w f", f=F)
        full = (WINS - 1) * P
        out_v = e.out[0:full, :].rearrange("(w p) f -> p w f", p=P)

        @block.sync
        def _(sp):
            sp.dma_start(wt_sb[:], e.wT.rearrange("(c p) n -> p c n", p=P)).then_inc(par_in, 16)
            sp.dma_start(bl_row[:, 0, :], e.bl.to_broadcast([P, F])).then_inc(par_in, 16)

            def body(n, par, nw, nxt, nxt2):
                sp.wait_ge(res_made, n + 1)
                if nw == 2:
                    sp.dma_start(out_v[:, bass.ds(2 * n, 2), :], res[:, par]).then_inc(res_out[par], 16)
                else:
                    rest = N_NODES - full
                    sp.dma_start(e.out[full:N_NODES, :], res[0:rest, par, 0, :]).then_inc(res_out[par], 16)

            pair_laps(sp, body)
            sp.wait_ge(res_out[0], 16 * (NLAPS + 1))
            sp.wait_ge(res_out[1], 16 * NLAPS)

        @block.vector
        def _(dve):
            STEPS = 9

            def period(n, par, nw, prev_nw):
                k = [0]

                def step(ins):
                    k[0] += 1
                    ins.then_inc(vec_d, 1)
                    return k[0]

                def need(count):
                    dve.wait_ge(vec_d, STEPS * n + count)

                if nw:
                    dve.wait_ge(y_mm, n + 1)
                    wait(dve, res_made, n - 1)
                    dve.tensor_tensor(y[:, par, 0:nw], ps_y[:, par, 0:nw, 0:F], bl_row[:].to_broadcast([P, nw, F]),
                                      ALU.add).then_inc(y_read, 1)
                if prev_nw:
                    dve.wait_ge(std_ready, n)
                    rec_at = step(dve.reciprocal(mv[:, 1 - par, 0:prev_nw, 3:4], mv[:, 1 - par, 0:prev_nw, 2:3]))
                if nw:
                    dve.wait_ge(y_read, n + 1)
                    y_at = step(dve.scalar_tensor_tensor(y[:, par, 0:nw], y[:, par, 0:nw], 0.0,
                                                         x1_s[:, bass.ds(2 * n, nw), :], ALU.max, ALU.add))
                if prev_nw:
                    need(rec_at)
                    wait(dve, res_out[1 - par], 8 * (n - 1 - (1 - par)))
                    for w in range(prev_nw):
                        ins = dve.tensor_scalar(res[:, 1 - par, w, :], y[:, 1 - par, w, :], mv[:, 1 - par, w, 0:1],
                                                mv[:, 1 - par, w, 3:4], ALU.subtract, ALU.mult)
                    ins.then_inc(res_made, 1)
                if nw:
                    need(y_at)
                    for w in range(nw):
                        y_at = step(dve.bn_stats(stats[:, w, :], y[:, par, w, :]))
                    need(y_at)
                    dve.sem_inc(settled, 1)
                    for w in range(nw):
                        y_at = step(dve.bn_aggr(mv[:, par, w, 0:2], stats[:, w, :]))
                    need(y_at)
                    dve.sem_inc(var_ready, 1)
                dve.sem_inc(vec_d, STEPS - k[0])

            def body(n, par, nw, nxt, nxt2):
                period(n, par, nw, 0 if isinstance(n, int) and n == 0 else 2)

            dve.wait_ge(par_in, 32)
            pair_laps(dve, body)
            period(PAIRS, 1, 0, 1)

        @block.scalar
        def _(act):
            def take_mean(n, par, nw):
                wait(act, mean_turned, n - 1)
                act.sem_inc(mean_turns, 1)
                for w in range(nw):
                    ins = act.activation(mean[:, par, w, :], e.acc[:, bass.ds((2 * n + w) * AW, F)], ACT.Copy,
                                         scale=e.cnt_rec[:, bass.ds(2 * n + w, 1)])
                ins.then_inc(mean_made, 1)

            def copy_turned(n, par, nw):
                act.wait_ge(mean_turned, n + 1)
                wait(act, y_mm, n - 1)
                act.activation(mean_t[:, par, :, 0:nw * P], ps_tr[:, par, :, 0:nw * P],
                               ACT.Copy).then_inc(mean_copied, 1)

            def body(n, par, nw, nxt, nxt2):
                if nxt:
                    copy_turned(n + 1, 1 - par, nxt)
                if nxt2:
                    take_mean(n + 2, par, nxt2)
                act.wait_ge(var_ready, n + 1)
                act.activation(mv[:, par, 0:nw, 2:3], mv[:, par, 0:nw, 1:2], ACT.Sqrt,
                               bias=e.eps_col[:]).then_inc(std_ready, 1)

            take_mean(0, 0, 2)
            take_mean(1, 1, 2)
            copy_turned(0, 0, 2)
            pair_laps(act, body)

        @block.tensor
        def _(pe):
            pe.wait_ge(par_in, 32)

            def turn(n, par, nw):
                pe.wait_ge(mean_made, n + 1)
                wait(pe, mean_copied, n - 1)
                for w in range(nw):
                    for c in range(FC):
                        mm = pe.transpose(ps_tr[:, par, c, w * P:(w + 1) * P], mean[:, par, w, c * P:(c + 1) * P],
                                          e.ident_f[:])
                mm.then_inc(mean_turned, 1)

            def body(n, par, nw, nxt, nxt2):
                pe.wait_ge(mean_copied, n + 1)
                wait(pe, y_read, n - 1)
                for w in range(nw):
                    for c in range(FC):
                        mm = pe.matmul(ps_y[:, par, w, 0:F], mean_t[:, par, c, w * P:(w + 1) * P], wt_sb[:, c, :],
                                       start=(c == 0), stop=(c == FC - 1))
                mm.then_inc(y_mm, 1)
                if nxt2:
                    turn(n + 2, par, nxt2)

            turn(0, 0, 2)
            turn(1, 1, 2)
            pair_laps(pe, body)


_INS = ["x", "xT", "edges", "wqkv", "ln_g", "ln_b", "w1", "b1", "alpha", "w2", "b2", "wT", "bl"]


def kernel(**inputs):
    import numpy as _np
    import concourse.bacc as _bacc
    from concourse.bass_utils import run_bass_kernel_spmd as _run

    g = {k: _np.asarray(v) for k, v in inputs.items()}
    x = _np.zeros((NODES_PAD, F), _np.float32)
    x[:N_NODES] = g["x"]
    edges = _np.zeros((TILES_PAD, 2, P), _np.int32)
    edges[:, 1] = NO_NODE
    pad = TILES_PAD * P - N_EDGES
    edges[:, 0] = _np.concatenate([g["src"], _np.zeros(pad, _np.int32)]).reshape(TILES_PAD, P)
    edges[:, 1] = _np.concatenate([g["dst"], _np.full(pad, NO_NODE, _np.int32)]).reshape(TILES_PAD, P)
    arrays = {
        "x": x,
        "xT": x.T,
        "edges": edges.reshape(TILES_PAD, 2 * P),
        "wqkv": _np.concatenate([g["L0_gnn_Wk"], g["L0_gnn_Wv"], g["L0_gnn_Wq"]], axis=1),
        "ln_g": g["L0_gnn_ln_g"].reshape(1, F),
        "ln_b": g["L0_gnn_ln_b"].reshape(1, F),
        "w1": g["L0_gnn_W1"],
        "b1": g["L0_gnn_b1"].reshape(HC, P).T,
        "alpha": g["L0_gnn_prelu_alpha"].reshape(HC, P).T,
        "w2": g["L0_gnn_W2"],
        "b2": g["L0_gnn_b2"].reshape(1, F),
        "wT": g["L1_gnn_W"].T,
        "bl": g["L1_gnn_b"].reshape(1, F),
    }
    arrays = {f"in_{k}": _np.ascontiguousarray(a) for k, a in arrays.items()}
    nc = _bacc.Bacc("TRN2", target_bir_lowering=False, num_devices=1)
    args = [nc.dram_tensor(f"in_{k}", arrays[f"in_{k}"].shape, mybir.dt.from_np(arrays[f"in_{k}"].dtype),
                           kind="ExternalInput").ap() for k in _INS]
    args.append(nc.dram_tensor("out_0", (N_NODES, F), F32, kind="ExternalOutput").ap())
    build(nc, *args)
    r = _run(nc, [arrays], core_ids=[0])
    return r.results[0]["out_0"]
```
